# Optimizing a Trainium2 kernel written in Bass

```python
import numpy as np
import jax
import jax.numpy as jnp

def _softmax(x, axis=-1):
    return jax.nn.softmax(x, axis=axis)

def _gelu(x):
    return jax.nn.gelu(x, approximate=True)

def _silu(x):
    return jax.nn.silu(x)

def _sigmoid(x):
    return jax.nn.sigmoid(x)

def _layernorm(x, axis=-1, eps=1e-05):
    m = jnp.mean(x, axis=axis, keepdims=True)
    v = jnp.var(x, axis=axis, keepdims=True)
    return (x - m) / jnp.sqrt(v + eps)

def _scatter_add(tgt, idx, src, axis=0):
    return tgt.at[idx].add(src)

def _segment_sum(src, seg, n):
    return jax.ops.segment_sum(src, seg, n)
kernel_name = 'mk_lm_tower_d2_tok_ids512_r4_271c32'

def setup_inputs(seed: int=0):
    np.random.seed(seed)
    _w = jnp.asarray

    def _rec_inputs():
        import jax
        import jax.numpy as jnp
        _rk = jax.random.key(seed)
        x = jax.random.randint(jax.random.fold_in(_rk, 1), (16, 1024), 0, 64, jnp.int32)
        return x
    x = _rec_inputs()

    def _L0_tok_setup():
        import jax, jax.numpy as jnp
        import numpy as np
        NGRAM_SIZES = (2, 3, 4)
        HASH_VOCAB = 25000
        EMBED_DIM = 128
        BATCH, SEQ = (8, 1024)

        def _ngram_hash_ids(byte_sequence, n):
            L = byte_sequence.shape[1] - n + 1
            h = jnp.zeros((byte_sequence.shape[0], L), dtype=jnp.int64)
            for j in range(n):
                h = (h * 64 + byte_sequence[:, j:j + L]) % HASH_VOCAB
            return h

        def _ngram_embed(byte_sequence, table, n):
            B, S = byte_sequence.shape
            ids = _ngram_hash_ids(byte_sequence, n)
            emb = table[ids]
            out = jnp.zeros((B, S, table.shape[1]), dtype=table.dtype)
            c = n // 2
            return out.at[:, c:c + emb.shape[1]].set(emb)
        key = jax.random.key(seed)
        ks = jax.random.split(key, 6)
        return {'byte_sequence': jax.random.randint(ks[0], (BATCH, SEQ), 0, 64, dtype=jnp.int64), 'emb_2': jax.random.normal(ks[1], (HASH_VOCAB, EMBED_DIM), dtype=jnp.float32), 'emb_3': jax.random.normal(ks[2], (HASH_VOCAB, EMBED_DIM), dtype=jnp.float32), 'emb_4': jax.random.normal(ks[3], (HASH_VOCAB, EMBED_DIM), dtype=jnp.float32), 'proj_w': jax.random.normal(ks[4], (EMBED_DIM, len(NGRAM_SIZES) * EMBED_DIM), dtype=jnp.float32) * 0.02, 'proj_b': jax.random.normal(ks[5], (EMBED_DIM,), dtype=jnp.float32) * 0.02}
    _L0_tok_all = _L0_tok_setup()
    _L0_tok_in = {k: v for k, v in _L0_tok_all.items() if k in ('emb_2', 'emb_3', 'emb_4', 'proj_w', 'proj_b')}
    del _L0_tok_all

    def _L0_attn_setup():
        import jax, jax.numpy as jnp
        import numpy as np
        B, N, C = (2, 1024, 128)
        NUM_HEADS = 8
        HEAD_DIM = C // NUM_HEADS
        SCALE = HEAD_DIM ** (-0.5)
        THETA = 10000.0

        def _rope(x, seq_len, head_dim):
            freqs = 1.0 / THETA ** (jnp.arange(0, head_dim, 2, dtype=jnp.float32) / head_dim)
            t = jnp.arange(seq_len, dtype=jnp.float32)
            freqs_cis = jnp.outer(t, freqs)
            sin_f = jnp.sin(freqs_cis)
            cos_f = jnp.cos(freqs_cis)
            x_even = x[..., ::2]
            x_odd = x[..., 1::2]
            rot = jnp.stack([x_even * cos_f - x_odd * sin_f, x_even * sin_f + x_odd * cos_f], axis=-1)
            return rot.reshape(x.shape)
        key = jax.random.key(seed)
        ks = jax.random.split(key, 5)
        x = jax.random.normal(ks[0], (B, N, C), dtype=jnp.float32)
        Wqkv = jax.random.normal(ks[1], (3 * C, C), dtype=jnp.float32) * 0.02
        bqkv = jax.random.normal(ks[2], (3 * C,), dtype=jnp.float32) * 0.02
        Wproj = jax.random.normal(ks[3], (C, C), dtype=jnp.float32) * 0.02
        bproj = jax.random.normal(ks[4], (C,), dtype=jnp.float32) * 0.02
        return {'x': x, 'Wqkv': Wqkv, 'bqkv': bqkv, 'Wproj': Wproj, 'bproj': bproj}
    _L0_attn_all = _L0_attn_setup()
    _L0_attn_in = {k: v for k, v in _L0_attn_all.items() if k in ('Wqkv', 'bqkv', 'Wproj', 'bproj')}
    del _L0_attn_all

    def _L0_ffn_setup():
        import math
        import jax, jax.numpy as jnp
        import numpy as np
        B, T, D, FF, E = (32, 256, 128, 512, 8)
        CAPACITY_FACTOR = 1.25
        CAP = int(math.ceil(CAPACITY_FACTOR * B * T / E))

        def _bank_residual(x2, Wr, br, W1, b1, W2, b2):
            N, d = x2.shape
            e = Wr.shape[1]
            logits = x2 @ Wr + br
            probs = jax.nn.softmax(logits, axis=-1)
            expert = jnp.argmax(probs, axis=-1)
            gate = jnp.take_along_axis(probs, expert[:, None], axis=-1)[:, 0]
            oneh = jax.nn.one_hot(expert, e, dtype=x2.dtype)
            pos = (jnp.cumsum(oneh, axis=0) * oneh).sum(-1).astype(jnp.int32) - 1
            keep = pos < CAP
            slot = expert.astype(jnp.int32) * CAP + jnp.minimum(pos, CAP - 1)
            xd = jnp.where(keep[:, None], x2, 0.0)
            buf = jnp.zeros((e * CAP, d), x2.dtype).at[slot].add(xd)
            buf = buf.reshape(e, CAP, d)
            h = jax.nn.gelu(jnp.einsum('ecd,edf->ecf', buf, W1) + b1[:, None, :], approximate=False)
            out = jnp.einsum('ecf,efd->ecd', h, W2) + b2[:, None, :]
            y = out.reshape(e * CAP, d)[slot]
            return y * (gate * keep.astype(x2.dtype))[:, None]
        key = jax.random.key(seed)
        ks = jax.random.split(key, 18)
        s = 0.02
        inp = {'x': jax.random.normal(ks[0], (B, T, D), dtype=jnp.float32), 'Wr_sp': jax.random.normal(ks[1], (D, E)) * s, 'br_sp': jnp.zeros((E,), jnp.float32), 'Wr_fq': jax.random.normal(ks[2], (D, E)) * s, 'br_fq': jnp.zeros((E,), jnp.float32), 'Ws1': jax.random.normal(ks[3], (D, FF)) * s, 'bs1': jnp.zeros((FF,), jnp.float32), 'Ws2': jax.random.normal(ks[4], (FF, D)) * s, 'bs2': jnp.zeros((D,), jnp.float32), 'W1_sp': jax.random.normal(ks[5], (E, D, FF)) * s, 'b1_sp': jnp.zeros((E, FF), jnp.float32), 'W2_sp': jax.random.normal(ks[6], (E, FF, D)) * s, 'b2_sp': jnp.zeros((E, D), jnp.float32), 'W1_fq': jax.random.normal(ks[7], (E, D, FF)) * s, 'b1_fq': jnp.zeros((E, FF), jnp.float32), 'W2_fq': jax.random.normal(ks[8], (E, FF, D)) * s, 'b2_fq': jnp.zeros((E, D), jnp.float32)}
        return inp
    _L0_ffn_all = _L0_ffn_setup()
    _L0_ffn_in = {k: v for k, v in _L0_ffn_all.items() if k in ('Wr_sp', 'br_sp', 'Wr_fq', 'br_fq', 'Ws1', 'bs1', 'Ws2', 'bs2', 'W1_sp', 'b1_sp', 'W2_sp', 'b2_sp', 'W1_fq', 'b1_fq', 'W2_fq', 'b2_fq')}
    del _L0_ffn_all

    def _L1_attn_setup():
        import jax, jax.numpy as jnp
        import numpy as np
        D_STATE = 16
        D_CONV = 4

        def _mamba(x, in_w, conv_w, conv_b, xp_w, dt_w, dt_b, A_log, D_skip, out_w):
            B, T, _ = x.shape
            di = conv_w.shape[0]
            xi, z = jnp.split(x @ in_w.T, 2, axis=-1)
            xpad = jnp.pad(xi, ((0, 0), (D_CONV - 1, 0), (0, 0)))
            xc = conv_b + sum((xpad[:, k:k + T, :] * conv_w[:, k] for k in range(D_CONV)))
            xc = jax.nn.silu(xc)
            dtr = dt_w.shape[1]
            dbl = xc @ xp_w.T
            dt, Bm, Cm = jnp.split(dbl, [dtr, dtr + D_STATE], axis=-1)
            dt = jax.nn.softplus(dt @ dt_w.T + dt_b)
            A = -jnp.exp(A_log)
            h0 = jnp.zeros((B, di, D_STATE), x.dtype)

            def step(h, inp):
                dt_t, B_t, C_t, x_t = inp
                h = h * jnp.exp(dt_t[:, :, None] * A) + (dt_t * x_t)[:, :, None] * B_t[:, None, :]
                return (h, jnp.einsum('bds,bs->bd', h, C_t))
            _, ys = jax.lax.scan(step, h0, (dt.transpose(1, 0, 2), Bm.transpose(1, 0, 2), Cm.transpose(1, 0, 2), xc.transpose(1, 0, 2)))
            y = ys.transpose(1, 0, 2) + xc * D_skip
            return y * jax.nn.silu(z) @ out_w.T

        def _interp_linear(x, size):
            Tin = x.shape[1]
            pos = jnp.clip((jnp.arange(size, dtype=jnp.float32) + 0.5) * (Tin / size) - 0.5, 0.0, Tin - 1.0)
            lo = jnp.floor(pos).astype(jnp.int32)
            hi = jnp.minimum(lo + 1, Tin - 1)
            w = (pos - lo.astype(jnp.float32))[None, :, None]
            return x[:, lo, :] * (1.0 - w) + x[:, hi, :] * w
        key = jax.random.key(seed)
        ks = jax.random.split(key, 10)
        S, Dm, di, dtr, ds, dc = (3, 128, 256, 32, 16, 4)
        B, T = (8, 512)
        n = jax.random.normal
        return {'x': n(ks[0], (B, T, Dm), jnp.float32), 'in_w': n(ks[1], (S, 2 * di, Dm), jnp.float32) * 0.02, 'conv_w': n(ks[2], (S, di, dc), jnp.float32) * 0.1, 'conv_b': jnp.zeros((S, di), jnp.float32), 'xp_w': n(ks[3], (S, dtr + 2 * ds, di), jnp.float32) * 0.02, 'dt_w': n(ks[4], (S, di, dtr), jnp.float32) * 0.05, 'dt_b': jnp.full((S, di), -4.6, jnp.float32) + n(ks[5], (S, di), jnp.float32) * 0.1, 'A_log': jnp.broadcast_to(jnp.log(jnp.arange(1, ds + 1, dtype=jnp.float32)), (S, di, ds)) + jnp.zeros((S, di, ds), jnp.float32), 'D_skip': jnp.ones((S, di), jnp.float32), 'out_w': n(ks[6], (S, Dm, di), jnp.float32) * 0.02, 'fusion_w': n(ks[7], (Dm, S * Dm), jnp.float32) * 0.02, 'fusion_b': jnp.zeros((Dm,), jnp.float32), 'ln_g': jnp.ones((Dm,), jnp.float32), 'ln_b': jnp.zeros((Dm,), jnp.float32)}
    _L1_attn_all = _L1_attn_setup()
    _L1_attn_in = {k: v for k, v in _L1_attn_all.items() if k in ('in_w', 'conv_w', 'conv_b', 'xp_w', 'dt_w', 'dt_b', 'A_log', 'D_skip', 'out_w', 'fusion_w', 'fusion_b', 'ln_g', 'ln_b')}
    del _L1_attn_all

    def _L1_ffn_setup():
        import jax, jax.numpy as jnp
        import numpy as np
        H = 128
        FF = 4 * H
        E = 8
        K = 2
        B, S = (4, 1024)
        key = jax.random.key(seed)
        ks = jax.random.split(key, 4)
        s = 0.02
        return {'x': jax.random.normal(ks[0], (B, S, H), dtype=jnp.float32), 'Wg': jax.random.normal(ks[1], (H, E), dtype=jnp.float32) * s, 'bg': jnp.zeros((E,), dtype=jnp.float32), 'W1': jax.random.normal(ks[2], (E, H, FF), dtype=jnp.float32) * s, 'b1': jnp.zeros((E, FF), dtype=jnp.float32), 'W2': jax.random.normal(ks[3], (E, FF, H), dtype=jnp.float32) * s, 'b2': jnp.zeros((E, H), dtype=jnp.float32)}
    _L1_ffn_all = _L1_ffn_setup()
    _L1_ffn_in = {k: v for k, v in _L1_ffn_all.items() if k in ('Wg', 'bg', 'W1', 'b1', 'W2', 'b2')}
    del _L1_ffn_all
    return {'x': x, 'L0_tok_emb_2': _L0_tok_in['emb_2'], 'L0_tok_emb_3': _L0_tok_in['emb_3'], 'L0_tok_emb_4': _L0_tok_in['emb_4'], 'L0_tok_proj_w': _L0_tok_in['proj_w'], 'L0_tok_proj_b': _L0_tok_in['proj_b'], 'L0_attn_Wqkv': _L0_attn_in['Wqkv'], 'L0_attn_bqkv': _L0_attn_in['bqkv'], 'L0_attn_Wproj': _L0_attn_in['Wproj'], 'L0_attn_bproj': _L0_attn_in['bproj'], 'L0_ffn_Wr_sp': _L0_ffn_in['Wr_sp'], 'L0_ffn_br_sp': _L0_ffn_in['br_sp'], 'L0_ffn_Wr_fq': _L0_ffn_in['Wr_fq'], 'L0_ffn_br_fq': _L0_ffn_in['br_fq'], 'L0_ffn_Ws1': _L0_ffn_in['Ws1'], 'L0_ffn_bs1': _L0_ffn_in['bs1'], 'L0_ffn_Ws2': _L0_ffn_in['Ws2'], 'L0_ffn_bs2': _L0_ffn_in['bs2'], 'L0_ffn_W1_sp': _L0_ffn_in['W1_sp'], 'L0_ffn_b1_sp': _L0_ffn_in['b1_sp'], 'L0_ffn_W2_sp': _L0_ffn_in['W2_sp'], 'L0_ffn_b2_sp': _L0_ffn_in['b2_sp'], 'L0_ffn_W1_fq': _L0_ffn_in['W1_fq'], 'L0_ffn_b1_fq': _L0_ffn_in['b1_fq'], 'L0_ffn_W2_fq': _L0_ffn_in['W2_fq'], 'L0_ffn_b2_fq': _L0_ffn_in['b2_fq'], 'L1_attn_in_w': _L1_attn_in['in_w'], 'L1_attn_conv_w': _L1_attn_in['conv_w'], 'L1_attn_conv_b': _L1_attn_in['conv_b'], 'L1_attn_xp_w': _L1_attn_in['xp_w'], 'L1_attn_dt_w': _L1_attn_in['dt_w'], 'L1_attn_dt_b': _L1_attn_in['dt_b'], 'L1_attn_A_log': _L1_attn_in['A_log'], 'L1_attn_D_skip': _L1_attn_in['D_skip'], 'L1_attn_out_w': _L1_attn_in['out_w'], 'L1_attn_fusion_w': _L1_attn_in['fusion_w'], 'L1_attn_fusion_b': _L1_attn_in['fusion_b'], 'L1_attn_ln_g': _L1_attn_in['ln_g'], 'L1_attn_ln_b': _L1_attn_in['ln_b'], 'L1_ffn_Wg': _L1_ffn_in['Wg'], 'L1_ffn_bg': _L1_ffn_in['bg'], 'L1_ffn_W1': _L1_ffn_in['W1'], 'L1_ffn_b1': _L1_ffn_in['b1'], 'L1_ffn_W2': _L1_ffn_in['W2'], 'L1_ffn_b2': _L1_ffn_in['b2']}

def reference(x, L0_tok_emb_2, L0_tok_emb_3, L0_tok_emb_4, L0_tok_proj_w, L0_tok_proj_b, L0_attn_Wqkv, L0_attn_bqkv, L0_attn_Wproj, L0_attn_bproj, L0_ffn_Wr_sp, L0_ffn_br_sp, L0_ffn_Wr_fq, L0_ffn_br_fq, L0_ffn_Ws1, L0_ffn_bs1, L0_ffn_Ws2, L0_ffn_bs2, L0_ffn_W1_sp, L0_ffn_b1_sp, L0_ffn_W2_sp, L0_ffn_b2_sp, L0_ffn_W1_fq, L0_ffn_b1_fq, L0_ffn_W2_fq, L0_ffn_b2_fq, L1_attn_in_w, L1_attn_conv_w, L1_attn_conv_b, L1_attn_xp_w, L1_attn_dt_w, L1_attn_dt_b, L1_attn_A_log, L1_attn_D_skip, L1_attn_out_w, L1_attn_fusion_w, L1_attn_fusion_b, L1_attn_ln_g, L1_attn_ln_b, L1_ffn_Wg, L1_ffn_bg, L1_ffn_W1, L1_ffn_b1, L1_ffn_W2, L1_ffn_b2):
    import jax
    import jax.numpy as jnp

    def _L0_tok_ref(byte_sequence, emb_2, emb_3, emb_4, proj_w, proj_b):
        import jax, jax.numpy as jnp
        import numpy as np
        NGRAM_SIZES = (2, 3, 4)
        HASH_VOCAB = 25000
        EMBED_DIM = 128
        BATCH, SEQ = (8, 1024)

        def _ngram_hash_ids(byte_sequence, n):
            L = byte_sequence.shape[1] - n + 1
            h = jnp.zeros((byte_sequence.shape[0], L), dtype=jnp.int64)
            for j in range(n):
                h = (h * 64 + byte_sequence[:, j:j + L]) % HASH_VOCAB
            return h

        def _ngram_embed(byte_sequence, table, n):
            B, S = byte_sequence.shape
            ids = _ngram_hash_ids(byte_sequence, n)
            emb = table[ids]
            out = jnp.zeros((B, S, table.shape[1]), dtype=table.dtype)
            c = n // 2
            return out.at[:, c:c + emb.shape[1]].set(emb)
        tables = (emb_2, emb_3, emb_4)
        combined = jnp.concatenate([_ngram_embed(byte_sequence, t, n) for t, n in zip(tables, NGRAM_SIZES)], axis=-1)
        return jnp.einsum('bsk,dk->bsd', combined, proj_w) + proj_b

    def _L0_attn_ref(x, Wqkv, bqkv, Wproj, bproj):
        import jax, jax.numpy as jnp
        import numpy as np
        B, N, C = (2, 1024, 128)
        NUM_HEADS = 8
        HEAD_DIM = C // NUM_HEADS
        SCALE = HEAD_DIM ** (-0.5)
        THETA = 10000.0

        def _rope(x, seq_len, head_dim):
            freqs = 1.0 / THETA ** (jnp.arange(0, head_dim, 2, dtype=jnp.float32) / head_dim)
            t = jnp.arange(seq_len, dtype=jnp.float32)
            freqs_cis = jnp.outer(t, freqs)
            sin_f = jnp.sin(freqs_cis)
            cos_f = jnp.cos(freqs_cis)
            x_even = x[..., ::2]
            x_odd = x[..., 1::2]
            rot = jnp.stack([x_even * cos_f - x_odd * sin_f, x_even * sin_f + x_odd * cos_f], axis=-1)
            return rot.reshape(x.shape)
        b, n, c = x.shape
        qkv = x @ Wqkv.T + bqkv
        qkv = qkv.reshape(b, n, 3, NUM_HEADS, HEAD_DIM)
        qkv = jnp.transpose(qkv, (2, 0, 3, 1, 4))
        q, k, v = (qkv[0], qkv[1], qkv[2])
        q = _rope(q, n, HEAD_DIM)
        k = _rope(k, n, HEAD_DIM)
        attn = jnp.einsum('bhqd,bhkd->bhqk', q, k) * SCALE
        attn = jax.nn.softmax(attn, axis=-1)
        out = jnp.einsum('bhqk,bhkd->bhqd', attn, v)
        out = jnp.transpose(out, (0, 2, 1, 3)).reshape(b, n, c)
        return out @ Wproj.T + bproj

    def _L0_ffn_ref(x, Wr_sp, br_sp, Wr_fq, br_fq, Ws1, bs1, Ws2, bs2, W1_sp, b1_sp, W2_sp, b2_sp, W1_fq, b1_fq, W2_fq, b2_fq):
        import math
        import jax, jax.numpy as jnp
        import numpy as np
        B, T, D, FF, E = (32, 256, 128, 512, 8)
        CAPACITY_FACTOR = 1.25
        CAP = int(math.ceil(CAPACITY_FACTOR * B * T / E))

        def _bank_residual(x2, Wr, br, W1, b1, W2, b2):
            N, d = x2.shape
            e = Wr.shape[1]
            logits = x2 @ Wr + br
            probs = jax.nn.softmax(logits, axis=-1)
            expert = jnp.argmax(probs, axis=-1)
            gate = jnp.take_along_axis(probs, expert[:, None], axis=-1)[:, 0]
            oneh = jax.nn.one_hot(expert, e, dtype=x2.dtype)
            pos = (jnp.cumsum(oneh, axis=0) * oneh).sum(-1).astype(jnp.int32) - 1
            keep = pos < CAP
            slot = expert.astype(jnp.int32) * CAP + jnp.minimum(pos, CAP - 1)
            xd = jnp.where(keep[:, None], x2, 0.0)
            buf = jnp.zeros((e * CAP, d), x2.dtype).at[slot].add(xd)
            buf = buf.reshape(e, CAP, d)
            h = jax.nn.gelu(jnp.einsum('ecd,edf->ecf', buf, W1) + b1[:, None, :], approximate=False)
            out = jnp.einsum('ecf,efd->ecd', h, W2) + b2[:, None, :]
            y = out.reshape(e * CAP, d)[slot]
            return y * (gate * keep.astype(x2.dtype))[:, None]
        b, t, d = x.shape
        x2 = x.reshape(b * t, d)
        shared = jax.nn.gelu(x2 @ Ws1 + bs1, approximate=False) @ Ws2 + bs2
        y = shared
        y = y + _bank_residual(x2, Wr_sp, br_sp, W1_sp, b1_sp, W2_sp, b2_sp)
        y = y + _bank_residual(x2, Wr_fq, br_fq, W1_fq, b1_fq, W2_fq, b2_fq)
        return y.reshape(b, t, d)

    def _L1_attn_ref(x, in_w, conv_w, conv_b, xp_w, dt_w, dt_b, A_log, D_skip, out_w, fusion_w, fusion_b, ln_g, ln_b):
        import jax, jax.numpy as jnp
        import numpy as np
        D_STATE = 16
        D_CONV = 4

        def _mamba(x, in_w, conv_w, conv_b, xp_w, dt_w, dt_b, A_log, D_skip, out_w):
            B, T, _ = x.shape
            di = conv_w.shape[0]
            xi, z = jnp.split(x @ in_w.T, 2, axis=-1)
            xpad = jnp.pad(xi, ((0, 0), (D_CONV - 1, 0), (0, 0)))
            xc = conv_b + sum((xpad[:, k:k + T, :] * conv_w[:, k] for k in range(D_CONV)))
            xc = jax.nn.silu(xc)
            dtr = dt_w.shape[1]
            dbl = xc @ xp_w.T
            dt, Bm, Cm = jnp.split(dbl, [dtr, dtr + D_STATE], axis=-1)
            dt = jax.nn.softplus(dt @ dt_w.T + dt_b)
            A = -jnp.exp(A_log)
            h0 = jnp.zeros((B, di, D_STATE), x.dtype)

            def step(h, inp):
                dt_t, B_t, C_t, x_t = inp
                h = h * jnp.exp(dt_t[:, :, None] * A) + (dt_t * x_t)[:, :, None] * B_t[:, None, :]
                return (h, jnp.einsum('bds,bs->bd', h, C_t))
            _, ys = jax.lax.scan(step, h0, (dt.transpose(1, 0, 2), Bm.transpose(1, 0, 2), Cm.transpose(1, 0, 2), xc.transpose(1, 0, 2)))
            y = ys.transpose(1, 0, 2) + xc * D_skip
            return y * jax.nn.silu(z) @ out_w.T

        def _interp_linear(x, size):
            Tin = x.shape[1]
            pos = jnp.clip((jnp.arange(size, dtype=jnp.float32) + 0.5) * (Tin / size) - 0.5, 0.0, Tin - 1.0)
            lo = jnp.floor(pos).astype(jnp.int32)
            hi = jnp.minimum(lo + 1, Tin - 1)
            w = (pos - lo.astype(jnp.float32))[None, :, None]
            return x[:, lo, :] * (1.0 - w) + x[:, hi, :] * w
        T = x.shape[1]
        outs = []
        for i in range(in_w.shape[0]):
            s = 2 ** i
            o = _mamba(x[:, ::s, :], in_w[i], conv_w[i], conv_b[i], xp_w[i], dt_w[i], dt_b[i], A_log[i], D_skip[i], out_w[i])
            if s > 1:
                o = _interp_linear(o, T)
            outs.append(o)
        f = jnp.concatenate(outs, axis=-1) @ fusion_w.T + fusion_b
        h = f + x
        mu = jnp.mean(h, axis=-1, keepdims=True)
        var = jnp.var(h, axis=-1, keepdims=True)
        return ln_g * (h - mu) / jnp.sqrt(var + 1e-05) + ln_b

    def _L1_ffn_ref(x, Wg, bg, W1, b1, W2, b2):
        import jax, jax.numpy as jnp
        import numpy as np
        H = 128
        FF = 4 * H
        E = 8
        K = 2
        B, S = (4, 1024)
        logits = x @ Wg + bg
        w, idx = jax.lax.top_k(logits, K)
        w = jax.nn.softmax(w, axis=-1)
        h = jax.nn.silu(jnp.einsum('bsh,ehf->ebsf', x, W1) + b1[:, None, None, :])
        y = jnp.einsum('ebsf,efh->ebsh', h, W2) + b2[:, None, None, :]
        comb = jnp.einsum('bske,bsk->ebs', jax.nn.one_hot(idx, E, dtype=x.dtype), w)
        return jnp.einsum('ebsh,ebs->bsh', y, comb)
    h = _L0_tok_ref(x, L0_tok_emb_2, L0_tok_emb_3, L0_tok_emb_4, L0_tok_proj_w, L0_tok_proj_b)
    h = h + _L0_attn_ref(_layernorm(h, axis=-1), L0_attn_Wqkv, L0_attn_bqkv, L0_attn_Wproj, L0_attn_bproj)
    h = h + _L0_ffn_ref(_layernorm(h, axis=-1), L0_ffn_Wr_sp, L0_ffn_br_sp, L0_ffn_Wr_fq, L0_ffn_br_fq, L0_ffn_Ws1, L0_ffn_bs1, L0_ffn_Ws2, L0_ffn_bs2, L0_ffn_W1_sp, L0_ffn_b1_sp, L0_ffn_W2_sp, L0_ffn_b2_sp, L0_ffn_W1_fq, L0_ffn_b1_fq, L0_ffn_W2_fq, L0_ffn_b2_fq)
    h = h + _L1_attn_ref(_layernorm(h, axis=-1), L1_attn_in_w, L1_attn_conv_w, L1_attn_conv_b, L1_attn_xp_w, L1_attn_dt_w, L1_attn_dt_b, L1_attn_A_log, L1_attn_D_skip, L1_attn_out_w, L1_attn_fusion_w, L1_attn_fusion_b, L1_attn_ln_g, L1_attn_ln_b)
    h = h + _L1_ffn_ref(_layernorm(h, axis=-1), L1_ffn_Wg, L1_ffn_bg, L1_ffn_W1, L1_ffn_b1, L1_ffn_W2, L1_ffn_b2)
    return h

_drawn_inputs = setup_inputs


def setup_inputs(seed=0):
    import zlib

    import numpy as np

    out = dict(_drawn_inputs(seed))
    spreads = {'L0_ffn_br_sp': (0.0, 0.1),
     'L0_ffn_br_fq': (0.0, 0.1),
     'L0_ffn_bs1': (0.0, 0.1),
     'L0_ffn_bs2': (0.0, 0.1),
     'L0_ffn_b1_sp': (0.0, 0.8),
     'L0_ffn_b2_sp': (0.0, 0.1),
     'L0_ffn_b1_fq': (0.0, 0.8),
     'L0_ffn_b2_fq': (0.0, 0.1),
     'L1_attn_conv_b': (0.0, 0.8),
     'L1_attn_D_skip': (1.0, 0.6),
     'L1_attn_fusion_b': (0.0, 0.1),
     'L1_attn_ln_g': (1.0, 0.2),
     'L1_attn_ln_b': (0.0, 0.1),
     'L1_ffn_bg': (0.0, 0.1),
     'L1_ffn_b1': (0.0, 0.679),
     'L1_ffn_b2': (0.0, 0.1)}
    factors = {'L0_attn_Wqkv': 4.888,
     'L0_attn_bqkv': 3.577,
     'L0_attn_Wproj': 3.013,
     'L0_ffn_W1_sp': 3.288,
     'L0_ffn_W2_sp': 3.015,
     'L0_ffn_W1_fq': 3.289,
     'L0_ffn_W2_fq': 2.981,
     'L1_attn_in_w': 8.0,
     'L1_attn_conv_w': 8.0,
     'L1_attn_xp_w': 8.0,
     'L1_attn_dt_w': 8.0,
     'L1_attn_dt_b': 8.0,
     'L1_attn_A_log': 8.0,
     'L1_attn_out_w': 8.0,
     'L1_attn_fusion_w': 8.0}
    for name, (base, spread) in spreads.items():
        noise = np.random.default_rng([zlib.crc32(name.encode()), seed]).standard_normal(out[name].shape)
        drawn = base * np.exp(spread * noise) if base else spread * noise
        out[name] = jnp.asarray(drawn.astype(out[name].dtype))
    for name, factor in factors.items():
        out[name] = (out[name] * factor).astype(out[name].dtype)
    return out
```

```python
from contextlib import ExitStack

import concourse.bass as bass
from concourse import mybir

F32 = mybir.dt.float32
BF16 = mybir.dt.bfloat16
I32 = mybir.dt.int32
U32 = mybir.dt.uint32
ALU = mybir.AluOpType
ACT = mybir.ActivationFunctionType
AX_X = mybir.AxisListType.X

P = 128
BATCH, SEQ, DM = 16, 1024, 128
TOK = BATCH * SEQ
TILES = TOK // P
TPB = SEQ // P
VOCAB = 25000
GRAMS = 3
LN_EPS = 1e-5


class Steps:

    def __init__(self, sem, base=0):
        self.sem, self.base, self.n = sem, base, 0

    def up(self, ins):
        self.n += 1
        ins.then_inc(self.sem, 1)
        return self.n

    def wait(self, eng, n=None):
        eng.wait_ge(self.sem, self.base + (self.n if n is None else n))

    def link(self, eng, ins):
        self.up(ins)
        self.wait(eng)


def embed_phase(nc, g, x, tables, proj_t, proj_b, slots_x):
    with ExitStack() as ctx:
        sb = lambda name, shape, dt=F32: ctx.enter_context(nc.sbuf_tensor("e_" + name, shape, dt))
        ps = lambda name, shape, dt=F32: ctx.enter_context(nc.psum_tensor("e_" + name, shape, dt))
        sem = lambda name: ctx.enter_context(nc.semaphore("e_" + name))
        W = P + 3
        xi = sb("xi", [P, W], I32)
        xf = sb("xf", [P, W])
        h2 = sb("h2", [P, W - 1])
        h3 = sb("h3", [P, W - 2])
        h4 = sb("h4", [P, W - 3])
        quo = sb("quo", [P, W], I32)
        tmp = sb("tmp", [P, W])
        raw = sb("raw", [P, W])
        ids = sb("ids", [P, TILES, GRAMS], U32)
        cols = sb("cols", [P, 2, TPB * GRAMS], U32)
        SLOTS = 4
        rows = sb("rows", [P, SLOTS, GRAMS * DM])
        rows_t = sb("rows_t", [P, 2, GRAMS * P])
        wproj = sb("wproj", [P, GRAMS, DM])
        bias = sb("bias", [P, DM])
        first = sb("first", [P, GRAMS])
        last = sb("last", [P, GRAMS])
        FILL = 8
        zeros = sb("zeros", [P, FILL, DM])
        turned = [ps(f"turned{i}", [P, 512]) for i in range(2)]
        summed = [ps(f"summed{i}", [P, 512]) for i in range(2)]

        s_zero = sem("x_zeroed")
        s_x = sem("x_loaded")
        s_w = sem("weights_loaded")
        s_fill = sem("zero_rows_set")
        s_filled = sem("slots_zeroed")
        s_mask0 = sem("masks_set")
        s_mask = sem("masks_ready")
        s_hash = sem("hash_steps")
        s_idst = sem("ids_turned")
        s_cols = sem("id_columns_ready")
        s_rows = [sem(f"rows_gathered{i}") for i in range(SLOTS)]
        s_masked = sem("rows_masked")
        s_turned = sem("rows_turned")
        s_rt = sem("rows_t_ready")
        s_sum = sem("projection_done")
        s_h = sem("h_written")
        s_pool = sem("pool_step")
        block = ctx.enter_context(nc.Block())
        x2 = x.rearrange("b (t p) -> (b t) p", p=P)
        PAIRS = BATCH // 2
        T2 = 2 * TPB

        @block.sync
        def _(sp):
            sp.dma_start(wproj[:], proj_t.rearrange("(g f) d -> f g d", g=GRAMS)).then_inc(s_w, 16)
            sp.dma_start(bias[:], proj_b.partition_broadcast(P)).then_inc(s_w, 16)
            sp.wait_ge(s_zero, 1)
            with nc.allow_non_contiguous_dma(reason="halo columns of the token ids"):
                sp.dma_start(xi[:, 2:P + 2], x2).then_inc(s_x, 16)
                sp.dma_start(xi[1:P, 0:2], x2[0:P - 1, P - 2:P]).then_inc(s_x, 16)
                sp.dma_start(xi[0:P - 1, P + 2:P + 3], x2[1:P, 0:1]).then_inc(s_x, 16)
            sp.wait_ge(s_fill, 1)
            fills = slots_x.shape[0] // (P * FILL)
            with sp.Fori(0, fills) as i:
                sp.dma_start(slots_x[bass.ds(i * (P * FILL), P * FILL), :].rearrange("(p j) d -> p j d", p=P),
                             zeros[:]).then_inc(s_filled, 16)
            sp.wait_ge(s_filled, fills * 16)

        @block.gpsimd
        def _(pool):
            nc.gpsimd.memset(zeros[:], 0.0).then_inc(s_fill, 1)
            nc.gpsimd.memset(first[:], 1.0).then_inc(s_mask0, 1)
            nc.gpsimd.memset(last[:], 1.0).then_inc(s_mask0, 1)
            pool.wait_ge(s_mask0, 2)
            for gram in range(GRAMS):
                lead = (gram + 2) // 2
                tail = gram + 1 - lead
                nc.gpsimd.affine_select(out=first[:, gram:gram + 1], in_=first[:, gram:gram + 1],
                                        compare_op=ALU.is_ge, fill=0.0, base=-lead, pattern=[[0, 1]],
                                        channel_multiplier=1).then_inc(s_mask, 1)
                nc.gpsimd.affine_select(out=last[:, gram:gram + 1], in_=last[:, gram:gram + 1],
                                        compare_op=ALU.is_ge, fill=0.0, base=P - 1 - tail, pattern=[[0, 1]],
                                        channel_multiplier=-1).then_inc(s_mask, 1)

            def gather(i, j, reused):
                slot = j % SLOTS
                if j % TPB == 0:
                    pool.wait_ge(s_cols, 2 * i + j // TPB + 1)
                if reused:
                    pool.wait_ge(s_turned, i * T2 + j - SLOTS + 1)
                pool.sem_inc(s_pool, 1)
                for gram in range(GRAMS):
                    c = (j % TPB) * GRAMS + gram
                    nc.gpsimd.indirect_dma_start(
                        rows[:, slot, gram * DM:(gram + 1) * DM], None, tables[gram],
                        bass.IndirectOffsetOnAxis(ap=cols[:, j // TPB, c:c + 1], axis=0)).then_inc(s_rows[slot], 16)

            for j in range(T2):
                gather(0, j, j >= SLOTS)
            with pool.Fori(1, PAIRS) as i:
                for j in range(T2):
                    gather(i, j, True)

        @block.vector
        def _(dve):
            st = Steps(s_hash)
            nc.vector.memset(xi[:], 0).then_inc(s_zero, 1)
            dve.wait_ge(s_x, 48)
            st.link(dve, nc.vector.tensor_copy(xf[:], xi[:]))

            def step(out, prev, nxt, n):
                r, t, q = raw[:, 0:n], tmp[:, 0:n], quo[:, 0:n]
                st.link(dve, nc.vector.scalar_tensor_tensor(out=r, in0=prev, scalar=64.0, in1=nxt,
                                                            op0=ALU.mult, op1=ALU.add))
                st.link(dve, nc.vector.tensor_scalar(q, r, 1.0 / VOCAB, None, ALU.mult))
                st.link(dve, nc.vector.tensor_copy(t, q))
                st.link(dve, nc.vector.scalar_tensor_tensor(out=r, in0=t, scalar=-float(VOCAB), in1=r,
                                                            op0=ALU.mult, op1=ALU.add))
                st.link(dve, nc.vector.tensor_scalar(t, r, 0.0, float(VOCAB), ALU.is_lt, ALU.mult))
                st.link(dve, nc.vector.tensor_tensor(r, r, t, ALU.add))
                st.link(dve, nc.vector.tensor_scalar(t, r, float(VOCAB), -float(VOCAB), ALU.is_ge, ALU.mult))
                st.link(dve, nc.vector.tensor_tensor(out, r, t, ALU.add))

            step(h2[:], xf[:, 0:W - 1], xf[:, 1:W], W - 1)
            step(h3[:], h2[:, 0:W - 2], xf[:, 2:W], W - 2)
            step(h4[:], h3[:, 0:W - 3], xf[:, 3:W], W - 3)
            dve.wait_ge(s_idst, GRAMS)
            st.link(dve, nc.vector.tensor_copy(ids[:].rearrange("p t g -> p g t"),
                                               turned[0][:, 0:GRAMS * P].rearrange("p (g t) -> p g t", g=GRAMS)))
            nc.vector.tensor_copy(cols[:, 0, :], ids[:, 0:TPB, :]).then_inc(s_cols, 1)
            nc.vector.tensor_copy(cols[:, 1, :], ids[:, TPB:2 * TPB, :]).then_inc(s_cols, 1)
            dve.wait_ge(s_w, 32)

            def mask(i, j):
                if j % TPB in (0, TPB - 1):
                    slot, m = j % SLOTS, first if j % TPB == 0 else last
                    dve.wait_ge(s_rows[slot], i * (T2 // SLOTS * 48) + (j // SLOTS + 1) * 48)
                    for gram in range(GRAMS):
                        c = slice(gram * DM, (gram + 1) * DM)
                        ins = nc.vector.tensor_scalar(rows[:, slot, c], rows[:, slot, c], m[:, gram:gram + 1], None,
                                                      ALU.mult)
                    ins.then_inc(s_masked, 1)

            def finish(i, j, tile):
                dve.wait_ge(s_sum, i * T2 + j + 1)
                nc.vector.tensor_tensor(g.h[:, tile, :], summed[j % 2][:, 0:DM], bias[:], ALU.add).then_inc(s_h, 1)
                dve.wait_ge(s_h, i * T2 + j + 1)
                nc.vector.bn_stats(g.stat[:, tile, :], g.h[:, tile, :])

            dve.wait_ge(s_mask, 2 * GRAMS)

            def tiles(i, fill):
                for j in range(T2):
                    mask(i, j)
                    if j >= 1:
                        finish(i, j - 1, i * T2 + (j - 1))
                    if fill and j % TPB == TPB - 1:
                        half = j // TPB
                        for slot in range(SLOTS):
                            dve.wait_ge(s_rows[slot], i * (T2 // SLOTS * 48) + (half + 1) * (TPB // SLOTS) * 48)
                        nc.vector.tensor_copy(cols[:, half, :],
                                              ids[:, bass.ds((i + 1) * T2 + half * TPB, TPB), :]).then_inc(s_cols, 1)
                finish(i, T2 - 1, i * T2 + (T2 - 1))

            with dve.Fori(0, PAIRS - 1) as i:
                tiles(i, True)
            tiles(PAIRS - 1, False)

        @block.scalar
        def _(act):
            def spread(i, j, reused):
                act.wait_ge(s_turned, i * T2 + j + 1)
                if reused:
                    act.wait_ge(s_sum, i * T2 + j - 1)
                nc.scalar.activation(rows_t[:, j % 2, :], turned[j % 2][:, 0:GRAMS * P], ACT.Copy).then_inc(s_rt, 1)

            for j in range(T2):
                spread(0, j, j >= 2)
            with act.Fori(1, PAIRS) as i:
                for j in range(T2):
                    spread(i, j, True)

        @block.tensor
        def _(pe):
            pe.wait_ge(s_hash, 1 + 8 * GRAMS)
            for gram, src in enumerate((h2[:, 1:P + 1], h3[:, 1:P + 1], h4[:])):
                nc.tensor.transpose(turned[0][:, gram * P:(gram + 1) * P], src, g.ident[:]).then_inc(s_idst, 1)
            pe.wait_ge(s_hash, 2 + 8 * GRAMS)
            pe.wait_ge(s_w, 32)

            def turn(i, j, reused):
                slot = j % SLOTS
                pe.wait_ge(s_rows[slot], i * (T2 // SLOTS * 48) + (j // SLOTS + 1) * 48)
                if j % TPB in (0, TPB - 1):
                    pe.wait_ge(s_masked, 4 * i + 2 * (j // TPB) + (1 if j % TPB == 0 else 2))
                if reused:
                    pe.wait_ge(s_rt, i * T2 + j - 1)
                for gram in range(GRAMS):
                    ins = nc.tensor.transpose(turned[j % 2][:, gram * P:(gram + 1) * P],
                                              rows[:, slot, gram * DM:(gram + 1) * DM], g.ident[:])
                ins.then_inc(s_turned, 1)

            def project(i, j, reused):
                pe.wait_ge(s_rt, i * T2 + j + 1)
                if reused:
                    pe.wait_ge(s_h, i * T2 + j - 1)
                for gram in range(GRAMS):
                    ins = nc.tensor.matmul(summed[j % 2][:, 0:DM], rows_t[:, j % 2, gram * P:(gram + 1) * P],
                                           wproj[:, gram, :], start=(gram == 0), stop=(gram == GRAMS - 1))
                ins.then_inc(s_sum, 1)

            for j in range(T2):
                turn(0, j, j >= 2)
                if j >= 1:
                    project(0, j - 1, j - 1 >= 2)
            with pe.Fori(1, PAIRS) as i:
                project(i - 1, T2 - 1, True)
                for j in range(T2):
                    turn(i, j, True)
                    if j >= 1:
                        project(i, j - 1, True)
            project(PAIRS - 1, T2 - 1, True)


class Resident:
    pass


def setup(nc, ctx, identity):
    g = Resident()
    sb = lambda name, shape, dt=F32: ctx.enter_context(nc.sbuf_tensor("g_" + name, shape, dt))
    g.stat = sb("stat", [P, TILES, 6])
    g.mean = sb("mean", [P, TILES])
    g.rstd = sb("rstd", [P, TILES])
    g.ident = sb("ident", [P, P])
    with nc.semaphore("g_identity_loaded") as s_id, nc.Block() as block:
        @block.sync
        def _(sp):
            sp.dma_start(g.ident[:], identity).then_inc(s_id, 16)
            sp.wait_ge(s_id, 16)
    return g


def setup_h(nc, ctx, g):
    sb = lambda name, shape, dt=F32: ctx.enter_context(nc.sbuf_tensor("g_" + name, shape, dt))
    g.h = sb("h", [P, TILES, DM])


def setup_slots(nc, ctx, g):
    sb = lambda name, shape, dt=F32: ctx.enter_context(nc.sbuf_tensor("g_" + name, shape, dt))
    g.gate = sb("gate", [P, TILES, BANKS])
    g.slot = sb("slot", [P, TILES, BANKS], U32)


def norm_phase(nc, g, name="n"):
    with ExitStack() as ctx:
        sb = lambda part, shape, dt=F32: ctx.enter_context(nc.sbuf_tensor(f"{name}_{part}", shape, dt))
        diff = sb("diff", [P, TILES])
        var = sb("var", [P, TILES])
        std = sb("std", [P, TILES])
        eps = sb("eps", [P, 1])
        s_step = ctx.enter_context(nc.semaphore(name + "_vector_step"))
        s_std = ctx.enter_context(nc.semaphore(name + "_std_ready"))
        block = ctx.enter_context(nc.Block())

        @block.vector
        def _(dve):
            st = Steps(s_step)
            st.up(nc.vector.memset(eps[:], LN_EPS))
            m0, m1, v0, v1 = (g.stat[:, :, c] for c in (1, 4, 2, 5))
            st.link(dve, nc.vector.tensor_tensor(diff[:], m0, m1, ALU.subtract))
            st.link(dve, nc.vector.tensor_tensor(g.mean[:], m0, m1, ALU.add))
            st.link(dve, nc.vector.tensor_scalar(g.mean[:], g.mean[:], 0.5, None, ALU.mult))
            st.link(dve, nc.vector.tensor_tensor(var[:], v0, v1, ALU.add))
            st.link(dve, nc.vector.tensor_tensor(diff[:], diff[:], diff[:], ALU.mult))
            st.link(dve, nc.vector.tensor_scalar(diff[:], diff[:], 0.25 * DM, None, ALU.mult))
            st.link(dve, nc.vector.tensor_tensor(var[:], var[:], diff[:], ALU.add))
            dve.wait_ge(s_std, 1)
            nc.vector.reciprocal(g.rstd[:], std[:])

        @block.scalar
        def _(act):
            act.wait_ge(s_step, 8)
            nc.scalar.activation(std[:], var[:], ACT.Sqrt, bias=eps[:], scale=1.0 / DM).then_inc(s_std, 1)


HEADS, HD = 8, 16
TERMS = ((0, 0), (0, 1), (0, 2), (1, 0), (1, 1), (2, 0))
KQ = HD * len(TERMS)
QUAD = 4
HALF = 512


def attention_phase(nc, g, w_qkv, b_qk, b_v, w_proj, b_proj, cos_t, sin_t, part_rows, max_rows):
    with ExitStack() as ctx:
        sb = lambda name, shape, dt=F32: ctx.enter_context(nc.sbuf_tensor("a_" + name, shape, dt))
        ps = lambda name, shape, dt=F32: ctx.enter_context(nc.psum_tensor("a_" + name, shape, dt))
        sem = lambda name: ctx.enter_context(nc.semaphore("a_" + name))
        wqkv = sb("wqkv", [P, 5, DM])
        bqk = sb("bqk", [P, 4])
        rowb = sb("rowb", [1, 3, DM])
        wproj = sb("wproj", [P, DM])
        cos = sb("cos", [P, SEQ])
        sin = sb("sin", [P, SEQ])
        xt = sb("xt", [P, SEQ])
        rope = [sb(f"rope{m}", [P, SEQ]) for m in range(2)]
        ot = rope[0]
        xn = rope[1][:].rearrange("p (i d) -> p i d", d=DM)
        aot = xt
        parts = [sb(f"parts{n}", [P, 3, SEQ], BF16) for n in range(2)]
        qs = [sb(f"qs{n}", [KQ + 3, HEADS, SEQ], BF16) for n in range(2)]
        ks = [sb(f"ks{n}", [KQ + 3, HEADS, SEQ], BF16) for n in range(2)]
        va = [sb(f"va{n}", [P, TPB, HEADS, 32]) for n in range(2)]
        RING = 4
        pt = sb("pt", [P, RING, SEQ])
        tops = sb("tops", [P, P])
        neg = sb("neg", [HEADS * TPB, P])
        rest = sb("rest", [HEADS * TPB, P])
        negp = sb("negp", [HEADS * TPB, 3, P], BF16)
        inv = sb("inv", [P, TPB, QUAD])
        ao = sb("ao", [P, TPB, DM])
        score = [ps(f"score{n}", [P, SEQ]) for n in range(2)]
        acc = ps("acc", [P, SEQ])
        work = ps("work", [P, SEQ])

        s_load = sem("weights_loaded")
        s_ones = sem("constants_set")
        s_xn = sem("norm_applied")
        s_ready = sem("work_ready")
        s_free = sem("work_free")
        s_rope = sem("rope_terms_ready")
        s_split = sem("split_steps")
        s_stack = sem("stack_loaded")
        s_pst = sem("parts_stored")
        s_neg = sem("max_split_steps")
        s_mst = sem("max_rows_stored")
        s_mld = sem("max_rows_loaded")
        s_score = sem("scores_ready")
        s_exp = sem("probs_ready")
        s_pv = sem("values_summed")
        s_oa = sem("out_copied_act")
        s_od = sem("out_copied_dve")
        s_ao = sem("norm_steps")
        s_poolstep = sem("pool_step")
        block = ctx.enter_context(nc.Block())

        SLOTS = HEADS * TPB
        LAG = 22
        MAXES = [("max", h, i) for h in range(HEADS) for i in range(TPB)]
        PREP = [("turn",), ("q", 0), ("q", 1), ("v",), ("q", 2), ("q", 3)]

        def place(slot):
            return slot // (SLOTS // 2), slot % (SLOTS // 2) // QUAD, slot % QUAD

        def schedule(prev, nxt):
            at = [([], []) for _ in range(SLOTS)]
            if nxt:
                for s, u in zip((5, 7, 8, 9, 13, 14), PREP):
                    at[s][0].append(u)
            if prev:
                for s, u in zip((1, 2, 4), (("out", 1), ("heads",), ("proj",))):
                    at[s][0].append(u)
            at[35][0].append(("out", 0))
            if nxt:
                todo = list(MAXES)
                span = range(LAG, 57)
                for k, s in enumerate(span):
                    share = len(todo) // (len(span) - k) + (len(todo) % (len(span) - k) > 0)
                    for n in range(share):
                        pos = 1 if n or at[s][0] else 0
                        at[s][pos].append(todo.pop(0))
                at[58][0].append(("tops",))
            return at

        FULL = schedule(True, True)
        NUSE = sum(len(a) + len(b) for a, b in FULL)
        FIRST_USES = len(PREP) + len(MAXES) + 1
        NFIRST = sum(len(a) + len(b) for a, b in schedule(False, True))

        def use_base(b):
            return FIRST_USES + NFIRST + NUSE * (b - 1)

        def walk(main):
            main(0, 0, FIRST_USES, schedule(False, True), False, True)
            return (lambda i: (main(i * 2 + 1, 1, use_base(i * 2 + 1), FULL, True, True),
                               main(i * 2 + 2, 0, use_base(i * 2 + 2), FULL, True, True)))

        LAST = BATCH - 1
        LAST_USE = use_base(LAST)
        END_PLAN = schedule(True, False)
        END_USE = LAST_USE + sum(len(a) + len(b) for a, b in END_PLAN)
        TAIL = [("out", 1), ("heads",), ("proj",)]

        @block.sync
        def _(sp):
            sp.dma_start(wqkv[:], w_qkv).then_inc(s_load, 16)
            sp.dma_start(bqk[:], b_qk).then_inc(s_load, 16)
            sp.dma_start(rowb[0:1, 0, :], b_v).then_inc(s_load, 16)
            sp.dma_start(rowb[0:1, 1, :], b_proj).then_inc(s_load, 16)
            sp.dma_start(wproj[:], w_proj).then_inc(s_load, 16)
            sp.dma_start(cos[:], cos_t).then_inc(s_load, 16)
            sp.dma_start(sin[:], sin_t).then_inc(s_load, 16)

            def stack(b, k):
                for n, dst in enumerate((qs[k], ks[k])):
                    sp.wait_ge(s_split, b * 10 + 5 * n + 5)
                    sp.dma_start(part_rows[n], parts[n][:]).then_inc(s_pst, 16)
                    sp.wait_ge(s_pst, b * 32 + 16 * n + 16)
                    for t, term in enumerate(TERMS):
                        src = part_rows[n, :, term[n], :].rearrange("(h d) t -> d h t", d=HD)
                        sp.dma_start(dst[t * HD:(t + 1) * HD, :, :], src).then_inc(s_stack, 16)
                sp.wait_ge(s_neg, b * 4 + 4)
                sp.dma_start(max_rows.rearrange("j (u q) -> u j q", q=P), negp[:]).then_inc(s_mst, 16)
                sp.wait_ge(s_mst, b * 16 + 16)
                sp.dma_start(qs[k][KQ:KQ + 3, :, :], max_rows.rearrange("j (h q) -> j h q", h=HEADS)).then_inc(s_mld, 16)

            stack(0, 0)
            stack(1, 1)
            with sp.Fori(0, (BATCH - 2) // 2) as i:
                stack(i * 2 + 2, 0)
                stack(i * 2 + 3, 1)

        @block.gpsimd
        def _(pool):
            st = Steps(s_ones)
            for n in range(2):
                st.link(pool, nc.gpsimd.memset(va[n][:], 1.0))
                st.link(pool, nc.gpsimd.memset(ks[n][KQ:KQ + 3, :, :], 1.0))
            st.link(pool, nc.gpsimd.memset(rowb[0:1, 2, :], 1.0))
            st.link(pool, nc.gpsimd.memset(tops[:, HEADS * TPB:], 0.0))

            def linked(st, ins):
                st.link(pool, ins)
                pool.sem_inc(s_poolstep, 1)

            def split(b, first):
                for n in range(2):
                    st = Steps(s_split, b * 10 + n * 5)
                    a, c = rope
                    hi, mid, lo = (parts[n][:, m, :] for m in range(3))
                    pool.wait_ge(s_rope, b * 2 + n + 1)
                    if not first:
                        pool.wait_ge(s_pst, b * 32)
                    pool.sem_inc(s_poolstep, 1)
                    linked(st, nc.gpsimd.tensor_tensor(a[:], a[:], c[:], ALU.add))
                    linked(st, nc.gpsimd.tensor_copy(hi, a[:]))
                    linked(st, nc.gpsimd.tensor_tensor(c[:], a[:], hi, ALU.subtract))
                    linked(st, nc.gpsimd.tensor_copy(mid, c[:]))
                    st.up(nc.gpsimd.tensor_tensor(lo, c[:], mid, ALU.subtract))

            split(0, True)
            with pool.Fori(1, BATCH) as b:
                split(b, False)

        @block.scalar
        def _(act):
            def consume(u, use, b, k):
                kind = use[0]
                if kind not in ("turn", "v", "heads"):
                    return
                act.wait_ge(s_ready, u + 1)
                if kind == "turn":
                    nc.scalar.activation(xt[:], work[:], ACT.Copy).then_inc(s_free, 1)
                elif kind == "v":
                    nc.scalar.activation(va[k][:, :, :, 0:HD], work[:].rearrange("p (i h d) -> p i h d", h=HEADS, d=HD),
                                         ACT.Copy).then_inc(s_free, 1)
                else:
                    nc.scalar.activation(aot[:], work[:], ACT.Copy).then_inc(s_free, 1)

            def copy_out(n, used):
                act.wait_ge(s_pv, n * (SLOTS // 2) + SLOTS // 2)
                if used is not None:
                    act.wait_ge(s_ready, used)
                nc.scalar.activation(ot[:, 0:HALF], acc[:, 0:HALF], ACT.Copy).then_inc(s_oa, 1)

            def main(b, k, base, plan, prev, nxt):
                u = base
                outs = {use[1]: n for n, use in enumerate(x for a, c in plan for x in a + c) if use[0] == "out"}
                for s in range(SLOTS):
                    n = b * SLOTS + s
                    act.wait_ge(s_score, n + 1)
                    if prev or s >= RING:
                        act.wait_ge(s_pv, n - RING + 1)
                    nc.scalar.activation(pt[:, s % RING, :], score[s % 2][:], ACT.Exp, scale=HD ** -0.5).then_inc(s_exp, 1)
                    if s == 0 and prev:
                        copy_out(b * 2 - 1, None)
                    if s == SLOTS // 2:
                        copy_out(b * 2, base + outs[1] + 1 if prev else None)
                    for use in plan[s][0] + plan[s][1]:
                        consume(u, use, b, 1 - k)
                        u = u + 1

            for n, use in enumerate(PREP):
                consume(n, use, 0, 0)
            rest_of = walk(main)
            with act.Fori(0, (BATCH - 2) // 2) as i:
                rest_of(i)
            main(LAST, LAST % 2, LAST_USE, END_PLAN, True, False)
            copy_out(LAST * 2 + 1, None)
            for n, use in enumerate(TAIL):
                consume(END_USE + n, use, LAST, 0)

        @block.vector
        def _(dve):
            def norm(b):
                for j in range(TPB):
                    tile = b * TPB + j
                    ins = nc.vector.tensor_scalar(xn[:, j, :], g.h[:, bass.ds(tile, 1), :].rearrange("p o d -> p (o d)"),
                                                  g.mean[:, bass.ds(tile, 1)],
                                                  g.rstd[:, bass.ds(tile, 1)], ALU.subtract, ALU.mult)
                ins.then_inc(s_xn, 1)

            def consume(u, use, b, nb, prev):
                kind = use[0]
                if kind in ("turn", "v", "heads"):
                    return
                dve.wait_ge(s_ready, u + 1)
                if kind == "q":
                    n, m = divmod(use[1], 2)
                    if m == 0 and (prev or n):
                        dve.wait_ge(s_split, nb * 10 + n * 5)
                    ins = nc.vector.scalar_tensor_tensor(out=rope[m][:], in0=work[:], scalar=bqk[:, use[1]:use[1] + 1],
                                                         in1=(cos, sin)[m][:], op0=ALU.add, op1=ALU.mult)
                    ins.then_inc(s_free, 1)
                    if m:
                        dve.wait_ge(s_free, u + 1)
                        dve.sem_inc(s_rope, 1)
                elif kind == "max":
                    col = use[1] * TPB + use[2]
                    nc.vector.tensor_reduce(tops[:, col:col + 1], work[:], AX_X, ALU.max).then_inc(s_free, 1)
                elif kind == "tops":
                    st = Steps(s_neg, nb * 4)
                    if prev:
                        dve.wait_ge(s_mst, nb * 16)
                    nc.vector.tensor_scalar(neg[:], work[0:HEADS * TPB, 0:P], -1.0, None, ALU.mult).then_inc(s_free, 1)
                    dve.wait_ge(s_free, u + 1)
                    st.link(dve, nc.vector.tensor_copy(negp[:, 0, :], neg[:]))
                    st.link(dve, nc.vector.tensor_tensor(rest[:], neg[:], negp[:, 0, :], ALU.subtract))
                    st.link(dve, nc.vector.tensor_copy(negp[:, 1, :], rest[:]))
                    st.up(nc.vector.tensor_tensor(negp[:, 2, :], rest[:], negp[:, 1, :], ALU.subtract))
                elif kind == "out":
                    quad = use[1]
                    w = work[:].rearrange("p (i h c) -> p i h c", h=QUAD, c=32)
                    n = b * 2 + quad
                    nc.vector.reciprocal(inv[:], w[:, :, :, HD]).then_inc(s_ao, 1)
                    dve.wait_ge(s_ao, n * 2 + 1)
                    view = ao[:, :, quad * QUAD * HD:(quad + 1) * QUAD * HD].rearrange("p i (h d) -> p i h d", d=HD)
                    for i in range(TPB):
                        ins = nc.vector.tensor_tensor(view[:, i], w[:, i, :, 0:HD],
                                                      inv[:, i, :].to_broadcast([P, QUAD, HD]), ALU.mult)
                    ins.then_inc(s_free, 1)
                    dve.wait_ge(s_free, u + 1)
                    dve.sem_inc(s_ao, 1)
                elif kind == "proj":
                    tiles = g.h[:, bass.ds(b * TPB, TPB), :].rearrange("p i d -> p (i d)")
                    nc.vector.tensor_tensor(tiles, tiles, work[:], ALU.add).then_inc(s_free, 1)
                    dve.wait_ge(s_free, u + 1)
                    for j in range(TPB):
                        tile = b * TPB + j
                        nc.vector.bn_stats(g.stat[:, bass.ds(tile, 1), :], g.h[:, bass.ds(tile, 1), :])

            def copy_out(n, used):
                dve.wait_ge(s_pv, n * (SLOTS // 2) + SLOTS // 2)
                if used is not None:
                    dve.wait_ge(s_ready, used)
                nc.vector.tensor_copy(ot[:, HALF:SEQ], acc[:, HALF:SEQ]).then_inc(s_od, 1)

            def main(b, k, base, plan, prev, nxt):
                u = base
                outs = {use[1]: n for n, use in enumerate(x for a, c in plan for x in a + c) if use[0] == "out"}
                if nxt:
                    dve.wait_ge(s_free, u)
                    norm(b + 1)
                for s in range(SLOTS):
                    if s == 0 and prev:
                        copy_out(b * 2 - 1, None)
                    if s == SLOTS // 2:
                        copy_out(b * 2, base + outs[1] + 1 if prev else None)
                    for use in plan[s][0] + plan[s][1]:
                        row = b - 1 if use[0] in ("heads", "proj") or use == ("out", 1) else b
                        consume(u, use, row, b + 1, True)
                        u = u + 1

            dve.wait_ge(s_load, 7 * 16)
            norm(0)
            for n, use in enumerate(PREP + MAXES + [("tops",)]):
                consume(n, use, 0, 0, False)
            rest_of = walk(main)
            with dve.Fori(0, (BATCH - 2) // 2) as i:
                rest_of(i)
            main(LAST, LAST % 2, LAST_USE, END_PLAN, True, False)
            copy_out(LAST * 2 + 1, None)
            for n, use in enumerate(TAIL):
                consume(END_USE + n, use, LAST, 0, True)

        @block.tensor
        def _(pe):
            def produce(u, use, b, nb, k, first=False):
                kind = use[0]
                if not first:
                    pe.wait_ge(s_free, u)
                if kind == "turn":
                    pe.wait_ge(s_xn, nb + 1)
                    for j in range(TPB):
                        ins = nc.tensor.transpose(work[:, j * P:(j + 1) * P], xn[:, j, :], g.ident[:])
                elif kind == "q":
                    for c in range(2):
                        ins = nc.tensor.matmul(work[:, c * HALF:(c + 1) * HALF], wqkv[:, use[1], :],
                                               xt[:, c * HALF:(c + 1) * HALF], start=True, stop=True)
                elif kind == "v":
                    for j in range(TPB):
                        o = work[:, j * P:(j + 1) * P]
                        nc.tensor.matmul(o, xt[:, j * P:(j + 1) * P], wqkv[:, 4, :], start=True, stop=False)
                        ins = nc.tensor.matmul(o, rowb[0:1, 2, :], rowb[0:1, 0, :], start=False, stop=True)
                elif kind == "max":
                    _, h, i = use
                    if (h, i) == (0, 0):
                        pe.wait_ge(s_stack, nb * 192 + 192)
                    for c in range(2):
                        ins = nc.tensor.matmul(work[:, c * HALF:(c + 1) * HALF], qs[k][0:KQ, h, i * P:(i + 1) * P],
                                               ks[k][0:KQ, h, c * HALF:(c + 1) * HALF], start=True, stop=True)
                elif kind == "tops":
                    ins = nc.tensor.transpose(work[:, 0:P], tops[:], g.ident[:])
                elif kind == "out":
                    n = b * 2 + use[1] + 1
                    pe.wait_ge(s_oa, n)
                    pe.wait_ge(s_od, n)
                    for j in range(TPB):
                        ins = nc.tensor.transpose(work[:, j * P:(j + 1) * P], ot[:, j * P:(j + 1) * P], g.ident[:])
                elif kind == "heads":
                    pe.wait_ge(s_ao, b * 4 + 4)
                    for j in range(TPB):
                        ins = nc.tensor.transpose(work[:, j * P:(j + 1) * P], ao[:, j, :], g.ident[:])
                elif kind == "proj":
                    for j in range(TPB):
                        o = work[:, j * P:(j + 1) * P]
                        nc.tensor.matmul(o, aot[:, j * P:(j + 1) * P], wproj[:], start=True, stop=False)
                        ins = nc.tensor.matmul(o, rowb[0:1, 2, :], rowb[0:1, 1, :], start=False, stop=True)
                ins.then_inc(s_ready, 1)

            def scores(b, k, s, reused):
                quad, i, hq = place(s)
                h = quad * QUAD + hq
                n = b * SLOTS + s
                if s == 0:
                    pe.wait_ge(s_mld, b * 16 + 16)
                if reused:
                    pe.wait_ge(s_exp, n - 1)
                for c in range(2):
                    ins = nc.tensor.matmul(score[s % 2][:, c * HALF:(c + 1) * HALF], ks[k][:, h, i * P:(i + 1) * P],
                                           qs[k][:, h, c * HALF:(c + 1) * HALF], start=True, stop=True)
                ins.then_inc(s_score, 1)

            def values(b, k, s, c):
                quad, i, hq = place(s)
                h = quad * QUAD + hq
                ins = nc.tensor.matmul(acc[32 * hq:32 * hq + 32, c * HALF:(c + 1) * HALF], va[k][:, i, h, :],
                                       pt[:, s % RING, c * HALF:(c + 1) * HALF], start=(i == 0), stop=(i == TPB - 1),
                                       tile_position=(0, 32 * hq))
                if c == 1:
                    ins.then_inc(s_pv, 1)

            def main(b, k, base, plan, prev, nxt):
                u = base
                for s in range(SLOTS):
                    row = b
                    for use in plan[s][0]:
                        row = b - 1 if use[0] in ("heads", "proj") or use == ("out", 1) else b
                        produce(u, use, row, b + 1, 1 - k)
                        u = u + 1
                    if s + 1 < SLOTS:
                        scores(b, k, s + 1, prev or s >= 1)
                    elif nxt:
                        scores(b + 1, 1 - k, 0, True)
                    pe.wait_ge(s_exp, b * SLOTS + s + 1)
                    if s % (SLOTS // 2) == 0 and (prev or s):
                        n = b * 2 + s // (SLOTS // 2)
                        pe.wait_ge(s_oa, n)
                        pe.wait_ge(s_od, n)
                    values(b, k, s, 0)
                    for use in plan[s][1]:
                        row = b - 1 if use[0] in ("heads", "proj") or use == ("out", 1) else b
                        produce(u, use, row, b + 1, 1 - k)
                        u = u + 1
                    values(b, k, s, 1)

            pe.wait_ge(s_load, 7 * 16)
            pe.wait_ge(s_ones, 6)
            for n, use in enumerate(PREP + MAXES + [("tops",)]):
                produce(n, use, 0, 0, 0, n == 0)
            scores(0, 0, 0, False)
            rest_of = walk(main)
            with pe.Fori(0, (BATCH - 2) // 2) as i:
                rest_of(i)
            main(LAST, LAST % 2, LAST_USE, END_PLAN, True, False)
            for n, use in enumerate(TAIL):
                produce(END_USE + n, use, LAST, 0, 0)


EXPERTS, FF = 8, 512
FT = FF // P
CAP = -(-5 * 32 * 256 // (4 * EXPERTS))
BANKS = 2
GE = BANKS * EXPERTS
CH = 4
CW = CH * P
CHUNKS = TILES // CH
SPILL = float(2 * GE * CAP)


def route_phase(nc, g, w_router, b_router, w1, b1, w2, b2, upto, slots_x):
    with ExitStack() as ctx:
        sb = lambda name, shape, dt=F32: ctx.enter_context(nc.sbuf_tensor("r_" + name, shape, dt))
        ps = lambda name, shape, dt=F32: ctx.enter_context(nc.psum_tensor("r_" + name, shape, dt))
        sem = lambda name: ctx.enter_context(nc.semaphore("r_" + name))
        wr = sb("wr", [P, GE])
        rows = sb("rows", [1, GE + DM + P])
        up_w = sb("up_w", [P, FF])
        up_b = sb("up_b", [P, FT])
        down_w = sb("down_w", [P, FT, DM])
        tri_f = sb("tri_f", [P, P])
        tri = sb("tri", [P, P], BF16)
        ones = sb("ones", [P, P], BF16)
        order = sb("order", [P, CH, BANKS, EXPERTS])
        shift = sb("shift", [P, CH, BANKS])
        xn = sb("xn", [P, 2, CH, DM])
        xt = sb("xt", [P, 2, CW])
        hid = sb("hid", [P, FT, CW])
        hot = sb("hot", [P, 2, CH, GE], BF16)
        seen = sb("seen", [P, GE])
        seen_b = sb("seen_b", [P, 2, GE], BF16)
        added = sb("added", [P, GE])
        shifted = sb("shifted", [P, TILES, GE])
        keep_ = sb("keep", [P, TILES, BANKS])
        top = sb("top", [P, CH * BANKS])
        rank = sb("rank", [P, CH * BANKS])
        flag = sb("flag", [P, CH * GE])
        place_f = sb("place_f", [P, CH * BANKS])
        drop = sb("drop", [P, CH * BANKS])
        slot_f = sb("slot_f", [P, CH * BANKS])
        slots = sb("slots", [P, 2, CH * BANKS], U32)
        turned = ps("turned", [P, CW])
        logit = ps("logit", [P, CW])
        counts = ps("counts", [P, CW])
        ups = [ps(f"up{f}", [P, CW]) for f in range(FT)]
        down = ps("down", [P, CW])

        s_load = sem("weights_loaded")
        s_const = sem("constants_set")
        s_xn = sem("norm_applied")
        s_turn = sem("rows_turned")
        s_xt = sem("rows_t_ready")
        s_logit = sem("logits_ready")
        s_r = sem("routing_steps")
        s_s = sem("slot_steps")
        s_tri = sem("triangle_ready")
        s_exp = sem("exp_done")
        s_hot = sem("choice_ready")
        s_count = sem("counts_ready")
        s_slots = sem("slots_ready")
        s_scat = [sem(f"rows_scattered{i}") for i in range(2)]
        s_up = sem("up_done")
        s_gelu = sem("gelu_done")
        s_down = sem("down_done")
        s_h = sem("h_updated")
        s_pool = sem("pool_step")
        block = ctx.enter_context(nc.Block())
        PAIRS = CHUNKS // 2
        R2 = 10

        @block.sync
        def _(sp):
            for dst, src in ((wr[:], w_router), (rows[0:1, 0:GE], b_router), (rows[0:1, GE:GE + DM], b2),
                             (up_w[:], w1), (up_b[:], b1), (down_w[:], w2), (tri_f[:], upto)):
                sp.dma_start(dst, src).then_inc(s_load, 16)

        @block.gpsimd
        def _(pool):
            st = Steps(s_const)
            st.link(pool, nc.gpsimd.memset(ones[:], 1.0))
            st.link(pool, nc.gpsimd.memset(rows[0:1, GE + DM:], 1.0))
            st.link(pool, nc.gpsimd.memset(seen[:], 0.0))
            st.link(pool, nc.gpsimd.memset(seen_b[:], 0.0))
            for e in range(EXPERTS):
                st.link(pool, nc.gpsimd.memset(order[:, :, :, e:e + 1], float(EXPERTS - e)))
            for n in range(BANKS):
                st.link(pool, nc.gpsimd.memset(shift[:, :, n:n + 1], float(n * EXPERTS * CAP - 1)))

            def scatter(i, k):
                pool.wait_ge(s_slots, i * 2 + k + 1)
                pool.sem_inc(s_pool, 1)
                for j in range(CH):
                    for n in range(BANKS):
                        c = j * BANKS + n
                        nc.gpsimd.indirect_dma_start(
                            slots_x, bass.IndirectOffsetOnAxis(ap=slots[:, k, c:c + 1], axis=0), xn[:, k, j, :], None,
                            bounds_check=GE * CAP - 1, oob_is_err=False).then_inc(s_scat[k], 16)

            with pool.Fori(0, PAIRS) as i:
                scatter(i, 0)
                scatter(i, 1)
            for k in range(2):
                pool.wait_ge(s_scat[k], PAIRS * CH * BANKS * 16)

        @block.scalar
        def _(act):
            def copy_t(c, k, reused):
                act.wait_ge(s_turn, c + 1)
                if reused:
                    act.wait_ge(s_logit, c - 1)
                    act.wait_ge(s_up, (c - 1) * FT)
                nc.scalar.activation(xt[:, k, :], turned[:], ACT.Copy).then_inc(s_xt, 1)

            def gelu(c, reused):
                for f in range(FT):
                    act.wait_ge(s_up, c * FT + f + 1)
                    if reused and f == 0:
                        act.wait_ge(s_down, c)
                    nc.scalar.activation(hid[:, f, :], ups[f][:], ACT.Gelu, bias=up_b[:, f:f + 1]).then_inc(s_gelu, 1)

            act.wait_ge(s_load, 7 * 16)
            copy_t(0, 0, False)
            gelu(0, False)
            copy_t(1, 1, False)
            gelu(1, True)
            with act.Fori(1, PAIRS) as i:
                for k in range(2):
                    copy_t(i * 2 + k, k, True)
                    gelu(i * 2 + k, True)
            act.wait_ge(s_hot, CHUNKS)
            nc.scalar.activation(shifted[:], shifted[:], ACT.Exp).then_inc(s_exp, 1)

        @block.vector
        def _(dve):
            def norm(c, k, reused):
                if reused:
                    dve.wait_ge(s_scat[k], (c - k) * (CH * BANKS * 8))
                    dve.wait_ge(s_turn, c - 1)
                for j in range(CH):
                    tile = c * CH + j
                    ins = nc.vector.tensor_scalar(xn[:, k, j, :],
                                                  g.h[:, bass.ds(tile, 1), :].rearrange("p o d -> p (o d)"),
                                                  g.mean[:, bass.ds(tile, 1)], g.rstd[:, bass.ds(tile, 1)],
                                                  ALU.subtract, ALU.mult)
                ins.then_inc(s_xn, 1)

            GROUP = [P, CH * BANKS, EXPERTS]
            groups = lambda ap: ap.rearrange("p (u e) -> p u e", e=EXPERTS)
            R1 = 4

            def choose(c, k, reused):
                st = Steps(s_r, c * R1)
                lg = logit[:, 0:CH * GE].rearrange("p (u e) -> p u e", e=EXPERTS)
                dve.wait_ge(s_logit, c + 1)
                st.link(dve, nc.vector.tensor_reduce(top[:], lg, AX_X, ALU.max))
                d = shifted[:, bass.ds(c * CH, CH), :].rearrange("p c (b e) -> p (c b) e", e=EXPERTS)
                st.link(dve, nc.vector.tensor_tensor(d, lg, top[:].to_broadcast(GROUP), ALU.subtract))
                st.link(dve, nc.vector.scalar_tensor_tensor(out=groups(flag[:]), in0=d, scalar=0.0,
                                                            in1=order[:].rearrange("p c b e -> p (c b) e"),
                                                            op0=ALU.is_ge, op1=ALU.mult))
                st.link(dve, nc.vector.tensor_reduce(rank[:], groups(flag[:]), AX_X, ALU.max))
                if reused:
                    dve.wait_ge(s_count, c - 1)
                nc.vector.tensor_tensor(hot[:, k].rearrange("p c (b e) -> p (c b) e", e=EXPERTS),
                                        order[:].rearrange("p c b e -> p (c b) e"), rank[:].to_broadcast(GROUP),
                                        ALU.is_equal).then_inc(s_hot, 1)

            def slot(c, k, reused):
                st = Steps(s_s, c * R2)
                cnt = counts[:, 0:CH * GE]
                dve.wait_ge(s_count, c + 1)
                dve.wait_ge(s_hot, c + 1)
                h = hot[:, k].rearrange("p c e -> p (c e)")
                st.link(dve, nc.vector.tensor_tensor(flag[:], cnt, h, ALU.mult))
                st.link(dve, nc.vector.tensor_reduce(place_f[:], groups(flag[:]), AX_X, ALU.add))
                st.link(dve, nc.vector.tensor_reduce(added[:], hot[:, k].rearrange("p c e -> p e c"), AX_X, ALU.add))
                st.link(dve, nc.vector.tensor_tensor(seen[:], seen[:], added[:], ALU.add))
                st.link(dve, nc.vector.tensor_copy(seen_b[:, 1 - k, :], seen[:]))
                keep = keep_[:, bass.ds(c * CH, CH), :].rearrange("p c b -> p (c b)")
                st.link(dve, nc.vector.tensor_scalar(keep, place_f[:], float(CAP), None, ALU.is_le))
                st.link(dve, nc.vector.tensor_scalar(drop[:], place_f[:], float(CAP), SPILL, ALU.is_gt, ALU.mult))
                st.link(dve, nc.vector.tensor_scalar(slot_f[:], rank[:], -float(CAP), float(EXPERTS * CAP), ALU.mult,
                                                     ALU.add))
                st.link(dve, nc.vector.scalar_tensor_tensor(out=place_f[:], in0=place_f[:], scalar=float(CAP),
                                                            in1=slot_f[:], op0=ALU.min, op1=ALU.add))
                st.link(dve, nc.vector.tensor_tensor(place_f[:], place_f[:], shift[:].rearrange("p c b -> p (c b)"),
                                                     ALU.add))
                nc.vector.tensor_copy(g.slot[:, bass.ds(c * CH, CH), :].rearrange("p c b -> p (c b)"), place_f[:])
                if reused:
                    dve.wait_ge(s_scat[k], (c - k) * (CH * BANKS * 8))
                nc.vector.tensor_tensor(slots[:, k, :], place_f[:], drop[:], ALU.add).then_inc(s_slots, 1)

            def add(c):
                dve.wait_ge(s_down, c + 1)
                tiles = g.h[:, bass.ds(c * CH, CH), :].rearrange("p i d -> p (i d)")
                nc.vector.tensor_tensor(tiles, tiles, down[:], ALU.add).then_inc(s_h, 1)

            dve.wait_ge(s_load, 7 * 16)
            dve.wait_ge(s_const, 4 + EXPERTS + BANKS)
            st0 = Steps(s_tri)
            st0.up(nc.vector.tensor_copy(tri[:], tri_f[:]))
            norm(0, 0, False)

            def step(c, k, reused, more, late):
                choose(c, k, reused)
                if more:
                    norm(c + 1, 1 - k, late)
                slot(c, k, reused)
                add(c)

            step(0, 0, False, True, False)
            step(1, 1, False, True, True)
            with dve.Fori(1, PAIRS - 1) as i:
                step(i * 2, 0, True, True, True)
                step(i * 2 + 1, 1, True, True, True)
            step(CHUNKS - 2, 0, True, True, True)
            step(CHUNKS - 1, 1, True, False, True)
            st = Steps(s_s, CHUNKS * R2)
            dve.wait_ge(s_exp, 1)
            gate = g.gate[:].rearrange("p t b -> p (t b)")
            st.link(dve, nc.vector.tensor_reduce(gate, shifted[:].rearrange("p t (b e) -> p (t b) e", e=EXPERTS),
                                                 AX_X, ALU.add))
            st.link(dve, nc.vector.reciprocal(gate, gate))
            nc.vector.tensor_tensor(gate, gate, keep_[:].rearrange("p t b -> p (t b)"), ALU.mult)

        @block.tensor
        def _(pe):
            def turn(c, k, reused):
                pe.wait_ge(s_xn, c + 1)
                if reused:
                    pe.wait_ge(s_xt, c)
                for j in range(CH):
                    ins = nc.tensor.transpose(turned[:, j * P:(j + 1) * P], xn[:, k, j, :], g.ident[:])
                ins.then_inc(s_turn, 1)

            def router(c, k, reused):
                pe.wait_ge(s_xt, c + 1)
                if reused:
                    pe.wait_ge(s_hot, c)
                for j in range(CH):
                    o = logit[:, j * GE:(j + 1) * GE]
                    nc.tensor.matmul(o, xt[:, k, j * P:(j + 1) * P], wr[:], start=True, stop=False)
                    ins = nc.tensor.matmul(o, rows[0:1, GE + DM:], rows[0:1, 0:GE], start=False, stop=True)
                ins.then_inc(s_logit, 1)

            def up(c, k, reused):
                for f in range(FT):
                    if reused:
                        pe.wait_ge(s_gelu, (c - 1) * FT + f + 1)
                    nc.tensor.matmul(ups[f][:], up_w[:, f * P:(f + 1) * P], xt[:, k, :], start=True,
                                     stop=True).then_inc(s_up, 1)

            def count(c, k, reused):
                pe.wait_ge(s_hot, c + 1)
                if reused:
                    pe.wait_ge(s_s, c * R2)
                for j in range(CH):
                    o = counts[:, j * GE:(j + 1) * GE]
                    nc.tensor.matmul(o, ones[:], seen_b[:, k, :], start=True, stop=False)
                    for before in range(j):
                        nc.tensor.matmul(o, ones[:], hot[:, k, before, :], start=False, stop=False)
                    ins = nc.tensor.matmul(o, tri[:], hot[:, k, j, :], start=False, stop=True)
                ins.then_inc(s_count, 1)

            def down_(c, reused):
                if reused:
                    pe.wait_ge(s_h, c)
                pe.wait_ge(s_gelu, c * FT + FT)
                for j in range(CH):
                    o = down[:, j * P:(j + 1) * P]
                    for f in range(FT):
                        nc.tensor.matmul(o, hid[:, f, j * P:(j + 1) * P], down_w[:, f, :], start=(f == 0), stop=False)
                    ins = nc.tensor.matmul(o, rows[0:1, GE + DM:], rows[0:1, GE:GE + DM], start=False, stop=True)
                ins.then_inc(s_down, 1)

            pe.wait_ge(s_load, 7 * 16)
            pe.wait_ge(s_const, 4 + EXPERTS + BANKS)
            pe.wait_ge(s_tri, 1)
            turn(0, 0, False)
            router(0, 0, False)

            def step(c, k, reused, more):
                up(c, k, reused)
                if more:
                    turn(c + 1, 1 - k, True)
                count(c, k, reused)
                if more:
                    router(c + 1, 1 - k, True)
                down_(c, reused)

            step(0, 0, False, True)
            step(1, 1, True, True)
            with pe.Fori(1, PAIRS - 1) as i:
                step(i * 2, 0, True, True)
                step(i * 2 + 1, 1, True, True)
            step(CHUNKS - 2, 0, True, True)
            step(CHUNKS - 1, 1, True, False)


def experts_phase(nc, g, slots_x, slots_y, w1, b1, w2, b2):
    with ExitStack() as ctx:
        sb = lambda name, shape, dt=F32: ctx.enter_context(nc.sbuf_tensor("x_" + name, shape, dt))
        ps = lambda name, shape, dt=F32: ctx.enter_context(nc.psum_tensor("x_" + name, shape, dt))
        sem = lambda name: ctx.enter_context(nc.semaphore("x_" + name))
        ET = CAP // P
        PARTS = [(t, min(CH, ET - t)) for t in range(0, ET, CH)]
        NP = len(PARTS)
        rows = sb("rows", [P, 2, ET, DM])
        outs = sb("outs", [P, 2, ET, DM])
        w_up = sb("w_up", [P, 2, FF])
        w_down = sb("w_down", [P, 2, FT, DM])
        b_down = sb("b_down", [1, 2, DM])
        b_up = sb("b_up", [P, GE, FT])
        b_cur = sb("b_cur", [P, 2, FT])
        ones = sb("ones", [1, P])
        xt = sb("xt", [P, 2, CW])
        hid = sb("hid", [P, FT, CW])
        turned = ps("turned", [P, CW])
        ups = [ps(f"up{f}", [P, CW]) for f in range(FT)]
        down = [ps(f"down{n}", [P, CW]) for n in range(2)]
        s_const = sem("constants_loaded")
        s_ones = sem("ones_set")
        s_in = [sem(f"expert_loaded{k}") for k in range(2)]
        s_turn = sem("rows_turned")
        s_xt = sem("rows_t_ready")
        s_up = sem("up_done")
        s_gelu = sem("gelu_done")
        s_down = sem("down_done")
        s_o = sem("outputs_ready")
        s_out = [sem(f"outputs_stored{k}") for k in range(2)]
        block = ctx.enter_context(nc.Block())
        PAIRS = GE // 2
        LOADS = 5 * 16

        def slot_rows(t, e):
            return t[bass.ds(e * CAP, CAP), :].rearrange("(j p) d -> p j d", p=P)

        @block.sync
        def _(sp):
            def load(e, k):
                sp.dma_start(rows[:, k], slot_rows(slots_x, e)).then_inc(s_in[k], 16)
                sp.dma_start(w_up[:, k, :], w1[bass.ds(e, 1), :, :].rearrange("o d f -> d (o f)")).then_inc(s_in[k], 16)
                sp.dma_start(w_down[:, k], w2[bass.ds(e, 1), :, :].rearrange("o (t f) d -> f (o t) d", f=P)).then_inc(s_in[k], 16)
                sp.dma_start(b_down[0:1, k, :], b2[bass.ds(e, 1), :]).then_inc(s_in[k], 16)
                sp.dma_start(b_cur[:, k, :], b1[bass.ds(e, 1), :, :].rearrange("o p t -> p (o t)")).then_inc(s_in[k], 16)

            def store(e, k):
                sp.wait_ge(s_o, (e + 1) * NP)
                sp.dma_start(slot_rows(slots_y, e), outs[:, k]).then_inc(s_out[k], 16)

            load(0, 0)
            load(1, 1)
            with sp.Fori(0, PAIRS - 1) as i:
                for k in range(2):
                    store(i * 2 + k, k)
                    sp.wait_ge(s_down, (i * 2 + (k + 1)) * NP)
                    load(i * 2 + (k + 2), k)
            for k in range(2):
                store(GE - 2 + k, k)
            for k in range(2):
                sp.wait_ge(s_out[k], PAIRS * 16)

        @block.gpsimd
        def _(pool):
            nc.gpsimd.memset(ones[:], 1.0).then_inc(s_ones, 1)

        def passes(body, eng):
            for e in range(2):
                for c in range(NP):
                    body(e * NP + c, e, c, e, True)
            with eng.Fori(1, PAIRS) as i:
                for k in range(2):
                    for c in range(NP):
                        body(i * (2 * NP) + (k * NP + c), k, c, i * 2 + k, False)

        @block.scalar
        def _(act):
            def gelu(n, k, c, e, first):
                width = PARTS[c][1] * P
                if c == 0:
                    act.wait_ge(s_in[k], ((e - k) * 8 if not first else 0) * 5 + LOADS)
                for f in range(FT):
                    act.wait_ge(s_up, n * FT + f + 1)
                    if f == 0 and not (first and k == 0 and c == 0):
                        act.wait_ge(s_down, n)
                    nc.scalar.activation(hid[:, f, 0:width], ups[f][:, 0:width], ACT.Gelu,
                                         bias=b_cur[:, k, f:f + 1]).then_inc(s_gelu, 1)

            passes(gelu, act)

        @block.vector
        def _(dve):
            def copies(n, k, c, e, first):
                t, m = PARTS[c]
                if not (first and k == 0 and c == 0):
                    out(n - 1, (k if c else 1 - k), (c - 1) % NP, (e if c else e - 1), first)
                dve.wait_ge(s_turn, n + 1)
                if not (first and k == 0 and c < 2):
                    dve.wait_ge(s_up, (n - 1) * FT)
                nc.vector.tensor_copy(xt[:, (k * NP + c) % 2, 0:m * P], turned[:, 0:m * P]).then_inc(s_xt, 1)

            def out(n, k, c, e, first):
                t, m = PARTS[c]
                dve.wait_ge(s_down, n + 1)
                if c == 0 and not first:
                    dve.wait_ge(s_out[k], (e - k) * 8)
                nc.vector.tensor_copy(outs[:, k, t:t + m, :].rearrange("p j d -> p (j d)"),
                                      down[(k * NP + c) % 2][:, 0:m * P]).then_inc(s_o, 1)

            passes(copies, dve)
            out(GE * NP - 1, 1, NP - 1, GE - 1, False)

        @block.tensor
        def _(pe):
            pe.wait_ge(s_ones, 1)

            def turn(n, k, c, e, first):
                t, m = PARTS[c]
                if c == 0:
                    pe.wait_ge(s_in[k], ((e - k) * 8 if not first else 0) * 5 + LOADS)
                if not (first and k == 0 and c == 0):
                    pe.wait_ge(s_xt, n)
                for j in range(m):
                    ins = nc.tensor.transpose(turned[:, j * P:(j + 1) * P], rows[:, k, t + j, :], g.ident[:])
                ins.then_inc(s_turn, 1)

            def work(n, k, c, e, first):
                t, m = PARTS[c]
                begins = first and k == 0 and c == 0
                pe.wait_ge(s_xt, n + 1)
                for f in range(FT):
                    if not begins:
                        pe.wait_ge(s_gelu, (n - 1) * FT + f + 1)
                    nc.tensor.matmul(ups[f][:, 0:m * P], w_up[:, k, f * P:(f + 1) * P], xt[:, (k * NP + c) % 2, 0:m * P],
                                     start=True, stop=True).then_inc(s_up, 1)

            def down_(n, k, c, e, first):
                t, m = PARTS[c]
                if not (first and k == 0 and c < 2):
                    pe.wait_ge(s_o, n - 1)
                pe.wait_ge(s_gelu, n * FT + FT)
                for j in range(m):
                    o = down[(k * NP + c) % 2][:, j * P:(j + 1) * P]
                    for f in range(FT):
                        nc.tensor.matmul(o, hid[:, f, j * P:(j + 1) * P], w_down[:, k, f, :], start=(f == 0), stop=False)
                    ins = nc.tensor.matmul(o, ones[:], b_down[0:1, k, :], start=False, stop=True)
                ins.then_inc(s_down, 1)

            def step(n, k, c, e, first):
                work(n, k, c, e, first)
                nk, nn = (k, c + 1) if c + 1 < NP else (1 - k, 0)
                ne = e if nk == k else e + 1
                turn(n + 1, nk, nn, ne, first and not (k == 1 and c == NP - 1))
                down_(n, k, c, e, first)

            turn(0, 0, 0, 0, True)
            for k in range(2):
                for c in range(NP):
                    step(k * NP + c, k, c, k, True)
            with pe.Fori(1, PAIRS - 1) as i:
                for k in range(2):
                    for c in range(NP):
                        step(i * (2 * NP) + (k * NP + c), k, c, i * 2 + k, False)
            for k in range(2):
                for c in range(NP):
                    n = (PAIRS - 1) * 2 * NP + k * NP + c
                    if (k, c) == (1, NP - 1):
                        work(n, k, c, GE - 1, False)
                        down_(n, k, c, GE - 1, False)
                    else:
                        step(n, k, c, GE - 2 + k, False)


def combine_phase(nc, g, slots_y, h_out):
    with ExitStack() as ctx:
        sb = lambda name, shape, dt=F32: ctx.enter_context(nc.sbuf_tensor("c_" + name, shape, dt))
        sem = lambda name: ctx.enter_context(nc.semaphore("c_" + name))
        SLOTS = 4
        cols = sb("cols", [P, 2, TPB * BANKS], U32)
        rows = sb("rows", [P, SLOTS, BANKS, DM])
        s_cols = sem("slot_columns_ready")
        s_rows = [sem(f"rows_gathered{i}") for i in range(SLOTS)]
        s_step = sem("vector_steps")
        s_pool = sem("pool_step")
        s_store = sem("h_stored")
        block = ctx.enter_context(nc.Block())
        PAIRS = BATCH // 2
        T2 = 2 * TPB
        PER = T2 // SLOTS * BANKS * 16

        @block.sync
        def _(sp):
            with sp.Fori(0, BATCH) as b:
                sp.wait_ge(s_step, (b + 1) * (TPB * BANKS))
                sp.dma_start(h_out[bass.ds(b * SEQ, SEQ), :].rearrange("(j p) d -> p j d", p=P),
                             g.h[:, bass.ds(b * TPB, TPB), :]).then_inc(s_store, 16)
            sp.wait_ge(s_store, BATCH * 16)

        @block.gpsimd
        def _(pool):
            def gather(i, j, reused):
                slot = j % SLOTS
                if j % TPB == 0:
                    pool.wait_ge(s_cols, i * 2 + (j // TPB + 1))
                if reused:
                    pool.wait_ge(s_step, (i * T2 + (j - SLOTS + 1)) * BANKS)
                pool.sem_inc(s_pool, 1)
                for n in range(BANKS):
                    c = (j % TPB) * BANKS + n
                    nc.gpsimd.indirect_dma_start(
                        rows[:, slot, n, :], None, slots_y,
                        bass.IndirectOffsetOnAxis(ap=cols[:, j // TPB, c:c + 1], axis=0)).then_inc(s_rows[slot], 16)

            for j in range(T2):
                gather(0, j, j >= SLOTS)
            with pool.Fori(1, PAIRS) as i:
                for j in range(T2):
                    gather(i, j, True)

        @block.vector
        def _(dve):
            def fill(pair, half):
                tile = pair * T2 + half * TPB
                nc.vector.tensor_copy(cols[:, half, :].rearrange("p (t b) -> p t b", b=BANKS),
                                      g.slot[:, bass.ds(tile, TPB), :]).then_inc(s_cols, 1)

            def tiles(i, more):
                for j in range(T2):
                    slot = j % SLOTS
                    tile = i * T2 + j
                    dve.wait_ge(s_rows[slot], i * PER + (j // SLOTS + 1) * BANKS * 16)
                    h = g.h[:, bass.ds(tile, 1), :].rearrange("p o d -> p (o d)")
                    for n in range(BANKS):
                        gate = g.gate[:, bass.ds(tile, 1), n]
                        nc.vector.scalar_tensor_tensor(out=h, in0=rows[:, slot, n, :], scalar=gate, in1=h,
                                                       op0=ALU.mult, op1=ALU.add).then_inc(s_step, 1)
                        dve.wait_ge(s_step, tile * BANKS + (n + 1))
                    nc.vector.bn_stats(g.stat[:, bass.ds(tile, 1), :], g.h[:, bass.ds(tile, 1), :])
                    if more and j % TPB == TPB - 1:
                        fill(i + 1, j // TPB)

            fill(0, 0)
            fill(0, 1)
            with dve.Fori(0, PAIRS - 1) as i:
                tiles(i, True)
            tiles(PAIRS - 1, False)


SCALES = 3
DI, ST, DTR, TAPS = 256, 16, 32, 4
DT2 = DI // P
UW = SEQ
HALF = 512
SERIES = 1e-4


def mamba_phase(nc, g, h_in, h_out, w):
    with ExitStack() as ctx:
        sb = lambda name, shape, dt=F32: ctx.enter_context(nc.sbuf_tensor("m_" + name, shape, dt))
        ps = lambda name, shape, dt=F32: ctx.enter_context(nc.psum_tensor("m_" + name, shape, dt))
        sem = lambda name: ctx.enter_context(nc.semaphore("m_" + name))
        LEN = [SEQ >> s for s in range(SCALES)]
        NS = [UW // t for t in LEN]
        UNITS = [ST // n for n in NS]
        FIRST_UNIT = [sum(UNITS[:s]) for s in range(SCALES)]
        NU = sum(UNITS)
        conv_w = sb("conv_w", [P, SCALES, TAPS, DI])
        z_w = sb("z_w", [P, SCALES, DI])
        xp_w = sb("xp_w", [P, SCALES, DT2, P])
        dt_w = sb("dt_w", [DTR, SCALES, DI])
        out_w = sb("out_w", [P, SCALES, DT2, DM])
        fus_w = sb("fus_w", [P, SCALES, DM])
        cols = sb("cols", [P, 3, SCALES, DT2])
        decay = sb("decay", [P, SCALES, DT2, ST])
        rowb = sb("rowb", [1, 2, DM])
        ln_g = sb("ln_g", [P, DM])
        ln_b = sb("ln_b", [P, DM])
        pick_f = sb("pick_f", [P, 2 * ST])
        pick = sb("pick", [P, 2 * ST, P], BF16)
        power = sb("power", [P, TPB])
        hl = sb("hl", [P, 2, TPB, DM])
        xn = sb("xn", [P, 2, TPB, DM])
        xts = [sb(f"xts{s}", [P, TAPS - 1 + LEN[s]]) for s in range(SCALES)]
        xc = [sb(f"xc{s}", [P, DT2, LEN[s]]) for s in range(SCALES)]
        sz = [sb(f"sz{s}", [P, DT2, LEN[s]]) for s in range(SCALES)]
        dt_ = [sb(f"dt{s}", [P, DT2, LEN[s]]) for s in range(SCALES)]
        dtx = [sb(f"dtx{s}", [P, DT2, LEN[s]]) for s in range(SCALES)]
        bc_f = sb("bc_f", [P, SEQ])
        bc = [sb(f"bc{s}", [P, LEN[s]], BF16) for s in range(SCALES)]
        t_exp = sb("t_exp", [P, UW])
        t_relu = sb("t_relu", [P, UW])
        t_ln = sb("t_ln", [P, UW])
        t_one = sb("t_one", [P, UW])
        da = sb("da", [P, 2, DT2, UW])
        hb = sb("hb", [P, 2, DT2, UW])
        o = [sb("o0", [P, SEQ])] + [sb(f"o{s}", [P, LEN[s] + 2]) for s in (1, 2)]
        oi = [o[0]] + [sb(f"oi{s}", [P, SEQ]) for s in (1, 2)]
        hh = sb("hh", [P, TPB, DM])
        st6 = sb("st6", [P, TPB, 6])
        st_d = sb("st_d", [P, TPB])
        st_m = sb("st_m", [P, TPB])
        st_v = sb("st_v", [P, TPB])
        work = ps("work", [P, UW])
        cps = ps("c", [P, UW])
        yps = ps("y", [P, DT2, UW])

        s_load = sem("weights_loaded")
        s_fold = sem("conv_folded")
        s_const = sem("constants_set")
        s_prep = sem("setup_steps")
        s_hl = [sem(f"h_loaded{k}") for k in range(2)]
        s_hs = [sem(f"h_stored{k}") for k in range(2)]
        s_xn = sem("norm_applied")
        s_wr = sem("work_ready")
        s_wf = sem("work_free")
        s_c = sem("c_ready")
        s_g = sem("states_times_c")
        s_da = sem("decay_ready")
        s_scan = sem("scan_done")
        s_y = sem("states_summed")
        s_post = sem("gated")
        s_post1 = sem("skip_added")
        s_bc = sem("bc_copied")
        s_split = sem("bc_split")
        s_splits = sem("bc_split_steps")
        s_sp = sem("softplus_parts")
        s_act = sem("softplus_steps")
        s_dtx = sem("dtx_ready")
        s_dts = sem("dtx_steps")
        s_o = sem("out_copied")
        s_oi = sem("interpolated")
        s_ois = sem("interp_steps")
        s_hh = sem("fused")
        s_hst = sem("fused_stats")
        s_lns = sem("ln_steps")
        s_rs = sem("ln_rstd_ready")
        s_nm = sem("ln_applied")
        s_h3 = sem("h_ready")
        s_h3s = sem("h_steps")
        s_pool = sem("pool_step")
        block = ctx.enter_context(nc.Block())

        PARTS = [[[0], [1]]] + [[[0, 1]]] * (SCALES - 1)
        prep = lambda s: ([("xi", s, p) for p in range(len(PARTS[s]))] + [("xp", s)]
                          + [("dt", s, p) for p in range(len(PARTS[s]))] + [("z", s, p) for p in range(len(PARTS[s]))])
        FIRST = [("turn",)] + prep(0)

        def plan(prev, nxt):
            at = {}
            if prev:
                at[1], at[4] = [("out", 2)], [("fuse",)]
            for u, use in zip((3, 5, 7, 9), prep(1)):
                at.setdefault(u, []).append(use)
            for u, use in zip((10, 11, 13, 14), prep(2)):
                at[u] = [use]
            at[17] = [("out", 0)]
            if nxt:
                at[16] = [("turn",)]
                for u, use in zip((18, 18, 19, 20, 21, 23, 24), prep(0)):
                    at.setdefault(u, []).append(use)
            at[26] = [("out", 1)]
            return at

        FULL = plan(True, True)
        N_FULL = NU + sum(map(len, FULL.values()))
        N_FIRST = NU + sum(map(len, plan(False, True).values()))
        N_LAST = NU + sum(map(len, plan(True, False).values()))
        TAIL = [("out", 2), ("fuse",)]
        LAST = BATCH - 1
        use_base = lambda b: len(FIRST) + N_FIRST + N_FULL * (b - 1)
        END = use_base(LAST) + N_LAST

        def scale_of(u):
            s = max(s for s in range(SCALES) if u >= FIRST_UNIT[s])
            return s, u - FIRST_UNIT[s]

        def batches(main, eng):
            main(0, 0, len(FIRST), plan(False, True), False, True)
            with eng.Fori(0, (BATCH - 2) // 2) as i:
                main(i * 2 + 1, 1, use_base(i * 2 + 1), FULL, True, True)
                main(i * 2 + 2, 0, use_base(i * 2 + 2), FULL, True, True)
            main(LAST, LAST % 2, use_base(LAST), plan(True, False), True, False)

        def row_of(use, b, u):
            if use in (("out", 2), ("fuse",)):
                return b - 1
            if use[0] == "turn" or (use[0] != "out" and use[1] == 0):
                return b + 1
            return b

        flat = lambda buf, tiles: buf[:, tiles[0]:tiles[-1] + 1, :].rearrange("p d t -> p (d t)")
        split_no = lambda b, s: b * 3 + (s + 1)
        dtx_no = lambda b, s, p: b * 4 + (p + 1 if s == 0 else s + 2)
        units_done = lambda b, s: b * NU + (FIRST_UNIT[s] + UNITS[s])

        @block.sync
        def _(sp):
            loads = ((conv_w[:], w["conv_w"].partition_broadcast(P)), (hb[:, 0, 0, 0:SCALES * DI], w["xi_w"]),
                     (z_w[:], w["z_w"]), (xp_w[:], w["xp_w"]), (dt_w[:], w["dt_w"]), (out_w[:], w["out_w"]),
                     (fus_w[:], w["fus_w"]), (cols[:], w["cols"]), (decay[:], w["a_log"]), (rowb[0:1, 0, :], w["fus_b"]),
                     (ln_g[:], w["ln_g"].partition_broadcast(P)), (ln_b[:], w["ln_b"].partition_broadcast(P)),
                     (pick_f[:], w["pick"]))
            assert len(loads) == 13
            for dst, src in loads:
                sp.dma_start(dst, src).then_inc(s_load, 16)

            def rows(t, b):
                return t[bass.ds(b * SEQ, SEQ), :].rearrange("(j p) d -> p j d", p=P)

            def load(b, k):
                sp.dma_start(hl[:, k], rows(h_in, b)).then_inc(s_hl[k], 16)

            def store(b, k):
                sp.wait_ge(s_h3, b + 1)
                sp.dma_start(rows(h_out, b), hl[:, k]).then_inc(s_hs[k], 16)
                sp.wait_ge(s_hs[k], (b - k) * 8 + 16)

            load(0, 0)
            load(1, 1)
            with sp.Fori(0, BATCH // 2 - 1) as i:
                for k in range(2):
                    store(i * 2 + k, k)
                    sp.wait_ge(s_hst, (i * 2 + k) * 2 + 2)
                    load(i * 2 + (k + 2), k)
            for k in range(2):
                store(BATCH - 2 + k, k)

        @block.gpsimd
        def _(pool):
            st = Steps(s_const)
            for x in xts:
                st.link(pool, nc.gpsimd.memset(x[:, 0:TAPS - 1], 0.0))
            st.link(pool, nc.gpsimd.memset(rowb[0:1, 1, :], 1.0))
            st.link(pool, nc.gpsimd.memset(power[:], -0.5))

            def go():
                pool.sem_inc(s_pool, 1)

            def linked(st, ins):
                st.up(ins)
                st.wait(pool)
                go()

            def split(b, s, first):
                t = LEN[s]
                st = Steps(s_splits, b * 9 + 3 * s)
                pool.wait_ge(s_bc, split_no(b, s))
                if not first:
                    pool.wait_ge(s_c, units_done(b - 1, s))
                go()
                linked(st, nc.gpsimd.tensor_copy(bc[s][:], bc_f[:, 0:t]))
                linked(st, nc.gpsimd.tensor_tensor(bc_f[64:P, 0:t], bc_f[64:P, 0:t], bc[s][64:P, :], ALU.subtract))
                linked(st, nc.gpsimd.tensor_copy(bc[s][64:P, :], bc_f[64:P, 0:t]))
                nc.gpsimd.tensor_tensor(bc[s][96:P, :], bc_f[96:P, 0:t], bc[s][96:P, :], ALU.subtract).then_inc(s_split, 1)
                pool.wait_ge(s_split, split_no(b, s))
                go()

            def softplus(b, s, p, first):
                tiles = PARTS[s][p]
                n = len(tiles) * LEN[s]
                st = Steps(s_dts, dtx_no(b, s, p) * 10 - 10)
                pool.wait_ge(s_sp, dtx_no(b, s, p))
                if not first:
                    pool.wait_ge(s_da, units_done(b - 1, s))
                go()
                linked(st, nc.gpsimd.tensor_scalar(t_one[:, 0:n], t_exp[:, 0:n], 1.0, 1.0, ALU.add, ALU.subtract))
                linked(st, nc.gpsimd.tensor_tensor(t_one[:, 0:n], t_one[:, 0:n], t_exp[:, 0:n], ALU.subtract))
                linked(st, nc.gpsimd.tensor_tensor(t_ln[:, 0:n], t_ln[:, 0:n], t_one[:, 0:n], ALU.subtract))
                linked(st, nc.gpsimd.tensor_scalar(t_one[:, 0:n], t_exp[:, 0:n], -0.5, 1.0, ALU.mult, ALU.add))
                linked(st, nc.gpsimd.tensor_tensor(t_one[:, 0:n], t_one[:, 0:n], t_exp[:, 0:n], ALU.mult))
                linked(st, nc.gpsimd.tensor_tensor(t_ln[:, 0:n], t_ln[:, 0:n], t_one[:, 0:n], ALU.subtract))
                linked(st, nc.gpsimd.tensor_scalar(t_exp[:, 0:n], t_exp[:, 0:n], SERIES, None, ALU.is_ge))
                linked(st, nc.gpsimd.tensor_tensor(t_ln[:, 0:n], t_ln[:, 0:n], t_exp[:, 0:n], ALU.mult))
                linked(st, nc.gpsimd.tensor_tensor(t_one[:, 0:n], t_one[:, 0:n], t_relu[:, 0:n], ALU.add))
                linked(st, nc.gpsimd.tensor_tensor(flat(dt_[s], tiles), t_one[:, 0:n], t_ln[:, 0:n], ALU.add))
                nc.gpsimd.tensor_tensor(flat(dtx[s], tiles), flat(dt_[s], tiles), flat(xc[s], tiles),
                                        ALU.mult).then_inc(s_dtx, 1)

            def interpolate(b, s, first):
                t, stride = LEN[s], 1 << s
                st = Steps(s_ois, b * 16 + (0 if s == 1 else 5))
                pool.wait_ge(s_o, b * 3 + (s + 1))
                if not first:
                    pool.wait_ge(s_hh, b)
                go()
                dst = oi[s][:].rearrange("p (t r) -> p t r", r=stride)
                for r in range(stride):
                    x = (r + 0.5) / stride - 0.5
                    near = o[s][:, 0:t] if x < 0 else o[s][:, 2:t + 2]
                    if r:
                        st.wait(pool)
                        go()
                    linked(st, nc.gpsimd.tensor_scalar(t_one[:, 0:t], near, abs(x), None, ALU.mult))
                    linked(st, nc.gpsimd.tensor_scalar(dst[:, :, r], o[s][:, 1:t + 1], 1.0 - abs(x), None, ALU.mult))
                    ins = nc.gpsimd.tensor_tensor(dst[:, :, r], dst[:, :, r], t_one[:, 0:t], ALU.add)
                    if r < stride - 1:
                        st.up(ins)
                ins.then_inc(s_oi, 1)
                pool.wait_ge(s_oi, b * 2 + s)
                go()

            def rstd(b):
                st = Steps(s_lns, b * 8)
                pool.wait_ge(s_hst, b * 2 + 1)
                go()
                m0, m1, v0, v1 = (st6[:, :, c] for c in (1, 4, 2, 5))
                linked(st, nc.gpsimd.tensor_tensor(st_d[:], m0, m1, ALU.subtract))
                linked(st, nc.gpsimd.tensor_tensor(st_m[:], m0, m1, ALU.add))
                linked(st, nc.gpsimd.tensor_scalar(st_m[:], st_m[:], 0.5, None, ALU.mult))
                linked(st, nc.gpsimd.tensor_tensor(st_v[:], v0, v1, ALU.add))
                linked(st, nc.gpsimd.tensor_scalar(st_v[:], st_v[:], 1.0 / DM, LN_EPS, ALU.mult, ALU.add))
                linked(st, nc.gpsimd.tensor_tensor(st_d[:], st_d[:], st_d[:], ALU.mult))
                linked(st, nc.gpsimd.tensor_scalar(st_d[:], st_d[:], 0.25, None, ALU.mult))
                linked(st, nc.gpsimd.tensor_tensor(st_v[:], st_v[:], st_d[:], ALU.add))
                nc.gpsimd.tensor_tensor(st_v[:], st_v[:], power[:], ALU.pow).then_inc(s_rs, 1)

            def finish(b, k):
                st = Steps(s_h3s, b * 2)
                pool.wait_ge(s_nm, b + 1)
                go()
                over = lambda ap: ap[:].unsqueeze(1).to_broadcast([P, TPB, DM])
                linked(st, nc.gpsimd.tensor_tensor(hh[:], hh[:], over(ln_g), ALU.mult))
                linked(st, nc.gpsimd.tensor_tensor(hh[:], hh[:], over(ln_b), ALU.add))
                nc.gpsimd.tensor_tensor(hl[:, k], hl[:, k], hh[:], ALU.add).then_inc(s_h3, 1)

            def main(b, k, base, at, prev, nxt):
                for u in range(NU):
                    for use in at.get(u, []):
                        if use == ("out", 2):
                            interpolate(b - 1, 2, False if prev else True)
                        elif use == ("out", 1):
                            interpolate(b, 1, not prev)
                        elif use[0] == "fuse":
                            rstd(b - 1)
                        elif use[0] == "xp":
                            split(b + (use[1] == 0), use[1], use[1] > 0 and not prev)
                        elif use[0] == "dt":
                            softplus(b + (use[1] == 0), use[1], use[2], use[1] > 0 and not prev)
                    if u == 8 and prev:
                        finish(b - 1, 1 - k)

            split(0, 0, True)
            for p in range(2):
                softplus(0, 0, p, True)
            batches(main, pool)
            interpolate(LAST, 2, False)
            rstd(LAST)
            finish(LAST, LAST % 2)

        @block.scalar
        def _(act):
            def consume(n, use, b, first):
                kind = use[0]
                if kind not in ("turn", "xi", "z", "xp", "dt", "out"):
                    return
                act.wait_ge(s_wr, n + 1)
                if kind == "turn":
                    for s in range(SCALES):
                        ins = nc.scalar.activation(xts[s][:, TAPS - 1:], work[:, ::1 << s], ACT.Copy)
                    ins.then_inc(s_wf, 1)
                elif kind in ("xi", "z"):
                    _, s, p = use
                    tiles = PARTS[s][p]
                    if not first:
                        act.wait_ge(s_post, (b - 1) * 3 + (s + 1))
                    for m, d in enumerate(tiles):
                        src = work[:, m * LEN[s]:(m + 1) * LEN[s]]
                        if kind == "xi":
                            ins = nc.scalar.activation(xc[s][:, d, :], src, ACT.Silu, bias=cols[:, 0, s, d:d + 1])
                        else:
                            ins = nc.scalar.activation(sz[s][:, d, :], src, ACT.Silu)
                    ins.then_inc(s_wf, 1)
                elif kind == "xp":
                    s = use[1]
                    if not (first and s == 0):
                        act.wait_ge(s_split, split_no(b, s) - 1)
                    nc.scalar.activation(bc_f[:, 0:LEN[s]], work[:, 0:LEN[s]], ACT.Copy).then_inc(s_wf, 1)
                    act.wait_ge(s_wf, n + 1)
                    act.sem_inc(s_bc, 1)
                elif kind == "dt":
                    _, s, p = use
                    tiles = PARTS[s][p]
                    w = len(tiles) * LEN[s]
                    no = dtx_no(b, s, p)
                    if not (first and (s, p) == (0, 0)):
                        act.wait_ge(s_dtx, no - 1)
                    for m, d in enumerate(tiles):
                        cut = slice(m * LEN[s], (m + 1) * LEN[s])
                        nc.scalar.activation(t_exp[:, cut], work[:, cut], ACT.Abs, bias=cols[:, 1, s, d:d + 1])
                        ins = nc.scalar.activation(t_relu[:, cut], work[:, cut], ACT.Relu, bias=cols[:, 1, s, d:d + 1])
                    ins.then_inc(s_wf, 1)
                    act.wait_ge(s_wf, n + 1)
                    nc.scalar.activation(t_exp[:, 0:w], t_exp[:, 0:w], ACT.Exp, scale=-1.0).then_inc(s_act, 1)
                    act.wait_ge(s_act, no)
                    nc.scalar.activation(t_ln[:, 0:w], t_exp[:, 0:w], ACT.Ln, bias=1.0).then_inc(s_sp, 1)
                else:
                    s = use[1]
                    if s == 0 and not first:
                        act.wait_ge(s_hh, b)
                    elif s and not first:
                        act.wait_ge(s_oi, b * 2 + (s - 2))
                    if s == 0:
                        nc.scalar.activation(o[0][:], work[:], ACT.Copy).then_inc(s_wf, 1)
                    else:
                        t = LEN[s]
                        nc.scalar.activation(o[s][:, 0:1], work[:, 0:1], ACT.Copy)
                        nc.scalar.activation(o[s][:, t + 1:t + 2], work[:, t - 1:t], ACT.Copy)
                        nc.scalar.activation(o[s][:, 1:t + 1], work[:, 0:t], ACT.Copy).then_inc(s_wf, 1)
                    act.wait_ge(s_wf, n + 1)
                    act.sem_inc(s_o, 1)

            def decays(b, u, begins):
                s, v = scale_of(u)
                n = b * NU + u
                r = u % 2
                act.wait_ge(s_dtx, b * 4 + (2, 3, 4)[s])
                if not begins:
                    act.wait_ge(s_scan, n - 1)
                for d in range(DT2):
                    for m in range(NS[s]):
                        q = v * NS[s] + m
                        ins = nc.scalar.activation(da[:, r, d, m * LEN[s]:(m + 1) * LEN[s]], dt_[s][:, d, :], ACT.Exp,
                                                   scale=decay[:, s, d, q:q + 1])
                ins.then_inc(s_da, 1)

            def main(b, k, base, at, prev, nxt):
                n = base
                for u in range(NU):
                    for use in at.get(u, []):
                        row = row_of(use, b, u)
                        later = use[0] == "turn" or (use[0] not in ("out", "fuse") and use[1] == 0)
                        consume(n, use, row, not prev and not later)
                        n = n + 1
                    n = n + 1
                    if u + 1 < NU:
                        decays(b, u + 1, not prev and u == 0)
                    elif nxt:
                        decays(b + 1, 0, False)

            act.wait_ge(s_load, 13 * 16)
            nc.scalar.activation(decay[:], decay[:], ACT.Exp).then_inc(s_prep, 1)
            act.wait_ge(s_const, 5)
            act.wait_ge(s_fold, SCALES + 2)
            for n, use in enumerate(FIRST):
                consume(n, use, 0, True)
            decays(0, 0, True)
            batches(main, act)
            consume(END, ("out", 2), LAST, False)

        @block.vector
        def _(dve):
            def norm(b, k):
                dve.wait_ge(s_hl[k], (b - k) * 8 + 16)
                for j in range(TPB):
                    tile = b * TPB + j
                    ins = nc.vector.tensor_scalar(xn[:, k, j, :], hl[:, k, j, :], g.mean[:, bass.ds(tile, 1)],
                                                  g.rstd[:, bass.ds(tile, 1)], ALU.subtract, ALU.mult)
                ins.then_inc(s_xn, 1)

            def gate_out(b, s):
                tiles = list(range(DT2))
                dve.wait_ge(s_y, units_done(b, s))
                for d in tiles:
                    ins = nc.vector.scalar_tensor_tensor(out=dtx[s][:, d, :], in0=xc[s][:, d, :], scalar=cols[:, 2, s, d:d + 1],
                                                         in1=yps[:, d, 0:LEN[s]], op0=ALU.mult, op1=ALU.add)
                ins.then_inc(s_post1, 1)
                dve.wait_ge(s_post1, b * 3 + (s + 1))
                nc.vector.tensor_tensor(flat(dtx[s], tiles), flat(dtx[s], tiles), flat(sz[s], tiles),
                                        ALU.mult).then_inc(s_post, 1)

            def fuse(n, b, k):
                dve.wait_ge(s_wr, n + 1)
                nc.vector.tensor_tensor(hh[:].rearrange("p j d -> p (j d)"), work[:], xn[:, k].rearrange("p j d -> p (j d)"),
                                        ALU.add).then_inc(s_wf, 1)
                dve.wait_ge(s_wf, n + 1)
                dve.sem_inc(s_hh, 1)
                for j in range(TPB):
                    ins = nc.vector.bn_stats(st6[:, j, :], hh[:, j, :])
                ins.then_inc(s_hst, 1)

            def normalise(b):
                dve.wait_ge(s_rs, b + 1)
                for j in range(TPB):
                    ins = nc.vector.tensor_scalar(hh[:, j, :], hh[:, j, :], st_m[:, j:j + 1], st_v[:, j:j + 1],
                                                  ALU.subtract, ALU.mult)
                ins.then_inc(s_nm, 1)

            def stats(b, k):
                dve.wait_ge(s_h3, b + 1)
                for j in range(TPB):
                    ins = nc.vector.bn_stats(g.stat[:, bass.ds(b * TPB + j, 1), :], hl[:, k, j, :])
                ins.then_inc(s_hst, 1)

            def main(b, k, base, at, prev, nxt):
                n = base
                for u in range(NU):
                    s, v = scale_of(u)
                    for use in at.get(u, []):
                        if use[0] == "fuse":
                            fuse(n, b - 1, 1 - k)
                        n = n + 1
                    i = b * NU + u
                    r = u % 2
                    if u == 15 and nxt:
                        norm(b + 1, 1 - k)
                    dve.wait_ge(s_wr, n + 1)
                    if v == 0:
                        dve.wait_ge(s_dtx, b * 4 + (2, 3, 4)[s])
                    if prev or u >= 2:
                        dve.wait_ge(s_y, i - 1)
                    shape = [P, NS[s], LEN[s]]
                    for d in range(DT2):
                        ins = nc.vector.tensor_tensor(hb[:, r, d, :].rearrange("p (n t) -> p n t", n=NS[s]),
                                                      work[:].rearrange("p (n t) -> p n t", n=NS[s]),
                                                      dtx[s][:, d, :].unsqueeze(1).to_broadcast(shape), ALU.mult)
                    ins.then_inc(s_wf, 1)
                    dve.wait_ge(s_wf, n + 1)
                    n = n + 1
                    dve.wait_ge(s_da, i + 1)
                    for d in range(DT2):
                        for m in range(NS[s]):
                            c = slice(m * LEN[s], (m + 1) * LEN[s])
                            ins = nc.vector.tensor_tensor_scan(hb[:, r, d, c], da[:, r, d, c], hb[:, r, d, c], 0.0,
                                                               ALU.mult, ALU.add)
                    ins.then_inc(s_scan, 1)
                    if v == 0 and s > 0:
                        gate_out(b, s - 1)
                    elif u == 0 and prev:
                        gate_out(b - 1, SCALES - 1)
                    dve.wait_ge(s_c, i + 1)
                    dve.wait_ge(s_scan, i + 1)
                    for d in range(DT2):
                        ins = nc.vector.tensor_tensor(hb[:, r, d, :], hb[:, r, d, :], cps[:], ALU.mult)
                    ins.then_inc(s_g, 1)
                    if prev and u == 7:
                        normalise(b - 1)
                    if prev and u == 12:
                        stats(b - 1, 1 - k)

            dve.wait_ge(s_load, 13 * 16)
            for s in range(SCALES):
                nc.vector.tensor_tensor(conv_w[:, s], conv_w[:, s],
                                        hb[:, 0, 0, s * DI:(s + 1) * DI].unsqueeze(1).to_broadcast([P, TAPS, DI]),
                                        ALU.mult).then_inc(s_fold, 1)
            nc.vector.tensor_copy(pick[:], pick_f[:].to_broadcast([P, 2 * ST, P])).then_inc(s_fold, 1)
            dve.wait_ge(s_prep, 1)
            nc.vector.tensor_scalar(decay[:], decay[:], -1.0, None, ALU.mult).then_inc(s_fold, 1)
            dve.wait_ge(s_fold, SCALES + 2)
            norm(0, 0)
            batches(main, dve)
            gate_out(LAST, SCALES - 1)
            fuse(END + 1, LAST, LAST % 2)
            normalise(LAST)
            stats(LAST, LAST % 2)

        @block.tensor
        def _(pe):
            def banks(t):
                return [(c, min(HALF, t - c)) for c in range(0, t, HALF)]

            def produce(n, use, b, k, first=False):
                kind = use[0]
                if not first:
                    pe.wait_ge(s_wf, n)
                if kind == "turn":
                    pe.wait_ge(s_xn, b + 1)
                    for j in range(TPB):
                        ins = nc.tensor.transpose(work[:, j * P:(j + 1) * P], xn[:, k, j, :], g.ident[:])
                elif kind == "xi":
                    _, s, p = use
                    for m, d in enumerate(PARTS[s][p]):
                        for c, wd in banks(LEN[s]):
                            for tap in range(TAPS):
                                ins = nc.tensor.matmul(work[:, m * LEN[s] + c:m * LEN[s] + c + wd],
                                                       conv_w[:, s, tap, d * P:(d + 1) * P],
                                                       xts[s][:, tap + c:tap + c + wd], start=(tap == 0),
                                                       stop=(tap == TAPS - 1))
                elif kind == "z":
                    _, s, p = use
                    for m, d in enumerate(PARTS[s][p]):
                        for c, wd in banks(LEN[s]):
                            ins = nc.tensor.matmul(work[:, m * LEN[s] + c:m * LEN[s] + c + wd],
                                                   z_w[:, s, d * P:(d + 1) * P],
                                                   xts[s][:, TAPS - 1 + c:TAPS - 1 + c + wd], start=True, stop=True)
                elif kind == "xp":
                    s = use[1]
                    for c, wd in banks(LEN[s]):
                        for d in range(DT2):
                            ins = nc.tensor.matmul(work[:, c:c + wd], xp_w[:, s, d, :], xc[s][:, d, c:c + wd],
                                                   start=(d == 0), stop=(d == DT2 - 1))
                elif kind == "dt":
                    _, s, p = use
                    for m, d in enumerate(PARTS[s][p]):
                        for c, wd in banks(LEN[s]):
                            ins = nc.tensor.matmul(work[:, m * LEN[s] + c:m * LEN[s] + c + wd],
                                                   dt_w[:, s, d * P:(d + 1) * P], bc_f[0:DTR, c:c + wd],
                                                   start=True, stop=True)
                elif kind == "out":
                    s = use[1]
                    pe.wait_ge(s_post, b * 3 + (s + 1))
                    for c, wd in banks(LEN[s]):
                        for d in range(DT2):
                            ins = nc.tensor.matmul(work[:, c:c + wd], out_w[:, s, d, :], dtx[s][:, d, c:c + wd],
                                                   start=(d == 0), stop=(d == DT2 - 1))
                elif kind == "fuse":
                    pe.wait_ge(s_oi, b * 2 + 2)
                    for j in range(TPB):
                        dst = work[:, j * P:(j + 1) * P]
                        for s in range(SCALES):
                            nc.tensor.matmul(dst, oi[s][:, j * P:(j + 1) * P], fus_w[:, s, :], start=(s == 0), stop=False)
                        ins = nc.tensor.matmul(dst, rowb[0:1, 1, :], rowb[0:1, 0, :], start=False, stop=True)
                ins.then_inc(s_wr, 1)

            def spread(dst, s, v, which, sem_):
                for m in range(NS[s]):
                    q = which * ST + v * NS[s] + m
                    for c, wd in banks(LEN[s]):
                        ins = nc.tensor.matmul(dst[:, m * LEN[s] + c:m * LEN[s] + c + wd], pick[:, q, :],
                                               bc[s][:, c:c + wd], start=True, stop=True)
                ins.then_inc(sem_, 1)

            def total(b, u, reused):
                s, v = scale_of(u)
                pe.wait_ge(s_g, b * NU + u + 1)
                if v == 0 and reused:
                    pe.wait_ge(s_post1, b * 3 + s)
                for d in range(DT2):
                    for m in range(NS[s]):
                        for c, wd in banks(LEN[s]):
                            at = m * LEN[s] + c
                            ins = nc.tensor.matmul(yps[:, d, c:c + wd], g.ident[:], hb[:, u % 2, d, at:at + wd],
                                                   start=(v == 0 and m == 0), stop=(v == UNITS[s] - 1 and m == NS[s] - 1))
                ins.then_inc(s_y, 1)

            def main(b, k, base, at, prev, nxt):
                n = base
                for u in range(NU):
                    s, v = scale_of(u)
                    for use in at.get(u, []):
                        produce(n, use, row_of(use, b, u), 1 - k)
                        n = n + 1
                    pe.wait_ge(s_wf, n)
                    if v == 0:
                        pe.wait_ge(s_split, split_no(b, s))
                    spread(work, s, v, 0, s_wr)
                    n = n + 1
                    if prev or u > 0:
                        pe.wait_ge(s_g, b * NU + u)
                    spread(cps, s, v, 1, s_c)
                    if u > 0:
                        total(b, u - 1, prev or u > 1)
                    elif prev:
                        total(b - 1, NU - 1, True)

            pe.wait_ge(s_const, 5)
            pe.wait_ge(s_fold, SCALES + 2)
            for n, use in enumerate(FIRST):
                produce(n, use, 0, 0, n == 0)
            batches(main, pe)
            total(LAST, NU - 1, True)
            produce(END, ("out", 2), LAST, 0)
            produce(END + 1, ("fuse",), LAST, 0)


E2, K2 = 8, 2


def moe_phase(nc, g, h_in, out, w):
    with ExitStack() as ctx:
        sb = lambda name, shape, dt=F32: ctx.enter_context(nc.sbuf_tensor("t_" + name, shape, dt))
        ps = lambda name, shape, dt=F32: ctx.enter_context(nc.psum_tensor("t_" + name, shape, dt))
        sem = lambda name: ctx.enter_context(nc.semaphore("t_" + name))
        wg = sb("wg", [P, E2])
        rows = sb("rows", [1, E2 + E2 * DM + P])
        up_w = sb("up_w", [P, E2, FF])
        up_b = sb("up_b", [P, E2, FT])
        down_w = sb("down_w", [P, E2, FT, DM])
        order = sb("order", [P, CH, E2])
        h = sb("h", [P, 2, CH, DM])
        xn = sb("xn", [P, CH, DM])
        xt = sb("xt", [P, 2, CW])
        hid = sb("hid", [P, 2, FT, CW])
        lg = sb("lg", [P, CH, E2])
        hot = sb("hot", [P, K2, CH, E2])
        rank = sb("rank", [P, CH])
        top = sb("top", [P, K2, CH])
        mix = sb("mix", [P, K2, CH])
        comb = sb("comb", [P, 2, CH, E2])
        turned = ps("turned", [P, CW])
        logit = ps("logit", [P, CW])
        ups = [ps(f"up{f}", [P, CW]) for f in range(FT)]
        down = [ps(f"down{n}", [P, CW]) for n in range(2)]
        s_load = sem("weights_loaded")
        s_const = sem("constants_set")
        s_h = [sem(f"h_loaded{k}") for k in range(2)]
        s_xn = sem("norm_applied")
        s_turn = sem("rows_turned")
        s_xt = sem("rows_t_ready")
        s_logit = sem("logits_ready")
        s_r = sem("routing_steps")
        s_w = sem("weight_steps")
        s_d = sem("top_difference_ready")
        s_e = sem("top_exp_ready")
        s_up = sem("up_done")
        s_act = sem("silu_done")
        s_down = sem("down_done")
        s_add = sem("outputs_added")
        s_out = [sem(f"stored{k}") for k in range(2)]
        block = ctx.enter_context(nc.Block())
        PAIRS = CHUNKS // 2
        R = 13

        def chunk(t, c):
            return t[bass.ds(c * CW, CW), :].rearrange("(j p) d -> p j d", p=P)

        @block.sync
        def _(sp):
            for dst, src in ((wg[:], w["wg"]), (rows[0:1, 0:E2], w["bg"]), (rows[0:1, E2:E2 + E2 * DM], w["b2"]),
                             (up_w[:], w["w1"]), (up_b[:], w["b1"]), (down_w[:], w["w2"])):
                sp.dma_start(dst, src).then_inc(s_load, 16)
            sp.dma_start(h[:, 0], chunk(h_in, 0)).then_inc(s_h[0], 16)
            sp.dma_start(h[:, 1], chunk(h_in, 1)).then_inc(s_h[1], 16)

            def store(c, k):
                sp.wait_ge(s_add, (c + 1) * E2)
                sp.dma_start(chunk(out, c), h[:, k]).then_inc(s_out[k], 16)
                sp.wait_ge(s_out[k], (c - k) * 8 + 16)

            with sp.Fori(0, PAIRS - 1) as i:
                for k in range(2):
                    store(i * 2 + k, k)
                    sp.dma_start(h[:, k], chunk(h_in, i * 2 + (k + 2))).then_inc(s_h[k], 16)
            store(CHUNKS - 2, 0)
            store(CHUNKS - 1, 1)

        @block.gpsimd
        def _(pool):
            st = Steps(s_const)
            st.link(pool, nc.gpsimd.memset(rows[0:1, E2 + E2 * DM:], 1.0))
            for e in range(E2):
                st.link(pool, nc.gpsimd.memset(order[:, :, e:e + 1], float(E2 - e)))

        def chunks(body, eng):
            body(0, 0, 0, True)
            body(1, 1, 1, True)
            with eng.Fori(1, PAIRS - 1) as i:
                body(i * 2, 0, 2, True)
                body(i * 2 + 1, 1, 2, True)
            body(CHUNKS - 2, 0, 2, True)
            body(CHUNKS - 1, 1, 2, False)

        @block.scalar
        def _(act):
            def copy_t(c, k, before):
                act.wait_ge(s_turn, c + 1)
                if before > 1:
                    act.wait_ge(s_up, (c - 1) * E2 * FT)
                    act.wait_ge(s_logit, c - 1)
                nc.scalar.activation(xt[:, k, :], turned[:], ACT.Copy).then_inc(s_xt, 1)

            def body(c, k, before, more):
                for e in range(E2):
                    n = c * E2 + e
                    for f in range(FT):
                        act.wait_ge(s_up, n * FT + (f + 1))
                        if f == 0 and (before or e >= 2):
                            act.wait_ge(s_down, n - 1)
                        nc.scalar.activation(hid[:, e % 2, f, :], ups[f][:], ACT.Silu,
                                             bias=up_b[:, e, f:f + 1]).then_inc(s_act, 1)
                    if e == 1 and more:
                        copy_t(c + 1, 1 - k, min(before + 1, 2))
                    if e == 5 and more:
                        act.wait_ge(s_d, c + 2)
                        nc.scalar.activation(mix[:, 1, :], mix[:, 0, :], ACT.Exp).then_inc(s_e, 1)

            act.wait_ge(s_load, 6 * 16)
            copy_t(0, 0, 0)
            act.wait_ge(s_d, 1)
            nc.scalar.activation(mix[:, 1, :], mix[:, 0, :], ACT.Exp).then_inc(s_e, 1)
            chunks(body, act)

        @block.vector
        def _(dve):
            def norm(c, k):
                dve.wait_ge(s_h[k], (c - k) * 8 + 16)
                for j in range(CH):
                    ins = nc.vector.tensor_scalar(xn[:, j, :], h[:, k, j, :], g.mean[:, bass.ds(c * CH + j, 1)],
                                                  g.rstd[:, bass.ds(c * CH + j, 1)], ALU.subtract, ALU.mult)
                ins.then_inc(s_xn, 1)

            BIG = [P, CH, E2]

            def choose(c, k):
                st = Steps(s_r, c * R)
                dve.wait_ge(s_logit, c + 1)
                st.link(dve, nc.vector.tensor_copy(lg[:].rearrange("p j e -> p (j e)"), logit[:, 0:CH * E2]))
                for n in range(K2):
                    st.link(dve, nc.vector.tensor_reduce(top[:, n, :], lg[:], AX_X, ALU.max))
                    st.link(dve, nc.vector.tensor_tensor(hot[:, n], lg[:], top[:, n, :].to_broadcast(BIG), ALU.is_ge))
                    st.link(dve, nc.vector.tensor_tensor(hot[:, n], hot[:, n], order[:], ALU.mult))
                    st.link(dve, nc.vector.tensor_reduce(rank[:], hot[:, n], AX_X, ALU.max))
                    st.link(dve, nc.vector.tensor_tensor(hot[:, n], order[:], rank[:].to_broadcast(BIG), ALU.is_equal))
                    if n == 0:
                        st.link(dve, nc.vector.scalar_tensor_tensor(out=lg[:], in0=hot[:, 0], scalar=-3e38, in1=lg[:],
                                                                    op0=ALU.mult, op1=ALU.add))
                st.up(nc.vector.tensor_tensor(mix[:, 0, :], top[:, 1, :], top[:, 0, :], ALU.subtract))
                st.wait(dve)
                dve.sem_inc(s_d, 1)

            def weigh(c, k, before):
                st = Steps(s_w, c * 6)
                dve.wait_ge(s_e, c + 1)
                st.link(dve, nc.vector.tensor_scalar(top[:, 0, :], mix[:, 1, :], 1.0, None, ALU.add))
                st.link(dve, nc.vector.reciprocal(top[:, 0, :], top[:, 0, :]))
                st.link(dve, nc.vector.tensor_tensor(top[:, 1, :], top[:, 0, :], mix[:, 1, :], ALU.mult))
                for n in range(K2):
                    st.link(dve, nc.vector.tensor_tensor(hot[:, n], hot[:, n], top[:, n, :].to_broadcast(BIG), ALU.mult))
                st.link(dve, nc.vector.tensor_tensor(comb[:, k], hot[:, 0], hot[:, 1], ALU.add))

            def body(c, k, before, more):
                for e in range(E2):
                    n = c * E2 + e
                    dve.wait_ge(s_down, n + 1)
                    if before or e:
                        dve.wait_ge(s_add, n)
                    for j in range(CH):
                        ins = nc.vector.scalar_tensor_tensor(out=h[:, k, j, :], in0=down[e % 2][:, j * P:(j + 1) * P],
                                                             scalar=comb[:, k, j, e:e + 1], in1=h[:, k, j, :],
                                                             op0=ALU.mult, op1=ALU.add)
                    ins.then_inc(s_add, 1)
                    if more and e == 0:
                        norm(c + 1, 1 - k)
                    if more and e == 3:
                        choose(c + 1, 1 - k)
                    if more and e == 6:
                        weigh(c + 1, 1 - k, before)

            dve.wait_ge(s_const, 1 + E2)
            norm(0, 0)
            choose(0, 0)
            weigh(0, 0, 0)
            chunks(body, dve)

        @block.tensor
        def _(pe):
            def turn(c, k, before):
                pe.wait_ge(s_xn, c + 1)
                if before:
                    pe.wait_ge(s_xt, c)
                for j in range(CH):
                    ins = nc.tensor.transpose(turned[:, j * P:(j + 1) * P], xn[:, j, :], g.ident[:])
                ins.then_inc(s_turn, 1)

            def router(c, k, before):
                pe.wait_ge(s_xt, c + 1)
                if before:
                    pe.wait_ge(s_r, c * R)
                for j in range(CH):
                    o = logit[:, j * E2:(j + 1) * E2]
                    nc.tensor.matmul(o, xt[:, k, j * P:(j + 1) * P], wg[:], start=True, stop=False)
                    ins = nc.tensor.matmul(o, rows[0:1, E2 + E2 * DM:], rows[0:1, 0:E2], start=False, stop=True)
                ins.then_inc(s_logit, 1)

            def up(n, e, k, begins):
                for f in range(FT):
                    if not begins:
                        pe.wait_ge(s_act, (n - 1) * FT + (f + 1))
                    nc.tensor.matmul(ups[f][:], up_w[:, e, f * P:(f + 1) * P], xt[:, k, :], start=True,
                                     stop=True).then_inc(s_up, 1)

            def down_(n, e, early):
                pe.wait_ge(s_act, n * FT + FT)
                if not early:
                    pe.wait_ge(s_add, n - 1)
                for j in range(CH):
                    o = down[e % 2][:, j * P:(j + 1) * P]
                    for f in range(FT):
                        nc.tensor.matmul(o, hid[:, e % 2, f, j * P:(j + 1) * P], down_w[:, e, f, :], start=(f == 0),
                                         stop=False)
                    ins = nc.tensor.matmul(o, rows[0:1, E2 + E2 * DM:], rows[0:1, E2 + e * DM:E2 + (e + 1) * DM],
                                           start=False, stop=True)
                ins.then_inc(s_down, 1)

            def body(c, k, before, more):
                for e in range(E2):
                    n = c * E2 + e
                    if e + 1 < E2:
                        up(n + 1, e + 1, k, False)
                    elif more:
                        up(n + 1, 0, 1 - k, False)
                    down_(n, e, not before and e < 2)
                    if more and e == 1:
                        turn(c + 1, 1 - k, True)
                    if more and e == 2:
                        router(c + 1, 1 - k, True)

            pe.wait_ge(s_load, 6 * 16)
            pe.wait_ge(s_const, 1 + E2)
            turn(0, 0, 0)
            router(0, 0, 0)
            up(0, 0, 0, True)
            chunks(body, pe)


def lm_tower(nc, out, a):
    scratch = lambda name, shape, dt=F32: nc.dram_tensor(name, shape, dt).ap()
    part_rows = scratch("part_rows", (2, P, 3, SEQ), BF16)
    max_rows = scratch("max_rows", (3, HEADS * SEQ), BF16)
    slots_x = scratch("slots_x", (GE * CAP, DM))
    slots_y = scratch("slots_y", (GE * CAP, DM))
    first_out = scratch("first_layer_out", (TOK, DM))
    mixed_out = scratch("mixed_out", (TOK, DM))
    with ExitStack() as ctx:
        g = setup(nc, ctx, a["identity"])
        with ExitStack() as first:
            setup_h(nc, first, g)
            embed_phase(nc, g, a["x"], [a["table2"], a["table3"], a["table4"]], a["tok_w"], a["tok_b"], slots_x)
            norm_phase(nc, g, "norm0")
            attention_phase(nc, g, a["attn_w"], a["attn_bqk"], a["attn_bv"], a["attn_out_w"], a["attn_out_b"],
                            a["rope_cos"], a["rope_sin"], part_rows, max_rows)
            norm_phase(nc, g, "norm1")
            setup_slots(nc, first, g)
            route_phase(nc, g, a["router_w"], a["router_b"], a["shared_w1"], a["shared_b1"], a["shared_w2"],
                        a["shared_b2"], a["upto"], slots_x)
            experts_phase(nc, g, slots_x, slots_y, a["experts_w1"], a["experts_b1"], a["experts_w2"], a["experts_b2"])
            combine_phase(nc, g, slots_y, first_out)
            norm_phase(nc, g, "norm2")
        mamba_phase(nc, g, first_out, mixed_out, {k[6:]: v for k, v in a.items() if k.startswith("mamba_")})
        norm_phase(nc, g, "norm3")
        moe_phase(nc, g, mixed_out, out, {k[4:]: v for k, v in a.items() if k.startswith("moe_")})


def lay_out(z):
    import numpy as np
    c = np.ascontiguousarray
    f = np.float32
    banks = lambda name: np.concatenate([z[f"L0_ffn_{name}_sp"], z[f"L0_ffn_{name}_fq"]], axis=-1 if name[1] == "r" else 0)
    a = {"identity": np.eye(P, dtype=f), "x": z["x"], "table2": z["L0_tok_emb_2"], "table3": z["L0_tok_emb_3"],
         "table4": z["L0_tok_emb_4"], "tok_w": c(z["L0_tok_proj_w"].T), "tok_b": z["L0_tok_proj_b"]}

    w, b = z["L0_attn_Wqkv"], z["L0_attn_bqkv"]
    swap = np.arange(DM) ^ 1
    q, k, v = (w[n * DM:(n + 1) * DM] for n in range(3))
    bq, bk = b[0:DM], b[DM:2 * DM]
    a["attn_w"] = c(np.stack([q.T, q[swap].T, k.T, k[swap].T, v.T], axis=1))
    a["attn_bqk"] = c(np.stack([bq, bq[swap], bk, bk[swap]], axis=1))
    a["attn_bv"] = c(b[None, 2 * DM:])
    a["attn_out_w"] = c(z["L0_attn_Wproj"].T)
    a["attn_out_b"] = c(z["L0_attn_bproj"][None])
    freq = (1.0 / (f(10000.0) ** (np.arange(0, HD, 2, dtype=f) / f(HD)))).astype(f)
    angle = np.outer(np.arange(SEQ, dtype=f), freq).astype(f).astype(np.float64)
    pair = np.arange(DM) % HD // 2
    sign = np.where(np.arange(DM) % 2, 1.0, -1.0)[:, None]
    a["rope_cos"] = c(np.cos(angle)[:, pair].T.astype(f))
    a["rope_sin"] = c((np.sin(angle)[:, pair].T * sign).astype(f))

    a["router_w"] = c(banks("Wr"))
    a["router_b"] = c(banks("br")[None])
    a["shared_w1"] = z["L0_ffn_Ws1"]
    a["shared_b1"] = c(z["L0_ffn_bs1"].reshape(FT, P).T)
    a["shared_w2"] = c(z["L0_ffn_Ws2"].reshape(FT, P, DM).transpose(1, 0, 2))
    a["shared_b2"] = c(z["L0_ffn_bs2"][None])
    a["upto"] = np.triu(np.ones((P, P), f))
    a["experts_w1"] = c(banks("W1"))
    a["experts_b1"] = c(banks("b1").reshape(GE, FT, P).transpose(0, 2, 1))
    a["experts_w2"] = c(banks("W2"))
    a["experts_b2"] = c(banks("b2"))

    m = lambda name: z["L1_attn_" + name]
    tiles = lambda v: v.reshape(SCALES, DT2, P).transpose(2, 0, 1)
    xp = m("xp_w")
    bc = xp[:, DTR:]
    pick = np.zeros((P, 2 * ST), f)
    for n in range(2 * ST):
        pick[[DTR * part + n for part in (1, 2, 3)], n] = 1.0
    a.update({
        "mamba_conv_w": c(m("conv_w").transpose(0, 2, 1)),
        "mamba_xi_w": c(m("in_w")[:, :DI].transpose(2, 0, 1).reshape(DM, SCALES * DI)),
        "mamba_z_w": c(m("in_w")[:, DI:].transpose(2, 0, 1)),
        "mamba_xp_w": c(np.concatenate([xp[:, :DTR], bc, bc, bc], 1).reshape(SCALES, P, DT2, P).transpose(3, 0, 2, 1)),
        "mamba_dt_w": c(m("dt_w").transpose(2, 0, 1)),
        "mamba_out_w": c(m("out_w").reshape(SCALES, DM, DT2, P).transpose(3, 0, 2, 1)),
        "mamba_fus_w": c(m("fusion_w").reshape(DM, SCALES, DM).transpose(2, 1, 0)),
        "mamba_cols": c(np.stack([tiles(m("conv_b")), tiles(m("dt_b")), tiles(m("D_skip"))], 1)),
        "mamba_a_log": c(m("A_log").reshape(SCALES, DT2, P, ST).transpose(2, 0, 1, 3)),
        "mamba_fus_b": c(m("fusion_b")[None]), "mamba_ln_g": m("ln_g"), "mamba_ln_b": m("ln_b"), "mamba_pick": pick})

    t = lambda name: z["L1_ffn_" + name]
    a.update({"moe_wg": t("Wg"), "moe_bg": c(t("bg")[None]), "moe_w1": c(t("W1").transpose(1, 0, 2)),
              "moe_b1": c(t("b1").reshape(E2, FT, P).transpose(2, 0, 1)),
              "moe_w2": c(t("W2").reshape(E2, FT, P, DM).transpose(2, 0, 1, 3)),
              "moe_b2": c(t("b2").reshape(1, E2 * DM))})
    return a


def kernel(**inputs):
    import numpy as np
    import concourse.bacc as bacc
    from concourse.bass_utils import run_bass_kernel_spmd

    arrays = lay_out({name: np.asarray(value) for name, value in inputs.items()})
    nc = bacc.Bacc("TRN2", target_bir_lowering=False, num_devices=1)
    aps = {name: nc.dram_tensor(name, value.shape, mybir.dt.from_np(value.dtype), kind="ExternalInput").ap()
           for name, value in arrays.items()}
    out = nc.dram_tensor("out", (TOK, DM), F32, kind="ExternalOutput").ap()
    lm_tower(nc, out, aps)
    result = run_bass_kernel_spmd(nc, [arrays], core_ids=[0])
    return result.results[0]["out"].reshape(BATCH, SEQ, DM)
```

```python
from contextlib import ExitStack

import concourse.bass as bass
from concourse import mybir

F32 = mybir.dt.float32
BF16 = mybir.dt.bfloat16
I32 = mybir.dt.int32
U32 = mybir.dt.uint32
ALU = mybir.AluOpType
ACT = mybir.ActivationFunctionType
AX_X = mybir.AxisListType.X

P = 128
BATCH, SEQ, DM = 16, 1024, 128
TOK = BATCH * SEQ
TILES = TOK // P
TPB = SEQ // P
VOCAB = 25000
GRAMS = 3
LN_EPS = 1e-5


class Steps:

    def __init__(self, sem, base=0):
        self.sem, self.base, self.n = sem, base, 0

    def up(self, ins):
        self.n += 1
        ins.then_inc(self.sem, 1)
        return self.n

    def wait(self, eng, n=None):
        eng.wait_ge(self.sem, self.base + (self.n if n is None else n))

    def link(self, eng, ins):
        self.up(ins)
        self.wait(eng)


def embed_phase(nc, g, x, tables, proj_t, proj_b, slots_x):
    with ExitStack() as ctx:
        sb = lambda name, shape, dt=F32: ctx.enter_context(nc.sbuf_tensor("e_" + name, shape, dt))
        ps = lambda name, shape, dt=F32: ctx.enter_context(nc.psum_tensor("e_" + name, shape, dt))
        sem = lambda name: ctx.enter_context(nc.semaphore("e_" + name))
        W = P + 3
        xi = sb("xi", [P, W], I32)
        xf = sb("xf", [P, W])
        h2 = sb("h2", [P, W - 1])
        h3 = sb("h3", [P, W - 2])
        h4 = sb("h4", [P, W - 3])
        quo = sb("quo", [P, W], I32)
        tmp = sb("tmp", [P, W])
        raw = sb("raw", [P, W])
        ids = sb("ids", [P, TILES, GRAMS], U32)
        cols = sb("cols", [P, 2, TPB * GRAMS], U32)
        SLOTS = 4
        rows = sb("rows", [P, SLOTS, GRAMS * DM])
        rows_t = sb("rows_t", [P, 2, GRAMS * P])
        wproj = sb("wproj", [P, GRAMS, DM])
        bias = sb("bias", [P, DM])
        first = sb("first", [P, GRAMS])
        last = sb("last", [P, GRAMS])
        FILL = 8
        zeros = sb("zeros", [P, FILL, DM])
        turned = [ps(f"turned{i}", [P, 512]) for i in range(2)]
        summed = [ps(f"summed{i}", [P, 512]) for i in range(2)]

        s_zero = sem("x_zeroed")
        s_x = sem("x_loaded")
        s_w = sem("weights_loaded")
        s_fill = sem("zero_rows_set")
        s_filled = sem("slots_zeroed")
        s_mask0 = sem("masks_set")
        s_mask = sem("masks_ready")
        s_hash = sem("hash_steps")
        s_idst = sem("ids_turned")
        s_cols = sem("id_columns_ready")
        s_rows = [sem(f"rows_gathered{i}") for i in range(SLOTS)]
        s_masked = sem("rows_masked")
        s_turned = sem("rows_turned")
        s_rt = sem("rows_t_ready")
        s_sum = sem("projection_done")
        s_h = sem("h_written")
        s_pool = sem("pool_step")
        block = ctx.enter_context(nc.Block())
        x2 = x.rearrange("b (t p) -> (b t) p", p=P)
        PAIRS = BATCH // 2
        T2 = 2 * TPB

        @block.sync
        def _(sp):
            sp.dma_start(wproj[:], proj_t.rearrange("(g f) d -> f g d", g=GRAMS)).then_inc(s_w, 16)
            sp.dma_start(bias[:], proj_b.partition_broadcast(P)).then_inc(s_w, 16)
            sp.wait_ge(s_zero, 1)
            with nc.allow_non_contiguous_dma(reason="halo columns of the token ids"):
                sp.dma_start(xi[:, 2:P + 2], x2).then_inc(s_x, 16)
                sp.dma_start(xi[1:P, 0:2], x2[0:P - 1, P - 2:P]).then_inc(s_x, 16)
                sp.dma_start(xi[0:P - 1, P + 2:P + 3], x2[1:P, 0:1]).then_inc(s_x, 16)
            sp.wait_ge(s_fill, 1)
            fills = slots_x.shape[0] // (P * FILL)
            with sp.Fori(0, fills) as i:
                sp.dma_start(slots_x[bass.ds(i * (P * FILL), P * FILL), :].rearrange("(p j) d -> p j d", p=P),
                             zeros[:]).then_inc(s_filled, 16)
            sp.wait_ge(s_filled, fills * 16)

        @block.gpsimd
        def _(pool):
            nc.gpsimd.memset(zeros[:], 0.0).then_inc(s_fill, 1)
            nc.gpsimd.memset(first[:], 1.0).then_inc(s_mask0, 1)
            nc.gpsimd.memset(last[:], 1.0).then_inc(s_mask0, 1)
            pool.wait_ge(s_mask0, 2)
            for gram in range(GRAMS):
                lead = (gram + 2) // 2
                tail = gram + 1 - lead
                nc.gpsimd.affine_select(out=first[:, gram:gram + 1], in_=first[:, gram:gram + 1],
                                        compare_op=ALU.is_ge, fill=0.0, base=-lead, pattern=[[0, 1]],
                                        channel_multiplier=1).then_inc(s_mask, 1)
                nc.gpsimd.affine_select(out=last[:, gram:gram + 1], in_=last[:, gram:gram + 1],
                                        compare_op=ALU.is_ge, fill=0.0, base=P - 1 - tail, pattern=[[0, 1]],
                                        channel_multiplier=-1).then_inc(s_mask, 1)

            def gather(i, j, reused):
                slot = j % SLOTS
                if j % TPB == 0:
                    pool.wait_ge(s_cols, 2 * i + j // TPB + 1)
                if reused:
                    pool.wait_ge(s_turned, i * T2 + j - SLOTS + 1)
                pool.sem_inc(s_pool, 1)
                for gram in range(GRAMS):
                    c = (j % TPB) * GRAMS + gram
                    nc.gpsimd.indirect_dma_start(
                        rows[:, slot, gram * DM:(gram + 1) * DM], None, tables[gram],
                        bass.IndirectOffsetOnAxis(ap=cols[:, j // TPB, c:c + 1], axis=0)).then_inc(s_rows[slot], 16)

            for j in range(T2):
                gather(0, j, j >= SLOTS)
            with pool.Fori(1, PAIRS) as i:
                for j in range(T2):
                    gather(i, j, True)

        @block.vector
        def _(dve):
            st = Steps(s_hash)
            nc.vector.memset(xi[:], 0).then_inc(s_zero, 1)
            dve.wait_ge(s_x, 48)
            st.link(dve, nc.vector.tensor_copy(xf[:], xi[:]))

            def step(out, prev, nxt, n):
                r, t, q = raw[:, 0:n], tmp[:, 0:n], quo[:, 0:n]
                st.link(dve, nc.vector.scalar_tensor_tensor(out=r, in0=prev, scalar=64.0, in1=nxt,
                                                            op0=ALU.mult, op1=ALU.add))
                st.link(dve, nc.vector.tensor_scalar(q, r, 1.0 / VOCAB, None, ALU.mult))
                st.link(dve, nc.vector.tensor_copy(t, q))
                st.link(dve, nc.vector.scalar_tensor_tensor(out=r, in0=t, scalar=-float(VOCAB), in1=r,
                                                            op0=ALU.mult, op1=ALU.add))
                st.link(dve, nc.vector.tensor_scalar(t, r, 0.0, float(VOCAB), ALU.is_lt, ALU.mult))
                st.link(dve, nc.vector.tensor_tensor(r, r, t, ALU.add))
                st.link(dve, nc.vector.tensor_scalar(t, r, float(VOCAB), -float(VOCAB), ALU.is_ge, ALU.mult))
                st.link(dve, nc.vector.tensor_tensor(out, r, t, ALU.add))

            step(h2[:], xf[:, 0:W - 1], xf[:, 1:W], W - 1)
            step(h3[:], h2[:, 0:W - 2], xf[:, 2:W], W - 2)
            step(h4[:], h3[:, 0:W - 3], xf[:, 3:W], W - 3)
            dve.wait_ge(s_idst, GRAMS)
            st.link(dve, nc.vector.tensor_copy(ids[:].rearrange("p t g -> p g t"),
                                               turned[0][:, 0:GRAMS * P].rearrange("p (g t) -> p g t", g=GRAMS)))
            nc.vector.tensor_copy(cols[:, 0, :], ids[:, 0:TPB, :]).then_inc(s_cols, 1)
            nc.vector.tensor_copy(cols[:, 1, :], ids[:, TPB:2 * TPB, :]).then_inc(s_cols, 1)
            dve.wait_ge(s_w, 32)

            def mask(i, j):
                if j % TPB in (0, TPB - 1):
                    slot, m = j % SLOTS, first if j % TPB == 0 else last
                    dve.wait_ge(s_rows[slot], i * (T2 // SLOTS * 48) + (j // SLOTS + 1) * 48)
                    for gram in range(GRAMS):
                        c = slice(gram * DM, (gram + 1) * DM)
                        ins = nc.vector.tensor_scalar(rows[:, slot, c], rows[:, slot, c], m[:, gram:gram + 1], None,
                                                      ALU.mult)
                    ins.then_inc(s_masked, 1)

            def finish(i, j, tile):
                dve.wait_ge(s_sum, i * T2 + j + 1)
                nc.vector.tensor_tensor(g.h[:, tile, :], summed[j % 2][:, 0:DM], bias[:], ALU.add).then_inc(s_h, 1)
                dve.wait_ge(s_h, i * T2 + j + 1)
                nc.vector.bn_stats(g.stat[:, tile, :], g.h[:, tile, :])

            dve.wait_ge(s_mask, 2 * GRAMS)

            def tiles(i, fill):
                for j in range(T2):
                    mask(i, j)
                    if j >= 1:
                        finish(i, j - 1, i * T2 + (j - 1))
                    if fill and j % TPB == TPB - 1:
                        half = j // TPB
                        for slot in range(SLOTS):
                            dve.wait_ge(s_rows[slot], i * (T2 // SLOTS * 48) + (half + 1) * (TPB // SLOTS) * 48)
                        nc.vector.tensor_copy(cols[:, half, :],
                                              ids[:, bass.ds((i + 1) * T2 + half * TPB, TPB), :]).then_inc(s_cols, 1)
                finish(i, T2 - 1, i * T2 + (T2 - 1))

            with dve.Fori(0, PAIRS - 1) as i:
                tiles(i, True)
            tiles(PAIRS - 1, False)

        @block.scalar
        def _(act):
            def spread(i, j, reused):
                act.wait_ge(s_turned, i * T2 + j + 1)
                if reused:
                    act.wait_ge(s_sum, i * T2 + j - 1)
                nc.scalar.activation(rows_t[:, j % 2, :], turned[j % 2][:, 0:GRAMS * P], ACT.Copy).then_inc(s_rt, 1)

            for j in range(T2):
                spread(0, j, j >= 2)
            with act.Fori(1, PAIRS) as i:
                for j in range(T2):
                    spread(i, j, True)

        @block.tensor
        def _(pe):
            pe.wait_ge(s_hash, 1 + 8 * GRAMS)
            for gram, src in enumerate((h2[:, 1:P + 1], h3[:, 1:P + 1], h4[:])):
                nc.tensor.transpose(turned[0][:, gram * P:(gram + 1) * P], src, g.ident[:]).then_inc(s_idst, 1)
            pe.wait_ge(s_hash, 2 + 8 * GRAMS)
            pe.wait_ge(s_w, 32)

            def turn(i, j, reused):
                slot = j % SLOTS
                pe.wait_ge(s_rows[slot], i * (T2 // SLOTS * 48) + (j // SLOTS + 1) * 48)
                if j % TPB in (0, TPB - 1):
                    pe.wait_ge(s_masked, 4 * i + 2 * (j // TPB) + (1 if j % TPB == 0 else 2))
                if reused:
                    pe.wait_ge(s_rt, i * T2 + j - 1)
                for gram in range(GRAMS):
                    ins = nc.tensor.transpose(turned[j % 2][:, gram * P:(gram + 1) * P],
                                              rows[:, slot, gram * DM:(gram + 1) * DM], g.ident[:])
                ins.then_inc(s_turned, 1)

            def project(i, j, reused):
                pe.wait_ge(s_rt, i * T2 + j + 1)
                if reused:
                    pe.wait_ge(s_h, i * T2 + j - 1)
                for gram in range(GRAMS):
                    ins = nc.tensor.matmul(summed[j % 2][:, 0:DM], rows_t[:, j % 2, gram * P:(gram + 1) * P],
                                           wproj[:, gram, :], start=(gram == 0), stop=(gram == GRAMS - 1))
                ins.then_inc(s_sum, 1)

            for j in range(T2):
                turn(0, j, j >= 2)
                if j >= 1:
                    project(0, j - 1, j - 1 >= 2)
            with pe.Fori(1, PAIRS) as i:
                project(i - 1, T2 - 1, True)
                for j in range(T2):
                    turn(i, j, True)
                    if j >= 1:
                        project(i, j - 1, True)
            project(PAIRS - 1, T2 - 1, True)


class Resident:
    pass


def setup(nc, ctx, identity):
    g = Resident()
    sb = lambda name, shape, dt=F32: ctx.enter_context(nc.sbuf_tensor("g_" + name, shape, dt))
    g.stat = sb("stat", [P, TILES, 6])
    g.mean = sb("mean", [P, TILES])
    g.rstd = sb("rstd", [P, TILES])
    g.ident = sb("ident", [P, P])
    with nc.semaphore("g_identity_loaded") as s_id, nc.Block() as block:
        @block.sync
        def _(sp):
            sp.dma_start(g.ident[:], identity).then_inc(s_id, 16)
            sp.wait_ge(s_id, 16)
    return g


def setup_h(nc, ctx, g):
    sb = lambda name, shape, dt=F32: ctx.enter_context(nc.sbuf_tensor("g_" + name, shape, dt))
    g.h = sb("h", [P, TILES, DM])


def setup_slots(nc, ctx, g):
    sb = lambda name, shape, dt=F32: ctx.enter_context(nc.sbuf_tensor("g_" + name, shape, dt))
    g.gate = sb("gate", [P, TILES, BANKS])
    g.slot = sb("slot", [P, TILES, BANKS], U32)


def norm_phase(nc, g, name="n"):
    with ExitStack() as ctx:
        sb = lambda part, shape, dt=F32: ctx.enter_context(nc.sbuf_tensor(f"{name}_{part}", shape, dt))
        diff = sb("diff", [P, TILES])
        var = sb("var", [P, TILES])
        std = sb("std", [P, TILES])
        eps = sb("eps", [P, 1])
        s_step = ctx.enter_context(nc.semaphore(name + "_vector_step"))
        s_std = ctx.enter_context(nc.semaphore(name + "_std_ready"))
        block = ctx.enter_context(nc.Block())

        @block.vector
        def _(dve):
            st = Steps(s_step)
            st.up(nc.vector.memset(eps[:], LN_EPS))
            m0, m1, v0, v1 = (g.stat[:, :, c] for c in (1, 4, 2, 5))
            st.link(dve, nc.vector.tensor_tensor(diff[:], m0, m1, ALU.subtract))
            st.link(dve, nc.vector.tensor_tensor(g.mean[:], m0, m1, ALU.add))
            st.link(dve, nc.vector.tensor_scalar(g.mean[:], g.mean[:], 0.5, None, ALU.mult))
            st.link(dve, nc.vector.tensor_tensor(var[:], v0, v1, ALU.add))
            st.link(dve, nc.vector.tensor_tensor(diff[:], diff[:], diff[:], ALU.mult))
            st.link(dve, nc.vector.tensor_scalar(diff[:], diff[:], 0.25 * DM, None, ALU.mult))
            st.link(dve, nc.vector.tensor_tensor(var[:], var[:], diff[:], ALU.add))
            dve.wait_ge(s_std, 1)
            nc.vector.reciprocal(g.rstd[:], std[:])

        @block.scalar
        def _(act):
            act.wait_ge(s_step, 8)
            nc.scalar.activation(std[:], var[:], ACT.Sqrt, bias=eps[:], scale=1.0 / DM).then_inc(s_std, 1)


HEADS, HD = 8, 16
TERMS = ((0, 0), (0, 1), (0, 2), (1, 0), (1, 1), (2, 0))
KQ = HD * len(TERMS)
QUAD = 4
HALF = 512


def attention_phase(nc, g, w_qkv, b_qk, b_v, w_proj, b_proj, cos_t, sin_t, part_rows, max_rows):
    with ExitStack() as ctx:
        sb = lambda name, shape, dt=F32: ctx.enter_context(nc.sbuf_tensor("a_" + name, shape, dt))
        ps = lambda name, shape, dt=F32: ctx.enter_context(nc.psum_tensor("a_" + name, shape, dt))
        sem = lambda name: ctx.enter_context(nc.semaphore("a_" + name))
        wqkv = sb("wqkv", [P, 5, DM])
        bqk = sb("bqk", [P, 4])
        rowb = sb("rowb", [1, 3, DM])
        vb = sb("vb", [P, 1])
        wproj = sb("wproj", [P, DM])
        cos = sb("cos", [P, SEQ])
        sin = sb("sin", [P, SEQ])
        xt = sb("xt", [P, SEQ])
        rope = [sb(f"rope{m}", [P, SEQ]) for m in range(2)]
        ot = rope[0]
        xn = rope[1][:].rearrange("p (i d) -> p i d", d=DM)
        aot = xt
        parts = [sb(f"parts{n}", [P, 3, SEQ], BF16) for n in range(2)]
        qs = [sb(f"qs{n}", [KQ + 3, HEADS, SEQ], BF16) for n in range(2)]
        ks = [sb(f"ks{n}", [KQ + 3, HEADS, SEQ], BF16) for n in range(2)]
        va = [sb(f"va{n}", [P, TPB, HEADS, 32]) for n in range(2)]
        RING = 4
        pt = sb("pt", [P, RING, SEQ])
        tops = sb("tops", [P, 2, HEADS * TPB])
        top = sb("top", [P, P])
        neg = sb("neg", [HEADS * TPB, P])
        negp = sb("negp", [HEADS * TPB, 3, P], BF16)
        inv = sb("inv", [P, TPB, QUAD])
        ao = sb("ao", [P, TPB, DM])
        score = [ps(f"score{n}", [P, SEQ]) for n in range(2)]
        acc = ps("acc", [P, SEQ])
        work = ps("work", [P, SEQ])

        s_load = sem("weights_loaded")
        s_ones = sem("constants_set")
        s_xn = sem("norm_applied")
        s_ready = sem("work_ready")
        s_free = [sem(f"work_free{c}") for c in range(2)]
        s_vb = sem("value_bias_projected")
        s_bias = sem("bias_ready")
        s_top = sem("maxima_ready")
        s_rope = sem("rope_terms_ready")
        s_split = sem("split_steps")
        s_stack = sem("stack_loaded")
        s_pst = sem("parts_stored")
        s_neg = sem("max_split_steps")
        s_mst = sem("max_rows_stored")
        s_mld = sem("max_rows_loaded")
        s_score = sem("scores_ready")
        s_exp = sem("probs_ready")
        s_pv = sem("values_summed")
        s_oa = sem("out_copied_act")
        s_od = sem("out_copied_dve")
        s_ao = sem("norm_steps")
        s_poolstep = sem("pool_step")
        block = ctx.enter_context(nc.Block())

        SLOTS = HEADS * TPB
        LAST = BATCH - 1
        MAXES = [("max", h, i) for h in range(HEADS) for i in range(TPB)]
        QK = [("turn",), ("q", 0), ("q", 1), ("q", 2), ("q", 3)]
        LAG, END_MAXES = 6, 57
        NORM_SLOT = 35
        QK_SLOTS = (37, 39, 40, 49, 50)

        def place(slot):
            return slot // (SLOTS // 2), slot % (SLOTS // 2) // QUAD, slot % QUAD

        def schedule(b):
            at = [([], []) for _ in range(SLOTS)]
            if b < LAST:
                at[1][0].append(("v",))
            if b > 0:
                for s, u in zip((2, 3, 4), (("out", 1), ("heads",), ("proj",))):
                    at[s][0].append(u)
            at[34][0].append(("out", 0))
            if b < LAST - 1:
                for s, u in zip(QK_SLOTS, QK):
                    at[s][0].append(u)
            if b < LAST:
                span = END_MAXES - LAG
                for k in range(span):
                    now = MAXES[k * len(MAXES) // span:(k + 1) * len(MAXES) // span]
                    s = LAG + k
                    at[s][1].extend(now)
                at[END_MAXES][0].append(("tops",))
            return at

        def row_of(use, b):
            if use in (("out", 1), ("heads",), ("proj",)):
                return b - 1
            if use[0] == "out":
                return b
            return b + (2 if use[0] in ("turn", "q") else 1)

        count = lambda plan: sum(len(before) + len(between) for before, between in plan)
        FULL = schedule(1)
        START = [(use, 0) for use in QK + [("v",)]] + [(use, 1) for use in QK] + [(use, 0) for use in MAXES + [("tops",)]]

        def use_base(b):
            return len(START) + count(schedule(0)) + count(FULL) * (b - 1)

        LATE_BASE = use_base(LAST - 1)
        LAST_BASE = LATE_BASE + count(schedule(LAST - 1))
        TAIL_BASE = LAST_BASE + count(schedule(LAST))
        TAIL = [("out", 1), ("heads",), ("proj",)]

        def rows(main, eng):
            main(0, 0, len(START), schedule(0), False, 2)
            with eng.Fori(0, (BATCH - 4) // 2) as i:
                main(i * 2 + 1, 1, use_base(i * 2 + 1), FULL, True, 2)
                main(i * 2 + 2, 0, use_base(i * 2 + 2), FULL, True, 2)
            main(LAST - 2, (LAST - 2) % 2, use_base(LAST - 2), FULL, True, 2)
            main(LAST - 1, (LAST - 1) % 2, LATE_BASE, schedule(LAST - 1), True, 1)
            main(LAST, LAST % 2, LAST_BASE, schedule(LAST), True, 0)

        @block.sync
        def _(sp):
            sp.dma_start(wqkv[:], w_qkv).then_inc(s_load, 16)
            sp.dma_start(bqk[:], b_qk).then_inc(s_load, 16)
            sp.dma_start(vb[:], b_v).then_inc(s_load, 16)
            sp.dma_start(rowb[0:1, 0, :], b_proj).then_inc(s_load, 16)
            sp.dma_start(wproj[:], w_proj).then_inc(s_load, 16)
            sp.dma_start(cos[:], cos_t).then_inc(s_load, 16)
            sp.dma_start(sin[:], sin_t).then_inc(s_load, 16)

            def store(r, n):
                sp.wait_ge(s_split, r * 10 + (5 * n + 5))
                sp.dma_start(part_rows[n], parts[n][:]).then_inc(s_pst, 16)

            def load(r, n, dst):
                sp.wait_ge(s_pst, r * 32 + (16 * n + 16))
                for t, term in enumerate(TERMS):
                    src = part_rows[n, :, term[n], :].rearrange("(h d) t -> d h t", d=HD)
                    sp.dma_start(dst[t * HD:(t + 1) * HD, :, :], src).then_inc(s_stack, 16)

            def stack(r, k, reused, more):
                if reused:
                    sp.wait_ge(s_score, (r - 1) * SLOTS)
                load(r, 0, qs[k])
                store(r, 1)
                load(r, 1, ks[k])
                sp.wait_ge(s_stack, r * 192 + 192)
                if more:
                    store(r + 1, 0)
                sp.wait_ge(s_neg, r * 4 + 4)
                sp.dma_start(max_rows.rearrange("j (u q) -> u j q", q=P), negp[:]).then_inc(s_mst, 16)
                sp.wait_ge(s_mst, r * 16 + 16)
                sp.dma_start(qs[k][KQ:KQ + 3, :, :], max_rows.rearrange("j (h q) -> j h q", h=HEADS)).then_inc(s_mld, 16)

            store(0, 0)
            stack(0, 0, False, True)
            stack(1, 1, False, True)
            with sp.Fori(1, BATCH // 2 - 1) as i:
                stack(i * 2, 0, True, True)
                stack(i * 2 + 1, 1, True, True)
            stack(LAST - 1, (LAST - 1) % 2, True, True)
            stack(LAST, LAST % 2, True, False)

        @block.gpsimd
        def _(pool):
            st = Steps(s_ones)
            for n in range(2):
                st.link(pool, nc.gpsimd.memset(va[n][:], 1.0))
                st.link(pool, nc.gpsimd.memset(ks[n][KQ:KQ + 3, :, :], 1.0))
            st.link(pool, nc.gpsimd.memset(rowb[0:1, 2, :], 1.0))
            st.link(pool, nc.gpsimd.memset(top[:, HEADS * TPB:], 0.0))

            def linked(st, ins):
                st.link(pool, ins)
                pool.sem_inc(s_poolstep, 1)

            def split(b, first):
                for n in range(2):
                    st = Steps(s_split, b * 10 + n * 5)
                    a, c = rope
                    hi, mid, lo = (parts[n][:, m, :] for m in range(3))
                    pool.wait_ge(s_rope, b * 2 + n + 1)
                    if not first:
                        pool.wait_ge(s_pst, b * 32 + 16 * (n - 1))
                    pool.sem_inc(s_poolstep, 1)
                    linked(st, nc.gpsimd.tensor_tensor(a[:], a[:], c[:], ALU.add))
                    linked(st, nc.gpsimd.tensor_copy(hi, a[:]))
                    linked(st, nc.gpsimd.tensor_tensor(c[:], a[:], hi, ALU.subtract))
                    linked(st, nc.gpsimd.tensor_copy(mid, c[:]))
                    st.up(nc.gpsimd.tensor_tensor(lo, c[:], mid, ALU.subtract))

            split(0, True)
            with pool.Fori(1, BATCH) as b:
                split(b, False)

        @block.scalar
        def _(act):
            def consume(u, use, b):
                kind = use[0]
                if kind not in ("turn", "v", "heads"):
                    return
                for c in range(2):
                    half = work[:, c * HALF:(c + 1) * HALF]
                    act.wait_ge(s_ready, u * 2 + (c + 1))
                    if kind == "v":
                        i = slice(c * TPB // 2, (c + 1) * TPB // 2)
                        ins = nc.scalar.activation(va[b][:, i, :, 0:HD],
                                                   half.rearrange("p (i h d) -> p i h d", h=HEADS, d=HD), ACT.Copy)
                    else:
                        dst = xt if kind == "turn" else aot
                        ins = nc.scalar.activation(dst[:, c * HALF:(c + 1) * HALF], half, ACT.Copy)
                    ins.then_inc(s_free[c], 1)

            def copy_out(n, used, split):
                act.wait_ge(s_pv, n * (SLOTS // 2) + SLOTS // 2)
                if used is not None:
                    act.wait_ge(s_ready, used)
                if split is not None:
                    act.wait_ge(s_split, split)
                nc.scalar.activation(ot[:, 0:HALF], acc[:, 0:HALF], ACT.Copy).then_inc(s_oa, 1)

            def main(b, k, base, plan, prev, more):
                u = base
                outs = {use[1]: n for n, use in enumerate(x for a, c in plan for x in a + c) if use[0] == "out"}
                for s in range(SLOTS):
                    n = b * SLOTS + s
                    act.wait_ge(s_score, n + 1)
                    if prev or s >= RING:
                        act.wait_ge(s_pv, n - RING + 1)
                    nc.scalar.activation(pt[:, s % RING, :], score[s % 2][:], ACT.Exp, scale=HD ** -0.5).then_inc(s_exp, 1)
                    if s == 0 and prev:
                        copy_out(b * 2 - 1, None, b * 10 + (20 if more else 10))
                    if s == SLOTS // 2:
                        copy_out(b * 2, (base + outs[1]) * 2 + 2 if prev else None, None if prev else 20)
                    for use in plan[s][0] + plan[s][1]:
                        consume(u, use, 1 - k if use[0] == "v" else None)
                        u = u + 1

            for n, (use, b) in enumerate(START):
                consume(n, use, b)
            rows(main, act)
            copy_out(LAST * 2 + 1, None, None)
            for n, use in enumerate(TAIL):
                consume(TAIL_BASE + n, use, None)

        @block.vector
        def _(dve):
            def norm(b):
                for j in range(TPB):
                    tile = b * TPB + j
                    ins = nc.vector.tensor_scalar(xn[:, j, :], g.h[:, bass.ds(tile, 1), :].rearrange("p o d -> p (o d)"),
                                                  g.mean[:, bass.ds(tile, 1)],
                                                  g.rstd[:, bass.ds(tile, 1)], ALU.subtract, ALU.mult)
                ins.then_inc(s_xn, 1)

            def consume(u, use, r, reused):
                kind = use[0]
                if kind in ("turn", "v", "heads"):
                    return
                if kind == "tops":
                    dve.wait_ge(s_free[0], u)
                    dve.wait_ge(s_free[1], u)
                    nc.vector.tensor_tensor(top[:, 0:HEADS * TPB], tops[:, 0, :], tops[:, 1, :],
                                            ALU.max).then_inc(s_top, 1)
                    st = Steps(s_neg, r * 4)
                    dve.wait_ge(s_ready, u * 2 + 2)
                    if reused:
                        dve.wait_ge(s_mst, r * 16)
                    nc.vector.tensor_scalar(neg[:], work[0:HEADS * TPB, 0:P], -1.0, None,
                                            ALU.mult).then_inc(s_free[0], 1)
                    dve.wait_ge(s_free[0], u + 1)
                    dve.sem_inc(s_free[1], 1)
                    st.link(dve, nc.vector.tensor_copy(negp[:, 0, :], neg[:]))
                    st.link(dve, nc.vector.tensor_tensor(neg[:], neg[:], negp[:, 0, :], ALU.subtract))
                    st.link(dve, nc.vector.tensor_copy(negp[:, 1, :], neg[:]))
                    st.up(nc.vector.tensor_tensor(negp[:, 2, :], neg[:], negp[:, 1, :], ALU.subtract))
                    return
                if kind == "q":
                    n, m = divmod(use[1], 2)
                    if m == 0 and (reused or n):
                        dve.wait_ge(s_split, r * 10 + n * 5)
                for c in range(2):
                    cols = slice(c * HALF, (c + 1) * HALF)
                    dve.wait_ge(s_ready, u * 2 + (c + 1))
                    if kind == "q":
                        ins = nc.vector.scalar_tensor_tensor(out=rope[m][:, cols], in0=work[:, cols],
                                                             scalar=bqk[:, use[1]:use[1] + 1],
                                                             in1=(cos, sin)[m][:, cols], op0=ALU.add, op1=ALU.mult)
                    elif kind == "max":
                        col = use[1] * TPB + use[2]
                        ins = nc.vector.tensor_reduce(tops[:, c, col:col + 1], work[:, cols], AX_X, ALU.max)
                    elif kind == "out":
                        quad, n = use[1], r * 2 + use[1]
                        i = slice(c * TPB // 2, (c + 1) * TPB // 2)
                        w = work[:, cols].rearrange("p (i h c) -> p i h c", h=QUAD, c=32)
                        nc.vector.reciprocal(inv[:, i, :], w[:, :, :, HD]).then_inc(s_ao, 1)
                        dve.wait_ge(s_ao, n * 3 + (c + 1))
                        view = ao[:, i, quad * QUAD * HD:(quad + 1) * QUAD * HD].rearrange("p i (h d) -> p i h d", d=HD)
                        ins = nc.vector.tensor_tensor(view, w[:, :, :, 0:HD],
                                                      inv[:, i, :].to_broadcast([P, TPB // 2, QUAD, HD]), ALU.mult)
                    elif kind == "proj":
                        tiles = g.h[:, bass.ds(r * TPB + c * (TPB // 2), TPB // 2), :].rearrange("p i d -> p (i d)")
                        ins = nc.vector.tensor_tensor(tiles, tiles, work[:, cols], ALU.add)
                    ins.then_inc(s_free[c], 1)
                if kind in ("q", "out", "proj") and use != ("q", 0) and use != ("q", 2):
                    dve.wait_ge(s_free[0], u + 1)
                    dve.wait_ge(s_free[1], u + 1)
                    if kind == "q":
                        dve.sem_inc(s_rope, 1)
                    elif kind == "out":
                        dve.sem_inc(s_ao, 1)
                    else:
                        for j in range(TPB):
                            tile = r * TPB + j
                            nc.vector.bn_stats(g.stat[:, bass.ds(tile, 1), :], g.h[:, bass.ds(tile, 1), :])

            def copy_out(n, used, split):
                dve.wait_ge(s_pv, n * (SLOTS // 2) + SLOTS // 2)
                if used is not None:
                    dve.wait_ge(s_ready, used)
                if split is not None:
                    dve.wait_ge(s_split, split)
                nc.vector.tensor_copy(ot[:, HALF:SEQ], acc[:, HALF:SEQ]).then_inc(s_od, 1)

            def main(b, k, base, plan, prev, more):
                u = base
                outs = {use[1]: n for n, use in enumerate(x for a, c in plan for x in a + c) if use[0] == "out"}
                for s in range(SLOTS):
                    if s == 0 and prev:
                        copy_out(b * 2 - 1, None, b * 10 + (20 if more else 10))
                    if s == SLOTS // 2:
                        copy_out(b * 2, (base + outs[1]) * 2 + 2 if prev else None, None if prev else 20)
                    for use in plan[s][0] + plan[s][1]:
                        consume(u, use, row_of(use, b), True)
                        u = u + 1
                    if s == NORM_SLOT and more == 2:
                        norm(b + 2)

            dve.wait_ge(s_load, 7 * 16)
            dve.wait_ge(s_vb, 1)
            nc.vector.tensor_tensor(rowb[0:1, 1, :], rowb[0:1, 0, :], work[0:1, 0:DM], ALU.add).then_inc(s_bias, 1)
            norm(0)
            for n, (use, r) in enumerate(START):
                if (use, r) == (("turn",), 1):
                    dve.wait_ge(s_split, 10)
                    norm(1)
                consume(n, use, r, r > 0)
            rows(main, dve)
            copy_out(LAST * 2 + 1, None, None)
            for n, use in enumerate(TAIL):
                consume(TAIL_BASE + n, use, LAST, True)

        @block.tensor
        def _(pe):
            def produce(u, use, r, k, first=False, halves=(0, 1)):
                kind = use[0]
                if kind == "turn":
                    pe.wait_ge(s_xn, r + 1)
                elif kind == "max" and use[1:] == (0, 0) and 0 in halves:
                    pe.wait_ge(s_stack, r * 192 + 192)
                elif kind == "tops":
                    pe.wait_ge(s_top, r + 1)
                    pe.wait_ge(s_free[0], u)
                    nc.tensor.transpose(work[:, 0:P], top[:], g.ident[:]).then_inc(s_ready, 2)
                    return
                elif kind == "heads":
                    pe.wait_ge(s_ao, r * 6 + 6)
                for c in halves:
                    if kind == "out":
                        pe.wait_ge((s_oa, s_od)[c], r * 2 + (use[1] + 1))
                    if not first:
                        pe.wait_ge(s_free[c], u)
                    cols = slice(c * HALF, (c + 1) * HALF)
                    if kind == "q":
                        ins = nc.tensor.matmul(work[:, cols], wqkv[:, use[1], :], xt[:, cols], start=True, stop=True)
                    elif kind == "max":
                        ins = nc.tensor.matmul(work[:, cols], qs[k][0:KQ, use[1], use[2] * P:(use[2] + 1) * P],
                                               ks[k][0:KQ, use[1], cols], start=True, stop=True)
                    else:
                        for j in range(c * TPB // 2, (c + 1) * TPB // 2):
                            o, x = work[:, j * P:(j + 1) * P], slice(j * P, (j + 1) * P)
                            if kind == "turn":
                                ins = nc.tensor.transpose(o, xn[:, j, :], g.ident[:])
                            elif kind == "out":
                                ins = nc.tensor.transpose(o, ot[:, x], g.ident[:])
                            elif kind == "heads":
                                ins = nc.tensor.transpose(o, ao[:, j, :], g.ident[:])
                            elif kind == "v":
                                ins = nc.tensor.matmul(o, xt[:, x], wqkv[:, 4, :], start=True, stop=True)
                            else:
                                nc.tensor.matmul(o, aot[:, x], wproj[:], start=True, stop=False)
                                ins = nc.tensor.matmul(o, rowb[0:1, 2, :], rowb[0:1, 1, :], start=False, stop=True)
                    ins.then_inc(s_ready, 1)

            def scores(b, k, s, c, reused):
                quad, i, hq = place(s)
                h = quad * QUAD + hq
                if c == 0:
                    if s == 0:
                        pe.wait_ge(s_mld, b * 16 + 16)
                    if reused:
                        pe.wait_ge(s_exp, b * SLOTS + s - 1)
                ins = nc.tensor.matmul(score[s % 2][:, c * HALF:(c + 1) * HALF], ks[k][:, h, i * P:(i + 1) * P],
                                       qs[k][:, h, c * HALF:(c + 1) * HALF], start=True, stop=True)
                if c:
                    ins.then_inc(s_score, 1)

            def values(b, k, s, c):
                quad, i, hq = place(s)
                h = quad * QUAD + hq
                ins = nc.tensor.matmul(acc[32 * hq:32 * hq + 32, c * HALF:(c + 1) * HALF], va[k][:, i, h, :],
                                       pt[:, s % RING, c * HALF:(c + 1) * HALF], start=(i == 0), stop=(i == TPB - 1),
                                       tile_position=(0, 32 * hq))
                if c == 1:
                    ins.then_inc(s_pv, 1)

            def main(b, k, base, plan, prev, more):
                u = base
                for s in range(SLOTS):
                    for use in plan[s][0]:
                        produce(u, use, row_of(use, b), 1 - k)
                        u = u + 1
                    fill = [(n // 2, use, n % 2) for n, use in enumerate(x for x in plan[s][1] for c in range(2))]
                    gaps = [fill[0:1], fill[1:2], fill[2:3], fill[3:4]] if len(fill) == 4 else [[], fill[0:1], [], fill[1:2]]

                    def among(n):
                        for m, use, c in gaps[n]:
                            produce(u + m, use, row_of(use, b), 1 - k, halves=(c,))

                    for c in range(2):
                        among(c)
                        if s + 1 < SLOTS:
                            scores(b, k, s + 1, c, prev or s >= 1)
                        elif more:
                            scores(b + 1, 1 - k, 0, c, True)
                    among(2)
                    pe.wait_ge(s_exp, b * SLOTS + s + 1)
                    if s % (SLOTS // 2) == 0 and (prev or s):
                        n = b * 2 + s // (SLOTS // 2)
                        pe.wait_ge(s_oa, n)
                        pe.wait_ge(s_od, n)
                    values(b, k, s, 0)
                    among(3)
                    values(b, k, s, 1)
                    u = u + len(plan[s][1])

            pe.wait_ge(s_load, 7 * 16)
            pe.wait_ge(s_ones, 6)
            nc.tensor.matmul(work[0:1, 0:DM], vb[:], wproj[:], start=True, stop=True).then_inc(s_vb, 1)
            pe.wait_ge(s_bias, 1)
            for n, (use, r) in enumerate(START):
                produce(n, use, r, r, n == 0)
            for c in range(2):
                scores(0, 0, 0, c, False)
            rows(main, pe)
            for n, use in enumerate(TAIL):
                produce(TAIL_BASE + n, use, LAST, None)


EXPERTS, FF = 8, 512
FT = FF // P
CAP = -(-5 * 32 * 256 // (4 * EXPERTS))
BANKS = 2
GE = BANKS * EXPERTS
CH = 4
CW = CH * P
CHUNKS = TILES // CH
SPILL = float(2 * GE * CAP)


def route_phase(nc, g, w_router, b_router, w1, b1, w2, b2, upto, slots_x):
    with ExitStack() as ctx:
        sb = lambda name, shape, dt=F32: ctx.enter_context(nc.sbuf_tensor("r_" + name, shape, dt))
        ps = lambda name, shape, dt=F32: ctx.enter_context(nc.psum_tensor("r_" + name, shape, dt))
        sem = lambda name: ctx.enter_context(nc.semaphore("r_" + name))
        RING = 4
        wr = sb("wr", [P, GE])
        rows = sb("rows", [1, GE + DM + P])
        up_w = sb("up_w", [P, FF])
        up_b = sb("up_b", [P, FT])
        down_w = sb("down_w", [P, FT, DM])
        tri_f = sb("tri_f", [P, P])
        tri = sb("tri", [P, P], BF16)
        ones = sb("ones", [P, P], BF16)
        order = sb("order", [P, CH, BANKS, EXPERTS])
        shift = sb("shift", [P, CH, BANKS])
        xn = sb("xn", [P, RING, CH, DM])
        xt = sb("xt", [P, 2, CW])
        hid = sb("hid", [P, FT, CW])
        hot = sb("hot", [P, 2, CH, GE], BF16)
        seen = sb("seen", [P, GE])
        seen_b = sb("seen_b", [P, 2, GE], BF16)
        added = sb("added", [P, GE])
        shifted = sb("shifted", [P, TILES, GE])
        keep_ = sb("keep", [P, TILES, BANKS])
        top = sb("top", [P, CH * BANKS])
        rank = sb("rank", [P, CH * BANKS])
        flag = sb("flag", [P, CH * GE])
        place_f = sb("place_f", [P, CH * BANKS])
        drop = sb("drop", [P, CH * BANKS])
        slot_f = sb("slot_f", [P, CH * BANKS])
        slots = sb("slots", [P, RING, CH * BANKS], U32)
        turned = ps("turned", [P, CW])
        logit = ps("logit", [P, CW])
        counts = ps("counts", [P, CW])
        ups = [ps(f"up{f}", [P, CW]) for f in range(FT)]
        down = ps("down", [P, CW])

        s_load = sem("weights_loaded")
        s_const = sem("constants_set")
        s_xn = sem("norm_applied")
        s_turn = sem("rows_turned")
        s_xt = sem("rows_t_ready")
        s_logit = sem("logits_ready")
        s_r = sem("routing_steps")
        s_s = sem("slot_steps")
        s_tri = sem("triangle_ready")
        s_exp = sem("exp_done")
        s_hot = sem("choice_ready")
        s_count = sem("counts_ready")
        s_slots = sem("slots_ready")
        s_scat = [sem(f"rows_scattered{i}") for i in range(RING)]
        s_up = sem("up_done")
        s_gelu = sem("gelu_done")
        s_down = sem("down_done")
        s_h = sem("h_updated")
        s_pool = sem("pool_step")
        block = ctx.enter_context(nc.Block())
        SCATTERS = CH * BANKS * 16

        def chunks(body, eng):
            for c in range(RING):
                body(c, c, c, True)
            with eng.Fori(1, CHUNKS // RING - 1) as i:
                for q in range(RING):
                    body(i * RING + q, q, RING, True)
            for q in range(RING):
                body(CHUNKS - RING + q, q, RING, q + 1 < RING)

        R2 = 10

        @block.sync
        def _(sp):
            for dst, src in ((wr[:], w_router), (rows[0:1, 0:GE], b_router), (rows[0:1, GE:GE + DM], b2),
                             (up_w[:], w1), (up_b[:], b1), (down_w[:], w2), (tri_f[:], upto)):
                sp.dma_start(dst, src).then_inc(s_load, 16)

        @block.gpsimd
        def _(pool):
            st = Steps(s_const)
            st.link(pool, nc.gpsimd.memset(ones[:], 1.0))
            st.link(pool, nc.gpsimd.memset(rows[0:1, GE + DM:], 1.0))
            st.link(pool, nc.gpsimd.memset(seen[:], 0.0))
            st.link(pool, nc.gpsimd.memset(seen_b[:], 0.0))
            for e in range(EXPERTS):
                st.link(pool, nc.gpsimd.memset(order[:, :, :, e:e + 1], float(EXPERTS - e)))
            for n in range(BANKS):
                st.link(pool, nc.gpsimd.memset(shift[:, :, n:n + 1], float(n * EXPERTS * CAP - 1)))

            def scatter(c, q):
                pool.wait_ge(s_slots, c + 1)
                pool.sem_inc(s_pool, 1)
                for j in range(CH):
                    for n in range(BANKS):
                        col = j * BANKS + n
                        nc.gpsimd.indirect_dma_start(
                            slots_x, bass.IndirectOffsetOnAxis(ap=slots[:, q, col:col + 1], axis=0), xn[:, q, j, :], None,
                            bounds_check=GE * CAP - 1, oob_is_err=False).then_inc(s_scat[q], 16)

            with pool.Fori(0, CHUNKS // RING) as i:
                for q in range(RING):
                    scatter(i * RING + q, q)
            for q in range(RING):
                pool.wait_ge(s_scat[q], CHUNKS // RING * SCATTERS)

        @block.scalar
        def _(act):
            def copy_t(c, k, reused):
                act.wait_ge(s_turn, c + 1)
                if reused:
                    act.wait_ge(s_logit, c - 1)
                    act.wait_ge(s_up, (c - 1) * FT)
                nc.scalar.activation(xt[:, k, :], turned[:], ACT.Copy).then_inc(s_xt, 1)

            def gelu(c, reused):
                for f in range(FT):
                    act.wait_ge(s_up, c * FT + f + 1)
                    if reused and f == 0:
                        act.wait_ge(s_down, c)
                    nc.scalar.activation(hid[:, f, :], ups[f][:], ACT.Gelu, bias=up_b[:, f:f + 1]).then_inc(s_gelu, 1)

            act.wait_ge(s_load, 7 * 16)

            def step(c, q, before, more):
                copy_t(c, q % 2, before >= 2)
                gelu(c, before >= 1)

            chunks(step, act)
            act.wait_ge(s_hot, CHUNKS)
            nc.scalar.activation(shifted[:], shifted[:], ACT.Exp).then_inc(s_exp, 1)

        @block.vector
        def _(dve):
            def norm(c, q, reused):
                if reused:
                    dve.wait_ge(s_scat[q], (c - q) * (SCATTERS // RING))
                    dve.wait_ge(s_turn, c - (RING - 1))
                for j in range(CH):
                    tile = c * CH + j
                    ins = nc.vector.tensor_scalar(xn[:, q, j, :],
                                                  g.h[:, bass.ds(tile, 1), :].rearrange("p o d -> p (o d)"),
                                                  g.mean[:, bass.ds(tile, 1)], g.rstd[:, bass.ds(tile, 1)],
                                                  ALU.subtract, ALU.mult)
                ins.then_inc(s_xn, 1)

            GROUP = [P, CH * BANKS, EXPERTS]
            groups = lambda ap: ap.rearrange("p (u e) -> p u e", e=EXPERTS)
            R1 = 4

            def choose(c, k, reused):
                st = Steps(s_r, c * R1)
                lg = logit[:, 0:CH * GE].rearrange("p (u e) -> p u e", e=EXPERTS)
                dve.wait_ge(s_logit, c + 1)
                st.link(dve, nc.vector.tensor_reduce(top[:], lg, AX_X, ALU.max))
                d = shifted[:, bass.ds(c * CH, CH), :].rearrange("p c (b e) -> p (c b) e", e=EXPERTS)
                st.link(dve, nc.vector.tensor_tensor(d, lg, top[:].to_broadcast(GROUP), ALU.subtract))
                st.link(dve, nc.vector.scalar_tensor_tensor(out=groups(flag[:]), in0=d, scalar=0.0,
                                                            in1=order[:].rearrange("p c b e -> p (c b) e"),
                                                            op0=ALU.is_ge, op1=ALU.mult))
                st.link(dve, nc.vector.tensor_reduce(rank[:], groups(flag[:]), AX_X, ALU.max))
                if reused:
                    dve.wait_ge(s_count, c - 1)
                nc.vector.tensor_tensor(hot[:, k].rearrange("p c (b e) -> p (c b) e", e=EXPERTS),
                                        order[:].rearrange("p c b e -> p (c b) e"), rank[:].to_broadcast(GROUP),
                                        ALU.is_equal).then_inc(s_hot, 1)

            def slot(c, q, reused):
                k = q % 2
                st = Steps(s_s, c * R2)
                cnt = counts[:, 0:CH * GE]
                dve.wait_ge(s_count, c + 1)
                dve.wait_ge(s_hot, c + 1)
                h = hot[:, k].rearrange("p c e -> p (c e)")
                st.link(dve, nc.vector.tensor_tensor(flag[:], cnt, h, ALU.mult))
                st.link(dve, nc.vector.tensor_reduce(place_f[:], groups(flag[:]), AX_X, ALU.add))
                st.link(dve, nc.vector.tensor_reduce(added[:], hot[:, k].rearrange("p c e -> p e c"), AX_X, ALU.add))
                st.link(dve, nc.vector.tensor_tensor(seen[:], seen[:], added[:], ALU.add))
                st.link(dve, nc.vector.tensor_copy(seen_b[:, 1 - k, :], seen[:]))
                keep = keep_[:, bass.ds(c * CH, CH), :].rearrange("p c b -> p (c b)")
                st.link(dve, nc.vector.tensor_scalar(keep, place_f[:], float(CAP), None, ALU.is_le))
                st.link(dve, nc.vector.tensor_scalar(drop[:], place_f[:], float(CAP), SPILL, ALU.is_gt, ALU.mult))
                st.link(dve, nc.vector.tensor_scalar(slot_f[:], rank[:], -float(CAP), float(EXPERTS * CAP), ALU.mult,
                                                     ALU.add))
                st.link(dve, nc.vector.scalar_tensor_tensor(out=place_f[:], in0=place_f[:], scalar=float(CAP),
                                                            in1=slot_f[:], op0=ALU.min, op1=ALU.add))
                st.link(dve, nc.vector.tensor_tensor(place_f[:], place_f[:], shift[:].rearrange("p c b -> p (c b)"),
                                                     ALU.add))
                nc.vector.tensor_copy(g.slot[:, bass.ds(c * CH, CH), :].rearrange("p c b -> p (c b)"), place_f[:])
                if reused:
                    dve.wait_ge(s_scat[q], (c - q) * (SCATTERS // RING))
                nc.vector.tensor_tensor(slots[:, q, :], place_f[:], drop[:], ALU.add).then_inc(s_slots, 1)

            def add(c):
                dve.wait_ge(s_down, c + 1)
                tiles = g.h[:, bass.ds(c * CH, CH), :].rearrange("p i d -> p (i d)")
                nc.vector.tensor_tensor(tiles, tiles, down[:], ALU.add).then_inc(s_h, 1)

            dve.wait_ge(s_load, 7 * 16)
            dve.wait_ge(s_const, 4 + EXPERTS + BANKS)
            st0 = Steps(s_tri)
            st0.up(nc.vector.tensor_copy(tri[:], tri_f[:]))
            norm(0, 0, False)

            def step(c, q, before, more):
                if more:
                    norm(c + 1, (q + 1) % RING, before + 1 >= RING)
                choose(c, q % 2, before >= 2)
                slot(c, q, before >= RING)
                add(c)

            chunks(step, dve)
            st = Steps(s_s, CHUNKS * R2)
            dve.wait_ge(s_exp, 1)
            gate = g.gate[:].rearrange("p t b -> p (t b)")
            st.link(dve, nc.vector.tensor_reduce(gate, shifted[:].rearrange("p t (b e) -> p (t b) e", e=EXPERTS),
                                                 AX_X, ALU.add))
            st.link(dve, nc.vector.reciprocal(gate, gate))
            nc.vector.tensor_tensor(gate, gate, keep_[:].rearrange("p t b -> p (t b)"), ALU.mult)

        @block.tensor
        def _(pe):
            def turn(c, q, reused):
                pe.wait_ge(s_xn, c + 1)
                if reused:
                    pe.wait_ge(s_xt, c)
                for j in range(CH):
                    ins = nc.tensor.transpose(turned[:, j * P:(j + 1) * P], xn[:, q, j, :], g.ident[:])
                ins.then_inc(s_turn, 1)

            def router(c, k, reused):
                pe.wait_ge(s_xt, c + 1)
                if reused:
                    pe.wait_ge(s_hot, c)
                for j in range(CH):
                    o = logit[:, j * GE:(j + 1) * GE]
                    nc.tensor.matmul(o, xt[:, k, j * P:(j + 1) * P], wr[:], start=True, stop=False)
                    ins = nc.tensor.matmul(o, rows[0:1, GE + DM:], rows[0:1, 0:GE], start=False, stop=True)
                ins.then_inc(s_logit, 1)

            def up(c, k, reused):
                for f in range(FT):
                    if reused:
                        pe.wait_ge(s_gelu, (c - 1) * FT + f + 1)
                    nc.tensor.matmul(ups[f][:], up_w[:, f * P:(f + 1) * P], xt[:, k, :], start=True,
                                     stop=True).then_inc(s_up, 1)

            def count(c, k, reused):
                pe.wait_ge(s_hot, c + 1)
                if reused:
                    pe.wait_ge(s_s, c * R2)
                for j in range(CH):
                    o = counts[:, j * GE:(j + 1) * GE]
                    nc.tensor.matmul(o, ones[:], seen_b[:, k, :], start=True, stop=False)
                    for before in range(j):
                        nc.tensor.matmul(o, ones[:], hot[:, k, before, :], start=False, stop=False)
                    ins = nc.tensor.matmul(o, tri[:], hot[:, k, j, :], start=False, stop=True)
                ins.then_inc(s_count, 1)

            def down_(c, reused):
                if reused:
                    pe.wait_ge(s_h, c)
                pe.wait_ge(s_gelu, c * FT + FT)
                for j in range(CH):
                    o = down[:, j * P:(j + 1) * P]
                    for f in range(FT):
                        nc.tensor.matmul(o, hid[:, f, j * P:(j + 1) * P], down_w[:, f, :], start=(f == 0), stop=False)
                    ins = nc.tensor.matmul(o, rows[0:1, GE + DM:], rows[0:1, GE:GE + DM], start=False, stop=True)
                ins.then_inc(s_down, 1)

            pe.wait_ge(s_load, 7 * 16)
            pe.wait_ge(s_const, 4 + EXPERTS + BANKS)
            pe.wait_ge(s_tri, 1)
            turn(0, 0, False)
            router(0, 0, False)

            def step(c, q, before, more):
                k = q % 2
                up(c, k, before >= 1)
                if more:
                    turn(c + 1, (q + 1) % RING, True)
                count(c, k, before >= 1)
                if more:
                    router(c + 1, 1 - k, True)
                down_(c, before >= 1)

            chunks(step, pe)


def experts_phase(nc, g, slots_x, slots_y, w1, b1, w2, b2):
    with ExitStack() as ctx:
        sb = lambda name, shape, dt=F32: ctx.enter_context(nc.sbuf_tensor("x_" + name, shape, dt))
        ps = lambda name, shape, dt=F32: ctx.enter_context(nc.psum_tensor("x_" + name, shape, dt))
        sem = lambda name: ctx.enter_context(nc.semaphore("x_" + name))
        ET = CAP // P
        PARTS = [(t, min(CH, ET - t)) for t in range(0, ET, CH)]
        NP = len(PARTS)
        rows = sb("rows", [P, 2, ET, DM])
        outs = sb("outs", [P, 2, ET, DM])
        w_up = sb("w_up", [P, 2, FF])
        w_down = sb("w_down", [P, 2, FT, DM])
        b_down = sb("b_down", [1, 2, DM])
        b_cur = sb("b_cur", [P, 2, FT])
        ones = sb("ones", [1, P])
        xt = sb("xt", [P, 2, CW])
        hid = sb("hid", [P, FT, CW])
        turned = ps("turned", [P, CW])
        ups = [ps(f"up{f}", [P, CW]) for f in range(FT)]
        down = [ps(f"down{n}", [P, CW]) for n in range(2)]
        s_ones = sem("ones_set")
        s_in = [sem(f"expert_loaded{k}") for k in range(2)]
        s_turn = sem("rows_turned")
        s_xt = sem("rows_t_ready")
        s_up = sem("up_done")
        s_gelu = sem("gelu_done")
        s_down = sem("down_done")
        s_o = sem("outputs_ready")
        s_out = [sem(f"outputs_stored{k}") for k in range(2)]
        block = ctx.enter_context(nc.Block())
        PAIRS = GE // 2
        LOADS = 5 * 16

        def slot_rows(t, e):
            return t[bass.ds(e * CAP, CAP), :].rearrange("(j p) d -> p j d", p=P)

        @block.sync
        def _(sp):
            def load(e, k):
                sp.dma_start(rows[:, k], slot_rows(slots_x, e)).then_inc(s_in[k], 16)
                sp.dma_start(w_up[:, k, :], w1[bass.ds(e, 1), :, :].rearrange("o d f -> d (o f)")).then_inc(s_in[k], 16)
                sp.dma_start(w_down[:, k], w2[bass.ds(e, 1), :, :].rearrange("o (t f) d -> f (o t) d", f=P)).then_inc(s_in[k], 16)
                sp.dma_start(b_down[0:1, k, :], b2[bass.ds(e, 1), :]).then_inc(s_in[k], 16)
                sp.dma_start(b_cur[:, k, :], b1[bass.ds(e, 1), :, :].rearrange("o p t -> p (o t)")).then_inc(s_in[k], 16)

            def store(e, k):
                sp.wait_ge(s_o, (e + 1) * NP)
                sp.dma_start(slot_rows(slots_y, e), outs[:, k]).then_inc(s_out[k], 16)

            load(0, 0)
            load(1, 1)
            with sp.Fori(0, PAIRS - 1) as i:
                for k in range(2):
                    store(i * 2 + k, k)
                    sp.wait_ge(s_down, (i * 2 + (k + 1)) * NP)
                    load(i * 2 + (k + 2), k)
            for k in range(2):
                store(GE - 2 + k, k)
            for k in range(2):
                sp.wait_ge(s_out[k], PAIRS * 16)

        @block.gpsimd
        def _(pool):
            nc.gpsimd.memset(ones[:], 1.0).then_inc(s_ones, 1)

        def passes(body, eng):
            for e in range(2):
                for c in range(NP):
                    body(e * NP + c, e, c, e, True)
            with eng.Fori(1, PAIRS) as i:
                for k in range(2):
                    for c in range(NP):
                        body(i * (2 * NP) + (k * NP + c), k, c, i * 2 + k, False)

        @block.scalar
        def _(act):
            def gelu(n, k, c, e, first):
                width = PARTS[c][1] * P
                if c == 0:
                    act.wait_ge(s_in[k], ((e - k) * 8 if not first else 0) * 5 + LOADS)
                for f in range(FT):
                    act.wait_ge(s_up, n * FT + f + 1)
                    if f == 0 and not (first and k == 0 and c == 0):
                        act.wait_ge(s_down, n)
                    nc.scalar.activation(hid[:, f, 0:width], ups[f][:, 0:width], ACT.Gelu,
                                         bias=b_cur[:, k, f:f + 1]).then_inc(s_gelu, 1)

            passes(gelu, act)

        @block.vector
        def _(dve):
            def copies(n, k, c, e, first):
                t, m = PARTS[c]
                dve.wait_ge(s_turn, n + 1)
                if not (first and k == 0 and c < 2):
                    dve.wait_ge(s_up, (n - 1) * FT)
                nc.vector.tensor_copy(xt[:, (k * NP + c) % 2, 0:m * P], turned[:, 0:m * P]).then_inc(s_xt, 1)
                if not (first and k == 0 and c == 0):
                    out(n - 1, (k if c else 1 - k), (c - 1) % NP, (e if c else e - 1), first)

            def out(n, k, c, e, first):
                t, m = PARTS[c]
                dve.wait_ge(s_down, n + 1)
                if c == 0 and not first:
                    dve.wait_ge(s_out[k], (e - k) * 8)
                nc.vector.tensor_copy(outs[:, k, t:t + m, :].rearrange("p j d -> p (j d)"),
                                      down[(k * NP + c) % 2][:, 0:m * P]).then_inc(s_o, 1)

            passes(copies, dve)
            out(GE * NP - 1, 1, NP - 1, GE - 1, False)

        @block.tensor
        def _(pe):
            pe.wait_ge(s_ones, 1)

            def turn(n, k, c, e, first):
                t, m = PARTS[c]
                if c == 0:
                    pe.wait_ge(s_in[k], ((e - k) * 8 if not first else 0) * 5 + LOADS)
                if not (first and k == 0 and c == 0):
                    pe.wait_ge(s_xt, n)
                for j in range(m):
                    ins = nc.tensor.transpose(turned[:, j * P:(j + 1) * P], rows[:, k, t + j, :], g.ident[:])
                ins.then_inc(s_turn, 1)

            def work(n, k, c, e, first):
                t, m = PARTS[c]
                begins = first and k == 0 and c == 0
                pe.wait_ge(s_xt, n + 1)
                for f in range(FT):
                    if not begins:
                        pe.wait_ge(s_gelu, (n - 1) * FT + f + 1)
                    nc.tensor.matmul(ups[f][:, 0:m * P], w_up[:, k, f * P:(f + 1) * P], xt[:, (k * NP + c) % 2, 0:m * P],
                                     start=True, stop=True).then_inc(s_up, 1)

            def down_(n, k, c, e, first):
                t, m = PARTS[c]
                if not (first and k == 0 and c < 2):
                    pe.wait_ge(s_o, n - 1)
                pe.wait_ge(s_gelu, n * FT + FT)
                for j in range(m):
                    o = down[(k * NP + c) % 2][:, j * P:(j + 1) * P]
                    for f in range(FT):
                        nc.tensor.matmul(o, hid[:, f, j * P:(j + 1) * P], w_down[:, k, f, :], start=(f == 0), stop=False)
                    ins = nc.tensor.matmul(o, ones[:], b_down[0:1, k, :], start=False, stop=True)
                ins.then_inc(s_down, 1)

            def step(n, k, c, e, first):
                work(n, k, c, e, first)
                nk, nn = (k, c + 1) if c + 1 < NP else (1 - k, 0)
                ne = e if nk == k else e + 1
                turn(n + 1, nk, nn, ne, first and not (k == 1 and c == NP - 1))
                down_(n, k, c, e, first)

            turn(0, 0, 0, 0, True)
            for k in range(2):
                for c in range(NP):
                    step(k * NP + c, k, c, k, True)
            with pe.Fori(1, PAIRS - 1) as i:
                for k in range(2):
                    for c in range(NP):
                        step(i * (2 * NP) + (k * NP + c), k, c, i * 2 + k, False)
            for k in range(2):
                for c in range(NP):
                    n = (PAIRS - 1) * 2 * NP + k * NP + c
                    if (k, c) == (1, NP - 1):
                        work(n, k, c, GE - 1, False)
                        down_(n, k, c, GE - 1, False)
                    else:
                        step(n, k, c, GE - 2 + k, False)


def combine_phase(nc, g, slots_y, h_out):
    with ExitStack() as ctx:
        sb = lambda name, shape, dt=F32: ctx.enter_context(nc.sbuf_tensor("c_" + name, shape, dt))
        sem = lambda name: ctx.enter_context(nc.semaphore("c_" + name))
        SLOTS = 4
        cols = sb("cols", [P, 2, TPB * BANKS], U32)
        rows = sb("rows", [P, SLOTS, BANKS, DM])
        s_cols = sem("slot_columns_ready")
        s_rows = [sem(f"rows_gathered{i}") for i in range(SLOTS)]
        s_step = sem("vector_steps")
        s_pool = sem("pool_step")
        s_store = sem("h_stored")
        block = ctx.enter_context(nc.Block())
        PAIRS = BATCH // 2
        T2 = 2 * TPB
        PER = T2 // SLOTS * BANKS * 16

        @block.sync
        def _(sp):
            with sp.Fori(0, BATCH) as b:
                sp.wait_ge(s_step, (b + 1) * (TPB * BANKS))
                sp.dma_start(h_out[bass.ds(b * SEQ, SEQ), :].rearrange("(j p) d -> p j d", p=P),
                             g.h[:, bass.ds(b * TPB, TPB), :]).then_inc(s_store, 16)
            sp.wait_ge(s_store, BATCH * 16)

        @block.gpsimd
        def _(pool):
            def gather(i, j, reused):
                slot = j % SLOTS
                if j % TPB == 0:
                    pool.wait_ge(s_cols, i * 2 + (j // TPB + 1))
                if reused:
                    pool.wait_ge(s_step, (i * T2 + (j - SLOTS + 1)) * BANKS)
                pool.sem_inc(s_pool, 1)
                for n in range(BANKS):
                    c = (j % TPB) * BANKS + n
                    nc.gpsimd.indirect_dma_start(
                        rows[:, slot, n, :], None, slots_y,
                        bass.IndirectOffsetOnAxis(ap=cols[:, j // TPB, c:c + 1], axis=0)).then_inc(s_rows[slot], 16)

            for j in range(T2):
                gather(0, j, j >= SLOTS)
            with pool.Fori(1, PAIRS) as i:
                for j in range(T2):
                    gather(i, j, True)

        @block.vector
        def _(dve):
            def fill(pair, half):
                tile = pair * T2 + half * TPB
                nc.vector.tensor_copy(cols[:, half, :].rearrange("p (t b) -> p t b", b=BANKS),
                                      g.slot[:, bass.ds(tile, TPB), :]).then_inc(s_cols, 1)

            def tiles(i, more):
                for j in range(T2):
                    slot = j % SLOTS
                    tile = i * T2 + j
                    dve.wait_ge(s_rows[slot], i * PER + (j // SLOTS + 1) * BANKS * 16)
                    h = g.h[:, bass.ds(tile, 1), :].rearrange("p o d -> p (o d)")
                    for n in range(BANKS):
                        gate = g.gate[:, bass.ds(tile, 1), n]
                        nc.vector.scalar_tensor_tensor(out=h, in0=rows[:, slot, n, :], scalar=gate, in1=h,
                                                       op0=ALU.mult, op1=ALU.add).then_inc(s_step, 1)
                        dve.wait_ge(s_step, tile * BANKS + (n + 1))
                    nc.vector.bn_stats(g.stat[:, bass.ds(tile, 1), :], g.h[:, bass.ds(tile, 1), :])
                    if more and j % TPB == TPB - 1:
                        fill(i + 1, j // TPB)

            fill(0, 0)
            fill(0, 1)
            with dve.Fori(0, PAIRS - 1) as i:
                tiles(i, True)
            tiles(PAIRS - 1, False)


SCALES = 3
DI, ST, DTR, TAPS = 256, 16, 32, 4
DT2 = DI // P
UW = SEQ
HALF = 512
SERIES = 1e-4


def mamba_phase(nc, g, h_in, h_out, w):
    with ExitStack() as ctx:
        sb = lambda name, shape, dt=F32: ctx.enter_context(nc.sbuf_tensor("m_" + name, shape, dt))
        ps = lambda name, shape, dt=F32: ctx.enter_context(nc.psum_tensor("m_" + name, shape, dt))
        sem = lambda name: ctx.enter_context(nc.semaphore("m_" + name))
        LEN = [SEQ >> s for s in range(SCALES)]
        NS = [UW // t for t in LEN]
        UNITS = [ST // n for n in NS]
        FIRST_UNIT = [sum(UNITS[:s]) for s in range(SCALES)]
        NU = sum(UNITS)
        conv_w = sb("conv_w", [P, SCALES, TAPS, DI])
        z_w = sb("z_w", [P, SCALES, DI])
        xp_w = sb("xp_w", [P, SCALES, DT2, P])
        dt_w = sb("dt_w", [DTR, SCALES, DI])
        out_w = sb("out_w", [P, SCALES, DT2, DM])
        fus_w = sb("fus_w", [P, SCALES, DM])
        fus_b = sb("fus_b", [P, 1])
        cols = sb("cols", [P, 3, SCALES, DT2])
        decay = sb("decay", [P, SCALES, DT2, ST])
        ln_g = sb("ln_g", [P, DM])
        ln_b = sb("ln_b", [P, DM])
        pick_f = sb("pick_f", [P, 2 * ST])
        pick = sb("pick", [P, 2 * ST, P], BF16)
        power = sb("power", [P, TPB])
        hl = sb("hl", [P, 2, TPB, DM])
        xn = sb("xn", [P, 2, TPB, DM])
        xts = [sb(f"xts{s}", [P, TAPS - 1 + LEN[s]]) for s in range(SCALES)]
        xc = [[sb(f"xc{s}_{k}", [P, DT2, LEN[s]]) for k in range(2 if s == 0 else 1)] * (1 if s == 0 else 2)
              for s in range(SCALES)]
        sz = [[sb(f"sz{s}_{k}", [P, DT2, LEN[s]]) for k in range(2 if s == 0 else 1)] * (1 if s == 0 else 2)
              for s in range(SCALES)]
        dt_ = [sb(f"dt{s}", [P, DT2, LEN[s]]) for s in range(SCALES)]
        dtx = [sb(f"dtx{s}", [P, DT2, LEN[s]]) for s in range(SCALES)]
        bc_f = sb("bc_f", [P, SEQ])
        bc = [sb(f"bc{s}", [P, LEN[s]], BF16) for s in range(SCALES)]
        t_exp = sb("t_exp", [P, UW])
        t_relu = sb("t_relu", [P, UW])
        t_ln = sb("t_ln", [P, UW])
        t_one = sb("t_one", [P, UW])
        da = sb("da", [P, 2, DT2, UW])
        zero = sb("zero", [P, DT2, NS[-1]])
        hb = sb("hb", [P, 2, DT2, UW])
        o = [sb("o0", [P, SEQ])] + [sb(f"o{s}", [P, LEN[s] + 2]) for s in (1, 2)]
        oi = sb("oi", [P, SEQ])
        hh = sb("hh", [P, TPB, DM])
        st6 = sb("st6", [P, TPB, 6])
        st_d = sb("st_d", [P, TPB])
        st_m = sb("st_m", [P, TPB])
        st_v = sb("st_v", [P, TPB])
        work = ps("work", [P, UW])
        cps = ps("c", [P, UW])
        yps = ps("y", [P, DT2, UW])

        s_load = sem("weights_loaded")
        s_fold = sem("conv_folded")
        s_fus = sem("fusion_products")
        s_fused_w = sem("fusion_folded")
        s_const = sem("constants_set")
        s_prep = sem("setup_steps")
        s_hl = [sem(f"h_loaded{k}") for k in range(2)]
        s_hs = [sem(f"h_stored{k}") for k in range(2)]
        s_xn = sem("norm_applied")
        s_wr = sem("work_ready")
        s_wf = sem("work_free")
        s_c = sem("c_ready")
        s_g = sem("states_times_c")
        s_da = sem("decay_ready")
        s_scan = sem("scan_done")
        s_y = sem("states_summed")
        s_post = sem("gated")
        s_post1 = sem("skip_added")
        s_bc = sem("bc_copied")
        s_split = sem("bc_split")
        s_splits = sem("bc_split_steps")
        s_sp = sem("softplus_parts")
        s_act = sem("softplus_steps")
        s_dtx = sem("dtx_ready")
        s_dts = sem("dtx_steps")
        s_o = sem("out_copied")
        s_oi = sem("interpolated")
        s_ois = sem("interp_steps")
        s_hh = sem("fused")
        s_hst = sem("fused_stats")
        s_lns = sem("ln_steps")
        s_rs = sem("ln_rstd_ready")
        s_nm = sem("ln_applied")
        s_h3 = sem("h_ready")
        s_h3s = sem("h_steps")
        s_pool = sem("pool_step")
        block = ctx.enter_context(nc.Block())

        PARTS = [[[0], [1]]] + [[[0, 1]]] * (SCALES - 1)
        prep = lambda s: ([("xi", s, j) for j in range(DT2 * LEN[s] // HALF)] + [("xp", s)]
                          + [("dt", s, 0)] + [("z", s, p) for p in range(len(PARTS[s]))]
                          + [("dt", s, p) for p in range(1, len(PARTS[s]))])
        FIRST = [("turn",)] + prep(0)

        def plan(prev, nxt):
            at = {u: [] for u in range(NU)}
            if prev:
                at[2].append(("out", 2))
                at[5].append(("fuse",))
            for u, use in zip((1, 3, 4, 6, 7), prep(1)):
                at[u].append(use)
            for u, use in zip((8, 9, 11, 12), prep(2)):
                at[u].append(use)
            if nxt:
                for u, use in zip((13, 14, 15, 16, 17, 18, 19, 21, 22, 24), FIRST):
                    at[u].append(use)
            at[18].append(("out", 0))
            at[26].append(("out", 1))
            return at

        FULL = plan(True, True)
        N_FULL = NU + sum(map(len, FULL.values()))
        N_FIRST = NU + sum(map(len, plan(False, True).values()))
        N_LAST = NU + sum(map(len, plan(True, False).values()))
        LAST = BATCH - 1
        use_base = lambda b: len(FIRST) + N_FIRST + N_FULL * (b - 1)
        END = use_base(LAST) + N_LAST

        def scale_of(u):
            s = max(s for s in range(SCALES) if u >= FIRST_UNIT[s])
            return s, u - FIRST_UNIT[s]

        def batches(main, eng):
            main(0, 0, len(FIRST), plan(False, True), False, True)
            with eng.Fori(0, (BATCH - 2) // 2) as i:
                main(i * 2 + 1, 1, use_base(i * 2 + 1), FULL, True, True)
                main(i * 2 + 2, 0, use_base(i * 2 + 2), FULL, True, True)
            main(LAST, LAST % 2, use_base(LAST), plan(True, False), True, False)

        def row_of(use, b, u):
            if use in (("out", 2), ("fuse",)):
                return b - 1
            if use[0] == "turn" or (use[0] != "out" and use[1] == 0):
                return b + 1
            return b

        def piece(s, j):
            at = j * HALF
            return [(c, (at + c) // LEN[s], (at + c) % LEN[s], min(HALF, LEN[s])) for c in range(0, HALF, min(HALF, LEN[s]))]

        def parity_of(use, k):
            return k if row_of(use, 0, 0) == 0 else 1 - k

        flat = lambda buf, tiles: buf[:, tiles[0]:tiles[-1] + 1, :].rearrange("p d t -> p (d t)")
        split_no = lambda b, s: b * 3 + (s + 1)
        dtx_no = lambda b, s, p: b * 4 + (p + 1 if s == 0 else s + 2)
        units_done = lambda b, s: b * NU + (FIRST_UNIT[s] + UNITS[s])

        @block.sync
        def _(sp):
            loads = ((conv_w[:], w["conv_w"].partition_broadcast(P)), (hb[:, 0, 0, 0:SCALES * DI], w["xi_w"]),
                     (z_w[:], w["z_w"]), (xp_w[:], w["xp_w"]), (dt_w[:], w["dt_w"]), (hb[:, 0, 1, 0:SCALES * DI], w["out_w"]),
                     (fus_w[:], w["fus_w"]), (cols[:], w["cols"]), (decay[:], w["a_log"]), (fus_b[:], w["fus_b"]),
                     (ln_g[:], w["ln_g"].partition_broadcast(P)), (ln_b[:], w["ln_b"].partition_broadcast(P)),
                     (pick_f[:], w["pick"]))
            assert len(loads) == 13
            for dst, src in loads:
                sp.dma_start(dst, src).then_inc(s_load, 16)

            def rows(t, b):
                return t[bass.ds(b * SEQ, SEQ), :].rearrange("(j p) d -> p j d", p=P)

            def load(b, k):
                sp.dma_start(hl[:, k], rows(h_in, b)).then_inc(s_hl[k], 16)

            def store(b, k):
                sp.wait_ge(s_h3, b + 1)
                sp.dma_start(rows(h_out, b), hl[:, k]).then_inc(s_hs[k], 16)
                sp.wait_ge(s_hs[k], (b - k) * 8 + 16)

            load(0, 0)
            load(1, 1)
            with sp.Fori(0, BATCH // 2 - 1) as i:
                for k in range(2):
                    store(i * 2 + k, k)
                    sp.wait_ge(s_hst, (i * 2 + k) * 2 + 2)
                    load(i * 2 + (k + 2), k)
            for k in range(2):
                store(BATCH - 2 + k, k)

        @block.gpsimd
        def _(pool):
            st = Steps(s_const)
            for x in xts:
                st.link(pool, nc.gpsimd.memset(x[:, 0:TAPS - 1], 0.0))
            st.link(pool, nc.gpsimd.memset(power[:], -0.5))
            st.link(pool, nc.gpsimd.memset(zero[:], 0.0))
            st.link(pool, nc.gpsimd.memset(da[:, :, :, 0:1], 0.0))

            def go():
                pool.sem_inc(s_pool, 1)

            def linked(st, ins):
                st.up(ins)
                st.wait(pool)
                go()

            def split(b, s, first):
                t = LEN[s]
                st = Steps(s_splits, b * 9 + 3 * s)
                pool.wait_ge(s_bc, split_no(b, s))
                if not first:
                    pool.wait_ge(s_c, units_done(b - 1, s))
                go()
                linked(st, nc.gpsimd.tensor_copy(bc[s][:], bc_f[:, 0:t]))
                linked(st, nc.gpsimd.tensor_tensor(bc_f[64:P, 0:t], bc_f[64:P, 0:t], bc[s][64:P, :], ALU.subtract))
                linked(st, nc.gpsimd.tensor_copy(bc[s][64:P, :], bc_f[64:P, 0:t]))
                nc.gpsimd.tensor_tensor(bc[s][96:P, :], bc_f[96:P, 0:t], bc[s][96:P, :], ALU.subtract).then_inc(s_split, 1)
                pool.wait_ge(s_split, split_no(b, s))
                go()

            def softplus(b, s, p, kr, first):
                tiles = PARTS[s][p]
                n = len(tiles) * LEN[s]
                st = Steps(s_dts, dtx_no(b, s, p) * 10 - 10)
                pool.wait_ge(s_sp, dtx_no(b, s, p))
                if not first:
                    pool.wait_ge(s_da, units_done(b - 1, s))
                go()
                linked(st, nc.gpsimd.tensor_scalar(t_one[:, 0:n], t_exp[:, 0:n], 1.0, 1.0, ALU.add, ALU.subtract))
                linked(st, nc.gpsimd.tensor_tensor(t_one[:, 0:n], t_one[:, 0:n], t_exp[:, 0:n], ALU.subtract))
                linked(st, nc.gpsimd.tensor_tensor(t_ln[:, 0:n], t_ln[:, 0:n], t_one[:, 0:n], ALU.subtract))
                linked(st, nc.gpsimd.tensor_scalar(t_one[:, 0:n], t_exp[:, 0:n], -0.5, 1.0, ALU.mult, ALU.add))
                linked(st, nc.gpsimd.tensor_tensor(t_one[:, 0:n], t_one[:, 0:n], t_exp[:, 0:n], ALU.mult))
                linked(st, nc.gpsimd.tensor_tensor(t_ln[:, 0:n], t_ln[:, 0:n], t_one[:, 0:n], ALU.subtract))
                linked(st, nc.gpsimd.tensor_scalar(t_exp[:, 0:n], t_exp[:, 0:n], SERIES, None, ALU.is_ge))
                linked(st, nc.gpsimd.tensor_tensor(t_ln[:, 0:n], t_ln[:, 0:n], t_exp[:, 0:n], ALU.mult))
                linked(st, nc.gpsimd.tensor_tensor(t_one[:, 0:n], t_one[:, 0:n], t_relu[:, 0:n], ALU.add))
                linked(st, nc.gpsimd.tensor_tensor(flat(dt_[s], tiles), t_one[:, 0:n], t_ln[:, 0:n], ALU.add))
                nc.gpsimd.tensor_tensor(flat(dtx[s], tiles), flat(dt_[s], tiles), flat(xc[s][kr], tiles),
                                        ALU.mult).then_inc(s_dtx, 1)

            def interpolate(b, s, first):
                t, stride = LEN[s], 1 << s
                st = Steps(s_ois, b * 18 + (0 if s == 1 else 6))
                pool.wait_ge(s_o, b * 3 + (s + 1))
                if not first:
                    pool.wait_ge(s_hh, b)
                go()
                dst = oi[:].rearrange("p (t r) -> p t r", r=stride)
                for r in range(stride):
                    x = (r + 0.5) / stride - 0.5
                    near = o[s][:, 0:t] if x < 0 else o[s][:, 2:t + 2]
                    if r:
                        st.wait(pool)
                        go()
                    linked(st, nc.gpsimd.tensor_scalar(t_one[:, 0:t], near, abs(x), None, ALU.mult))
                    linked(st, nc.gpsimd.tensor_scalar(dst[:, :, r], o[s][:, 1:t + 1], 1.0 - abs(x), None, ALU.mult))
                    ins = nc.gpsimd.tensor_tensor(dst[:, :, r], dst[:, :, r], t_one[:, 0:t], ALU.add)
                    st.up(ins)
                st.wait(pool)
                go()
                nc.gpsimd.tensor_tensor(o[0][:], o[0][:], oi[:], ALU.add).then_inc(s_oi, 1)
                pool.wait_ge(s_oi, b * 2 + s)
                go()

            def rstd(b):
                st = Steps(s_lns, b * 8)
                pool.wait_ge(s_hst, b * 2 + 1)
                go()
                m0, m1, v0, v1 = (st6[:, :, c] for c in (1, 4, 2, 5))
                linked(st, nc.gpsimd.tensor_tensor(st_d[:], m0, m1, ALU.subtract))
                linked(st, nc.gpsimd.tensor_tensor(st_m[:], m0, m1, ALU.add))
                linked(st, nc.gpsimd.tensor_scalar(st_m[:], st_m[:], 0.5, None, ALU.mult))
                linked(st, nc.gpsimd.tensor_tensor(st_v[:], v0, v1, ALU.add))
                linked(st, nc.gpsimd.tensor_scalar(st_v[:], st_v[:], 1.0 / DM, LN_EPS, ALU.mult, ALU.add))
                linked(st, nc.gpsimd.tensor_tensor(st_d[:], st_d[:], st_d[:], ALU.mult))
                linked(st, nc.gpsimd.tensor_scalar(st_d[:], st_d[:], 0.25, None, ALU.mult))
                linked(st, nc.gpsimd.tensor_tensor(st_v[:], st_v[:], st_d[:], ALU.add))
                nc.gpsimd.tensor_tensor(st_v[:], st_v[:], power[:], ALU.pow).then_inc(s_rs, 1)

            def finish(b, k):
                st = Steps(s_h3s, b * 2)
                pool.wait_ge(s_nm, b + 1)
                go()
                over = lambda ap: ap[:].unsqueeze(1).to_broadcast([P, TPB, DM])
                linked(st, nc.gpsimd.tensor_tensor(hh[:], hh[:], over(ln_g), ALU.mult))
                linked(st, nc.gpsimd.tensor_tensor(hh[:], hh[:], over(ln_b), ALU.add))
                nc.gpsimd.tensor_tensor(hl[:, k], hl[:, k], hh[:], ALU.add).then_inc(s_h3, 1)

            def main(b, k, base, at, prev, nxt):
                for u in range(NU):
                    for use in at.get(u, []):
                        if use == ("out", 2):
                            interpolate(b - 1, 2, False if prev else True)
                        elif use == ("out", 1):
                            interpolate(b, 1, not prev)
                        elif use[0] == "fuse":
                            rstd(b - 1)
                        elif use[0] == "xp":
                            split(b + (use[1] == 0), use[1], use[1] > 0 and not prev)
                        elif use[0] == "dt":
                            softplus(b + (use[1] == 0), use[1], use[2], 1 - k if use[1] == 0 else k, use[1] > 0 and not prev)
                    if u == 8 and prev:
                        finish(b - 1, 1 - k)

            split(0, 0, True)
            for p in range(2):
                softplus(0, 0, p, 0, True)
            batches(main, pool)
            interpolate(LAST, 2, False)
            rstd(LAST)
            finish(LAST, LAST % 2)

        @block.scalar
        def _(act):
            def consume(n, use, b, kr, first):
                kind = use[0]
                if kind not in ("turn", "xi", "z", "xp", "dt", "out"):
                    return
                act.wait_ge(s_wr, n + 1)
                if kind == "turn":
                    for s in range(SCALES):
                        ins = nc.scalar.activation(xts[s][:, TAPS - 1:], work[:, ::1 << s], ACT.Copy)
                    ins.then_inc(s_wf, 1)
                elif kind in ("xi", "z"):
                    _, s, p = use
                    if not first:
                        act.wait_ge(s_post, (b - 2) * 3 + 1 if s == 0 else (b - 1) * 3 + (s + 1))
                    if kind == "xi":
                        for at, d, t, wd in piece(s, p):
                            ins = nc.scalar.activation(xc[s][kr][:, d, t:t + wd], work[:, at:at + wd], ACT.Silu,
                                                       bias=cols[:, 0, s, d:d + 1])
                    else:
                        for m, d in enumerate(PARTS[s][p]):
                            ins = nc.scalar.activation(sz[s][kr][:, d, :], work[:, m * LEN[s]:(m + 1) * LEN[s]], ACT.Silu)
                    ins.then_inc(s_wf, 1)
                elif kind == "xp":
                    s = use[1]
                    if not (first and s == 0):
                        act.wait_ge(s_split, split_no(b, s) - 1)
                    nc.scalar.activation(bc_f[:, 0:LEN[s]], work[:, 0:LEN[s]], ACT.Copy).then_inc(s_wf, 1)
                    act.wait_ge(s_wf, n + 1)
                    act.sem_inc(s_bc, 1)
                elif kind == "dt":
                    _, s, p = use
                    tiles = PARTS[s][p]
                    w = len(tiles) * LEN[s]
                    no = dtx_no(b, s, p)
                    if not (first and (s, p) == (0, 0)):
                        act.wait_ge(s_dtx, no - 1)
                    for m, d in enumerate(tiles):
                        cut = slice(m * LEN[s], (m + 1) * LEN[s])
                        nc.scalar.activation(t_exp[:, cut], work[:, cut], ACT.Abs, bias=cols[:, 1, s, d:d + 1])
                        ins = nc.scalar.activation(t_relu[:, cut], work[:, cut], ACT.Relu, bias=cols[:, 1, s, d:d + 1])
                    ins.then_inc(s_wf, 1)
                    act.wait_ge(s_wf, n + 1)
                    nc.scalar.activation(t_exp[:, 0:w], t_exp[:, 0:w], ACT.Exp, scale=-1.0).then_inc(s_act, 1)
                    act.wait_ge(s_act, no)
                    nc.scalar.activation(t_ln[:, 0:w], t_exp[:, 0:w], ACT.Ln, bias=1.0).then_inc(s_sp, 1)
                else:
                    s = use[1]
                    if s == 0 and not first:
                        act.wait_ge(s_hh, b)
                    elif s and not first:
                        act.wait_ge(s_oi, b * 2 + (s - 2))
                    if s == 0:
                        nc.scalar.activation(o[0][:], work[:], ACT.Identity, bias=fus_b[:]).then_inc(s_wf, 1)
                    else:
                        t = LEN[s]
                        nc.scalar.activation(o[s][:, 0:1], work[:, 0:1], ACT.Copy)
                        nc.scalar.activation(o[s][:, t + 1:t + 2], work[:, t - 1:t], ACT.Copy)
                        nc.scalar.activation(o[s][:, 1:t + 1], work[:, 0:t], ACT.Copy).then_inc(s_wf, 1)
                    act.wait_ge(s_wf, n + 1)
                    act.sem_inc(s_o, 1)

            def decays(b, u, begins):
                s, v = scale_of(u)
                n = b * NU + u
                r = u % 2
                act.wait_ge(s_dtx, b * 4 + (2, 3, 4)[s])
                if not begins:
                    act.wait_ge(s_scan, n - 1)
                if s and v < 2:
                    nc.scalar.activation(da[:, r, :, LEN[s]::LEN[s]], zero[:, :, 0:NS[s] - 1], ACT.Copy)
                for d in range(DT2):
                    for m in range(NS[s]):
                        q = v * NS[s] + m
                        ins = nc.scalar.activation(da[:, r, d, m * LEN[s] + 1:(m + 1) * LEN[s]], dt_[s][:, d, 1:],
                                                   ACT.Exp, scale=decay[:, s, d, q:q + 1])
                ins.then_inc(s_da, 1)

            def main(b, k, base, at, prev, nxt):
                n = base
                for u in range(NU):
                    for use in at.get(u, []):
                        row = row_of(use, b, u)
                        later = use[0] == "turn" or (use[0] not in ("out", "fuse") and use[1] == 0)
                        if use[0] in ("xi", "z") and use[1] == 0:
                            fresh = not prev
                        else:
                            fresh = not prev and not later
                        consume(n, use, row, parity_of(use, k), fresh)
                        n = n + 1
                    n = n + 1
                    if u + 1 < NU:
                        decays(b, u + 1, not prev and u == 0)
                    elif nxt:
                        decays(b + 1, 0, False)

            act.wait_ge(s_load, 13 * 16)
            nc.scalar.activation(decay[:], decay[:], ACT.Exp).then_inc(s_prep, 1)
            act.wait_ge(s_const, 6)
            act.wait_ge(s_fold, SCALES + 2)
            for n, use in enumerate(FIRST):
                consume(n, use, 0, 0, True)
            decays(0, 0, True)
            batches(main, act)
            consume(END, ("out", 2), LAST, LAST % 2, False)

        @block.vector
        def _(dve):
            def norm(b, k):
                dve.wait_ge(s_hl[k], (b - k) * 8 + 16)
                for j in range(TPB):
                    tile = b * TPB + j
                    ins = nc.vector.tensor_scalar(xn[:, k, j, :], hl[:, k, j, :], g.mean[:, bass.ds(tile, 1)],
                                                  g.rstd[:, bass.ds(tile, 1)], ALU.subtract, ALU.mult)
                ins.then_inc(s_xn, 1)

            def gate_out(b, k, s):
                tiles = list(range(DT2))
                dve.wait_ge(s_y, units_done(b, s))
                for d in tiles:
                    ins = nc.vector.scalar_tensor_tensor(out=dtx[s][:, d, :], in0=xc[s][k][:, d, :], scalar=cols[:, 2, s, d:d + 1],
                                                         in1=yps[:, d, 0:LEN[s]], op0=ALU.mult, op1=ALU.add)
                ins.then_inc(s_post1, 1)
                dve.wait_ge(s_post1, b * 3 + (s + 1))
                nc.vector.tensor_tensor(flat(dtx[s], tiles), flat(dtx[s], tiles), flat(sz[s][k], tiles),
                                        ALU.mult).then_inc(s_post, 1)

            def fuse(n, b, k):
                dve.wait_ge(s_wr, n + 1)
                nc.vector.tensor_tensor(hh[:].rearrange("p j d -> p (j d)"), work[:], xn[:, k].rearrange("p j d -> p (j d)"),
                                        ALU.add).then_inc(s_wf, 1)
                dve.wait_ge(s_wf, n + 1)
                dve.sem_inc(s_hh, 1)
                for j in range(TPB):
                    ins = nc.vector.bn_stats(st6[:, j, :], hh[:, j, :])
                ins.then_inc(s_hst, 1)

            def normalise(b):
                dve.wait_ge(s_rs, b + 1)
                for j in range(TPB):
                    ins = nc.vector.tensor_scalar(hh[:, j, :], hh[:, j, :], st_m[:, j:j + 1], st_v[:, j:j + 1],
                                                  ALU.subtract, ALU.mult)
                ins.then_inc(s_nm, 1)

            def stats(b, k):
                dve.wait_ge(s_h3, b + 1)
                for j in range(TPB):
                    ins = nc.vector.bn_stats(g.stat[:, bass.ds(b * TPB + j, 1), :], hl[:, k, j, :])
                ins.then_inc(s_hst, 1)

            def main(b, k, base, at, prev, nxt):
                n = base
                for u in range(NU):
                    s, v = scale_of(u)
                    for use in at.get(u, []):
                        if use[0] == "fuse":
                            fuse(n, b - 1, 1 - k)
                        n = n + 1
                    i = b * NU + u
                    r = u % 2
                    if u == 12 and nxt:
                        norm(b + 1, 1 - k)
                    dve.wait_ge(s_wr, n + 1)
                    if v == 0:
                        dve.wait_ge(s_dtx, b * 4 + (2, 3, 4)[s])
                    if prev or u >= 2:
                        dve.wait_ge(s_y, i - 1)
                    shape = [P, DT2, NS[s], LEN[s]]
                    nc.vector.tensor_tensor(hb[:, r].rearrange("p d (n t) -> p d n t", n=NS[s]),
                                            work[:].rearrange("p (n t) -> p n t", n=NS[s]).unsqueeze(1).to_broadcast(shape),
                                            dtx[s][:].unsqueeze(2).to_broadcast(shape), ALU.mult).then_inc(s_wf, 1)
                    dve.wait_ge(s_wf, n + 1)
                    n = n + 1
                    dve.wait_ge(s_da, i + 1)
                    every = hb[:, r].rearrange("p d c -> p (d c)")
                    nc.vector.tensor_tensor_scan(every, da[:, r].rearrange("p d c -> p (d c)"), every, 0.0,
                                                 ALU.mult, ALU.add).then_inc(s_scan, 1)
                    dve.wait_ge(s_c, i + 1)
                    dve.wait_ge(s_scan, i + 1)
                    nc.vector.tensor_tensor(hb[:, r], hb[:, r], cps[:].unsqueeze(1).to_broadcast([P, DT2, UW]),
                                            ALU.mult).then_inc(s_g, 1)
                    if v == 0 and s > 0:
                        gate_out(b, k, s - 1)
                    elif u == 0 and prev:
                        gate_out(b - 1, 1 - k, SCALES - 1)
                    if prev and u == 7:
                        normalise(b - 1)
                    if prev and u == 10:
                        stats(b - 1, 1 - k)

            dve.wait_ge(s_load, 13 * 16)
            for s in range(SCALES):
                nc.vector.tensor_tensor(conv_w[:, s], conv_w[:, s],
                                        hb[:, 0, 0, s * DI:(s + 1) * DI].unsqueeze(1).to_broadcast([P, TAPS, DI]),
                                        ALU.mult).then_inc(s_fold, 1)
            nc.vector.tensor_copy(pick[:], pick_f[:].to_broadcast([P, 2 * ST, P])).then_inc(s_fold, 1)
            dve.wait_ge(s_prep, 1)
            nc.vector.tensor_scalar(decay[:], decay[:], -1.0, None, ALU.mult).then_inc(s_fold, 1)
            dve.wait_ge(s_fold, SCALES + 2)
            dve.wait_ge(s_fus, 1)
            nc.vector.tensor_copy(out_w[:].rearrange("p s d o -> p (s d o)"),
                                  work[:, 0:SCALES * DT2 * DM]).then_inc(s_fused_w, 1)
            norm(0, 0)
            dve.wait_ge(s_const, 6)
            batches(main, dve)
            gate_out(LAST, LAST % 2, SCALES - 1)
            fuse(END + 1, LAST, LAST % 2)
            normalise(LAST)
            stats(LAST, LAST % 2)

        @block.tensor
        def _(pe):
            def banks(t):
                return [(c, min(HALF, t - c)) for c in range(0, t, HALF)]

            def produce(n, use, b, k, first=False):
                kind = use[0]
                if not first:
                    pe.wait_ge(s_wf, n)
                if kind == "turn":
                    pe.wait_ge(s_xn, b + 1)
                    for j in range(TPB):
                        ins = nc.tensor.transpose(work[:, j * P:(j + 1) * P], xn[:, k, j, :], g.ident[:])
                elif kind == "xi":
                    _, s, j = use
                    for at, d, t, wd in piece(s, j):
                        for tap in range(TAPS):
                            ins = nc.tensor.matmul(work[:, at:at + wd], conv_w[:, s, tap, d * P:(d + 1) * P],
                                                   xts[s][:, tap + t:tap + t + wd], start=(tap == 0),
                                                   stop=(tap == TAPS - 1))
                elif kind == "z":
                    _, s, p = use
                    for m, d in enumerate(PARTS[s][p]):
                        for c, wd in banks(LEN[s]):
                            ins = nc.tensor.matmul(work[:, m * LEN[s] + c:m * LEN[s] + c + wd],
                                                   z_w[:, s, d * P:(d + 1) * P],
                                                   xts[s][:, TAPS - 1 + c:TAPS - 1 + c + wd], start=True, stop=True)
                elif kind == "xp":
                    s = use[1]
                    for c, wd in banks(LEN[s]):
                        for d in range(DT2):
                            ins = nc.tensor.matmul(work[:, c:c + wd], xp_w[:, s, d, :], xc[s][k][:, d, c:c + wd],
                                                   start=(d == 0), stop=(d == DT2 - 1))
                elif kind == "dt":
                    _, s, p = use
                    for m, d in enumerate(PARTS[s][p]):
                        for c, wd in banks(LEN[s]):
                            ins = nc.tensor.matmul(work[:, m * LEN[s] + c:m * LEN[s] + c + wd],
                                                   dt_w[:, s, d * P:(d + 1) * P], bc_f[0:DTR, c:c + wd],
                                                   start=True, stop=True)
                elif kind == "out":
                    s = use[1]
                    pe.wait_ge(s_post, b * 3 + (s + 1))
                    for c, wd in banks(LEN[s]):
                        for d in range(DT2):
                            ins = nc.tensor.matmul(work[:, c:c + wd], out_w[:, s, d, :], dtx[s][:, d, c:c + wd],
                                                   start=(d == 0), stop=(d == DT2 - 1))
                elif kind == "fuse":
                    pe.wait_ge(s_oi, b * 2 + 2)
                    for j in range(TPB):
                        ins = nc.tensor.transpose(work[:, j * P:(j + 1) * P], o[0][:, j * P:(j + 1) * P], g.ident[:])
                ins.then_inc(s_wr, 1)

            def spread(dst, s, v, which, sem_):
                for m in range(NS[s]):
                    q = which * ST + v * NS[s] + m
                    for c, wd in banks(LEN[s]):
                        ins = nc.tensor.matmul(dst[:, m * LEN[s] + c:m * LEN[s] + c + wd], pick[:, q, :],
                                               bc[s][:, c:c + wd], start=True, stop=True)
                ins.then_inc(sem_, 1)

            def total(b, u, d, reused):
                s, v = scale_of(u)
                if v == 0 and reused:
                    pe.wait_ge(s_post1, b * 3 + s)
                for m in range(NS[s]):
                    for c, wd in banks(LEN[s]):
                        at = m * LEN[s] + c
                        ins = nc.tensor.matmul(yps[:, d, c:c + wd], g.ident[:], hb[:, u % 2, d, at:at + wd],
                                               start=(v == 0 and m == 0), stop=(v == UNITS[s] - 1 and m == NS[s] - 1))
                if d == DT2 - 1:
                    ins.then_inc(s_y, 1)

            def main(b, k, base, at, prev, nxt):
                n = base
                for u in range(NU):
                    s, v = scale_of(u)
                    pe.wait_ge(s_wf, n)
                    if v == 0:
                        pe.wait_ge(s_split, split_no(b, s))
                    spread(work, s, v, 0, s_wr)
                    n = n + 1
                    if prev or u > 0:
                        pe.wait_ge(s_g, b * NU + u)
                    spread(cps, s, v, 1, s_c)
                    last = (b, u - 1, prev or u > 1) if u else (b - 1, NU - 1, True)
                    if prev or u > 0:
                        total(last[0], last[1], 0, last[2])
                    for use in at.get(u + 1, []):
                        produce(n, use, row_of(use, b, u + 1), parity_of(use, k))
                        n = n + 1
                    if prev or u > 0:
                        total(last[0], last[1], 1, last[2])

            pe.wait_ge(s_const, 6)
            pe.wait_ge(s_fold, SCALES + 2)
            pe.wait_ge(s_load, 13 * 16)
            for n in range(SCALES * DT2):
                ins = nc.tensor.matmul(work[:, n * DM:(n + 1) * DM], hb[:, 0, 1, n * P:(n + 1) * P],
                                       fus_w[:, n // DT2, :], start=True, stop=True)
            ins.then_inc(s_fus, 1)
            pe.wait_ge(s_fused_w, 1)
            for n, use in enumerate(FIRST):
                produce(n, use, 0, 0, n == 0)
            batches(main, pe)
            pe.wait_ge(s_g, BATCH * NU)
            for d in range(DT2):
                total(LAST, NU - 1, d, True)
            produce(END, ("out", 2), LAST, LAST % 2)
            produce(END + 1, ("fuse",), LAST, LAST % 2)


E2, K2 = 8, 2


def moe_phase(nc, g, h_in, out, w):
    with ExitStack() as ctx:
        sb = lambda name, shape, dt=F32: ctx.enter_context(nc.sbuf_tensor("t_" + name, shape, dt))
        ps = lambda name, shape, dt=F32: ctx.enter_context(nc.psum_tensor("t_" + name, shape, dt))
        sem = lambda name: ctx.enter_context(nc.semaphore("t_" + name))
        wg = sb("wg", [P, E2])
        rows = sb("rows", [1, E2 + P])
        down_b = sb("down_b", [P, CH * DM])
        up_w = sb("up_w", [P, E2, FF])
        up_b = sb("up_b", [P, E2, FT])
        down_w = sb("down_w", [P, E2, FT, DM])
        order = sb("order", [P, CH, E2])
        h = sb("h", [P, 2, CH, DM])
        xn = sb("xn", [P, CH, DM])
        xt = sb("xt", [P, 2, CW])
        hid = sb("hid", [P, 2, FT, CW])
        lg = sb("lg", [P, CH, E2])
        hot = sb("hot", [P, K2, CH, E2])
        rank = sb("rank", [P, CH])
        top = sb("top", [P, K2, CH])
        mix = sb("mix", [P, K2, CH])
        comb = sb("comb", [P, 2, P])
        comb_t = sb("comb_t", [P, P])
        turned = ps("turned", [P, CW])
        logit = ps("logit", [P, CW])
        ups = [ps(f"up{f}", [P, CW]) for f in range(FT)]
        down = [ps(f"down{n}", [P, CW]) for n in range(2)]
        s_load = sem("weights_loaded")
        s_const = sem("constants_set")
        s_h = [sem(f"h_loaded{k}") for k in range(2)]
        s_xn = sem("norm_applied")
        s_turn = sem("rows_turned")
        s_xt = sem("rows_t_ready")
        s_logit = sem("logits_ready")
        s_r = sem("routing_steps")
        s_w = sem("weight_steps")
        s_d = sem("top_difference_ready")
        s_e = sem("top_exp_ready")
        s_up = sem("up_done")
        s_act = sem("silu_done")
        s_down = sem("down_done")
        s_ct = sem("weights_turned")
        s_cs = sem("weights_t_ready")
        s_b = sem("biases_weighed")
        s_ba = sem("biases_added")
        s_add = sem("outputs_added")
        s_out = [sem(f"stored{k}") for k in range(2)]
        block = ctx.enter_context(nc.Block())
        PAIRS = CHUNKS // 2
        R = 13

        def chunk(t, c):
            return t[bass.ds(c * CW, CW), :].rearrange("(j p) d -> p j d", p=P)

        @block.sync
        def _(sp):
            for dst, src in ((wg[:], w["wg"]), (rows[0:1, 0:E2], w["bg"]), (down_b[:], w["b2"]),
                             (up_w[:], w["w1"]), (up_b[:], w["b1"]), (down_w[:], w["w2"])):
                sp.dma_start(dst, src).then_inc(s_load, 16)
            sp.dma_start(h[:, 0], chunk(h_in, 0)).then_inc(s_h[0], 16)
            sp.dma_start(h[:, 1], chunk(h_in, 1)).then_inc(s_h[1], 16)

            def store(c, k):
                sp.wait_ge(s_add, (c + 1) * E2)
                sp.dma_start(chunk(out, c), h[:, k]).then_inc(s_out[k], 16)
                sp.wait_ge(s_out[k], (c - k) * 8 + 16)

            with sp.Fori(0, PAIRS - 1) as i:
                for k in range(2):
                    store(i * 2 + k, k)
                    sp.dma_start(h[:, k], chunk(h_in, i * 2 + (k + 2))).then_inc(s_h[k], 16)
            store(CHUNKS - 2, 0)
            store(CHUNKS - 1, 1)

        @block.gpsimd
        def _(pool):
            st = Steps(s_const)
            st.link(pool, nc.gpsimd.memset(rows[0:1, E2:], 1.0))
            st.link(pool, nc.gpsimd.memset(comb[:], 0.0))
            for e in range(E2):
                st.link(pool, nc.gpsimd.memset(order[:, :, e:e + 1], float(E2 - e)))

        def chunks(body, eng):
            body(0, 0, 0, True)
            body(1, 1, 1, True)
            with eng.Fori(1, PAIRS - 1) as i:
                body(i * 2, 0, 2, True)
                body(i * 2 + 1, 1, 2, True)
            body(CHUNKS - 2, 0, 2, True)
            body(CHUNKS - 1, 1, 2, False)

        @block.scalar
        def _(act):
            def copy_t(c, k, before):
                act.wait_ge(s_turn, c + 1)
                if before > 1:
                    act.wait_ge(s_up, (c - 1) * E2 * FT)
                    act.wait_ge(s_logit, c - 1)
                nc.scalar.activation(xt[:, k, :], turned[:], ACT.Copy).then_inc(s_xt, 1)

            def body(c, k, before, more):
                for e in range(E2):
                    n = c * E2 + e
                    for f in range(FT):
                        act.wait_ge(s_up, n * FT + (f + 1))
                        if f == 0 and (before or e >= 2):
                            act.wait_ge(s_down, n - 1)
                        nc.scalar.activation(hid[:, e % 2, f, :], ups[f][:], ACT.Silu,
                                             bias=up_b[:, e, f:f + 1]).then_inc(s_act, 1)
                    if e == 0:
                        act.wait_ge(s_ct, c + 1)
                        if before:
                            act.wait_ge(s_b, c)
                        nc.scalar.activation(comb_t[:], logit[:, P:2 * P], ACT.Copy).then_inc(s_cs, 1)
                    if e == 2 and more:
                        copy_t(c + 1, 1 - k, min(before + 1, 2))
                    if e == 5 and more:
                        act.wait_ge(s_d, c + 2)
                        nc.scalar.activation(mix[:, 1, :], mix[:, 0, :], ACT.Exp).then_inc(s_e, 1)

            act.wait_ge(s_load, 6 * 16)
            copy_t(0, 0, 0)
            act.wait_ge(s_d, 1)
            nc.scalar.activation(mix[:, 1, :], mix[:, 0, :], ACT.Exp).then_inc(s_e, 1)
            chunks(body, act)

        @block.vector
        def _(dve):
            def norm(c, k):
                dve.wait_ge(s_h[k], (c - k) * 8 + 16)
                for j in range(CH):
                    ins = nc.vector.tensor_scalar(xn[:, j, :], h[:, k, j, :], g.mean[:, bass.ds(c * CH + j, 1)],
                                                  g.rstd[:, bass.ds(c * CH + j, 1)], ALU.subtract, ALU.mult)
                ins.then_inc(s_xn, 1)

            BIG = [P, CH, E2]

            def choose(c, k):
                st = Steps(s_r, c * R)
                dve.wait_ge(s_logit, c + 1)
                st.link(dve, nc.vector.tensor_copy(lg[:].rearrange("p j e -> p (j e)"), logit[:, 0:CH * E2]))
                for n in range(K2):
                    st.link(dve, nc.vector.tensor_reduce(top[:, n, :], lg[:], AX_X, ALU.max))
                    st.link(dve, nc.vector.tensor_tensor(hot[:, n], lg[:], top[:, n, :].to_broadcast(BIG), ALU.is_ge))
                    st.link(dve, nc.vector.tensor_tensor(hot[:, n], hot[:, n], order[:], ALU.mult))
                    st.link(dve, nc.vector.tensor_reduce(rank[:], hot[:, n], AX_X, ALU.max))
                    st.link(dve, nc.vector.tensor_tensor(hot[:, n], order[:], rank[:].to_broadcast(BIG), ALU.is_equal))
                    if n == 0:
                        st.link(dve, nc.vector.scalar_tensor_tensor(out=lg[:], in0=hot[:, 0], scalar=-3e38, in1=lg[:],
                                                                    op0=ALU.mult, op1=ALU.add))
                st.up(nc.vector.tensor_tensor(mix[:, 0, :], top[:, 1, :], top[:, 0, :], ALU.subtract))
                st.wait(dve)
                dve.sem_inc(s_d, 1)

            def weigh(c, k, before):
                st = Steps(s_w, c * 6)
                dve.wait_ge(s_e, c + 1)
                st.link(dve, nc.vector.tensor_scalar(top[:, 0, :], mix[:, 1, :], 1.0, None, ALU.add))
                st.link(dve, nc.vector.reciprocal(top[:, 0, :], top[:, 0, :]))
                st.link(dve, nc.vector.tensor_tensor(top[:, 1, :], top[:, 0, :], mix[:, 1, :], ALU.mult))
                for n in range(K2):
                    st.link(dve, nc.vector.tensor_tensor(hot[:, n], hot[:, n], top[:, n, :].to_broadcast(BIG), ALU.mult))
                st.link(dve, nc.vector.tensor_tensor(comb[:, k, 0:CH * E2].rearrange("p (j e) -> p j e", e=E2), hot[:, 0], hot[:, 1],
                                                     ALU.add))

            def body(c, k, before, more):
                for e in range(E2):
                    n = c * E2 + e
                    dve.wait_ge(s_down, n + 1)
                    if before or e:
                        dve.wait_ge(s_add, n)
                    if e == 2:
                        dve.wait_ge(s_ba, c + 1)
                    for j in range(CH):
                        ins = nc.vector.scalar_tensor_tensor(out=h[:, k, j, :], in0=down[e % 2][:, j * P:(j + 1) * P],
                                                             scalar=comb[:, k, j * E2 + e:j * E2 + e + 1], in1=h[:, k, j, :],
                                                             op0=ALU.mult, op1=ALU.add)
                    ins.then_inc(s_add, 1)
                    if e == 1:
                        dve.wait_ge(s_b, c + 1)
                        dve.wait_ge(s_add, n + 1)
                        rows_k = h[:, k].rearrange("p j d -> p (j d)")
                        nc.vector.tensor_tensor(rows_k, rows_k, turned[:], ALU.add).then_inc(s_ba, 1)
                    if more and e == 0:
                        norm(c + 1, 1 - k)
                    if more and e == 4:
                        choose(c + 1, 1 - k)
                    if more and e == 6:
                        weigh(c + 1, 1 - k, before)

            dve.wait_ge(s_const, 2 + E2)
            norm(0, 0)
            choose(0, 0)
            weigh(0, 0, 0)
            chunks(body, dve)

        @block.tensor
        def _(pe):
            def turn(c, k, before):
                pe.wait_ge(s_xn, c + 1)
                if before:
                    pe.wait_ge(s_ba, c)
                for j in range(CH):
                    ins = nc.tensor.transpose(turned[:, j * P:(j + 1) * P], xn[:, j, :], g.ident[:])
                ins.then_inc(s_turn, 1)

            def router(c, k, before):
                pe.wait_ge(s_xt, c + 1)
                if before:
                    pe.wait_ge(s_r, c * R)
                for j in range(CH):
                    o = logit[:, j * E2:(j + 1) * E2]
                    nc.tensor.matmul(o, xt[:, k, j * P:(j + 1) * P], wg[:], start=True, stop=False)
                    ins = nc.tensor.matmul(o, rows[0:1, E2:], rows[0:1, 0:E2], start=False, stop=True)
                ins.then_inc(s_logit, 1)

            def up(n, e, k, begins):
                for f in range(FT):
                    if not begins:
                        pe.wait_ge(s_act, (n - 1) * FT + (f + 1))
                    nc.tensor.matmul(ups[f][:], up_w[:, e, f * P:(f + 1) * P], xt[:, k, :], start=True,
                                     stop=True).then_inc(s_up, 1)

            def down_(n, e, early):
                pe.wait_ge(s_act, n * FT + FT)
                if not early:
                    pe.wait_ge(s_add, n - 1)
                for j in range(CH):
                    o = down[e % 2][:, j * P:(j + 1) * P]
                    for f in range(FT):
                        ins = nc.tensor.matmul(o, hid[:, e % 2, f, j * P:(j + 1) * P], down_w[:, e, f, :],
                                               start=(f == 0), stop=(f == FT - 1))
                ins.then_inc(s_down, 1)

            def body(c, k, before, more):
                for e in range(E2):
                    n = c * E2 + e
                    if e + 1 < E2:
                        up(n + 1, e + 1, k, False)
                    elif more:
                        up(n + 1, 0, 1 - k, False)
                    if e == 1:
                        pe.wait_ge(s_cs, c + 1)
                        nc.tensor.matmul(turned[:], comb_t[:], down_b[:], start=True, stop=True).then_inc(s_b, 1)
                    down_(n, e, not before and e < 2)
                    if e == 0:
                        pe.wait_ge(s_w, (c + 1) * 6)
                        nc.tensor.transpose(logit[:, P:2 * P], comb[:, k, :], g.ident[:]).then_inc(s_ct, 1)
                    if more and e == 2:
                        turn(c + 1, 1 - k, True)
                    if more and e == 3:
                        router(c + 1, 1 - k, True)

            pe.wait_ge(s_load, 6 * 16)
            pe.wait_ge(s_const, 2 + E2)
            turn(0, 0, 0)
            router(0, 0, 0)
            up(0, 0, 0, True)
            chunks(body, pe)


def lm_tower(nc, out, a):
    scratch = lambda name, shape, dt=F32: nc.dram_tensor(name, shape, dt).ap()
    part_rows = scratch("part_rows", (2, P, 3, SEQ), BF16)
    max_rows = scratch("max_rows", (3, HEADS * SEQ), BF16)
    slots_x = scratch("slots_x", (GE * CAP, DM))
    slots_y = scratch("slots_y", (GE * CAP, DM))
    first_out = scratch("first_layer_out", (TOK, DM))
    mixed_out = scratch("mixed_out", (TOK, DM))
    with ExitStack() as ctx:
        g = setup(nc, ctx, a["identity"])
        with ExitStack() as first:
            setup_h(nc, first, g)
            embed_phase(nc, g, a["x"], [a["table2"], a["table3"], a["table4"]], a["tok_w"], a["tok_b"], slots_x)
            norm_phase(nc, g, "norm0")
            attention_phase(nc, g, a["attn_w"], a["attn_bqk"], a["attn_bv"], a["attn_out_w"], a["attn_out_b"],
                            a["rope_cos"], a["rope_sin"], part_rows, max_rows)
            norm_phase(nc, g, "norm1")
            setup_slots(nc, first, g)
            route_phase(nc, g, a["router_w"], a["router_b"], a["shared_w1"], a["shared_b1"], a["shared_w2"],
                        a["shared_b2"], a["upto"], slots_x)
            experts_phase(nc, g, slots_x, slots_y, a["experts_w1"], a["experts_b1"], a["experts_w2"], a["experts_b2"])
            combine_phase(nc, g, slots_y, first_out)
            norm_phase(nc, g, "norm2")
        mamba_phase(nc, g, first_out, mixed_out, {k[6:]: v for k, v in a.items() if k.startswith("mamba_")})
        norm_phase(nc, g, "norm3")
        moe_phase(nc, g, mixed_out, out, {k[4:]: v for k, v in a.items() if k.startswith("moe_")})


def lay_out(z):
    import numpy as np
    c = np.ascontiguousarray
    f = np.float32
    banks = lambda name: np.concatenate([z[f"L0_ffn_{name}_sp"], z[f"L0_ffn_{name}_fq"]], axis=-1 if name[1] == "r" else 0)
    a = {"identity": np.eye(P, dtype=f), "x": z["x"], "table2": z["L0_tok_emb_2"], "table3": z["L0_tok_emb_3"],
         "table4": z["L0_tok_emb_4"], "tok_w": c(z["L0_tok_proj_w"].T), "tok_b": z["L0_tok_proj_b"]}

    w, b = z["L0_attn_Wqkv"], z["L0_attn_bqkv"]
    swap = np.arange(DM) ^ 1
    q, k, v = (w[n * DM:(n + 1) * DM] for n in range(3))
    bq, bk = b[0:DM], b[DM:2 * DM]
    a["attn_w"] = c(np.stack([q.T, q[swap].T, k.T, k[swap].T, v.T], axis=1))
    a["attn_bqk"] = c(np.stack([bq, bq[swap], bk, bk[swap]], axis=1))
    a["attn_bv"] = c(b[2 * DM:, None])
    a["attn_out_w"] = c(z["L0_attn_Wproj"].T)
    a["attn_out_b"] = c(z["L0_attn_bproj"][None])
    freq = (1.0 / (f(10000.0) ** (np.arange(0, HD, 2, dtype=f) / f(HD)))).astype(f)
    angle = np.outer(np.arange(SEQ, dtype=f), freq).astype(f).astype(np.float64)
    pair = np.arange(DM) % HD // 2
    sign = np.where(np.arange(DM) % 2, 1.0, -1.0)[:, None]
    a["rope_cos"] = c(np.cos(angle)[:, pair].T.astype(f))
    a["rope_sin"] = c((np.sin(angle)[:, pair].T * sign).astype(f))

    a["router_w"] = c(banks("Wr"))
    a["router_b"] = c(banks("br")[None])
    a["shared_w1"] = z["L0_ffn_Ws1"]
    a["shared_b1"] = c(z["L0_ffn_bs1"].reshape(FT, P).T)
    a["shared_w2"] = c(z["L0_ffn_Ws2"].reshape(FT, P, DM).transpose(1, 0, 2))
    a["shared_b2"] = c(z["L0_ffn_bs2"][None])
    a["upto"] = np.triu(np.ones((P, P), f))
    a["experts_w1"] = c(banks("W1"))
    a["experts_b1"] = c(banks("b1").reshape(GE, FT, P).transpose(0, 2, 1))
    a["experts_w2"] = c(banks("W2"))
    a["experts_b2"] = c(banks("b2"))

    m = lambda name: z["L1_attn_" + name]
    tiles = lambda v: v.reshape(SCALES, DT2, P).transpose(2, 0, 1)
    xp = m("xp_w")
    bc = xp[:, DTR:]
    pick = np.zeros((P, 2 * ST), f)
    for n in range(2 * ST):
        pick[[DTR * part + n for part in (1, 2, 3)], n] = 1.0
    a.update({
        "mamba_conv_w": c(m("conv_w").transpose(0, 2, 1)),
        "mamba_xi_w": c(m("in_w")[:, :DI].transpose(2, 0, 1).reshape(DM, SCALES * DI)),
        "mamba_z_w": c(m("in_w")[:, DI:].transpose(2, 0, 1)),
        "mamba_xp_w": c(np.concatenate([xp[:, :DTR], bc, bc, bc], 1).reshape(SCALES, P, DT2, P).transpose(3, 0, 2, 1)),
        "mamba_dt_w": c(m("dt_w").transpose(2, 0, 1)),
        "mamba_out_w": c(m("out_w").transpose(1, 0, 2).reshape(DM, SCALES * DI)),
        "mamba_fus_w": c(m("fusion_w").reshape(DM, SCALES, DM).transpose(2, 1, 0)),
        "mamba_cols": c(np.stack([tiles(m("conv_b")), tiles(m("dt_b")), tiles(m("D_skip"))], 1)),
        "mamba_a_log": c(m("A_log").reshape(SCALES, DT2, P, ST).transpose(2, 0, 1, 3)),
        "mamba_fus_b": c(m("fusion_b")[:, None]), "mamba_ln_g": m("ln_g"), "mamba_ln_b": m("ln_b"), "mamba_pick": pick})

    t = lambda name: z["L1_ffn_" + name]
    down_b = np.zeros((P, CH * DM), f)
    for j in range(CH):
        down_b[j * E2:(j + 1) * E2, j * DM:(j + 1) * DM] = t("b2")
    a.update({"moe_wg": t("Wg"), "moe_bg": c(t("bg")[None]), "moe_w1": c(t("W1").transpose(1, 0, 2)),
              "moe_b1": c(t("b1").reshape(E2, FT, P).transpose(2, 0, 1)),
              "moe_w2": c(t("W2").reshape(E2, FT, P, DM).transpose(2, 0, 1, 3)),
              "moe_b2": down_b})
    return a


def kernel(**inputs):
    import numpy as np
    import concourse.bacc as bacc
    from concourse.bass_utils import run_bass_kernel_spmd

    arrays = lay_out({name: np.asarray(value) for name, value in inputs.items()})
    nc = bacc.Bacc("TRN2", target_bir_lowering=False, num_devices=1)
    aps = {name: nc.dram_tensor(name, value.shape, mybir.dt.from_np(value.dtype), kind="ExternalInput").ap()
           for name, value in arrays.items()}
    out = nc.dram_tensor("out", (TOK, DM), F32, kind="ExternalOutput").ap()
    lm_tower(nc, out, aps)
    result = run_bass_kernel_spmd(nc, [arrays], core_ids=[0])
    return result.results[0]["out"].reshape(BATCH, SEQ, DM)
```
